# Optimizing a Trainium2 kernel written in Bass

```python
import numpy as np
import jax
import jax.numpy as jnp

def _softmax(x, axis=-1):
    return jax.nn.softmax(x, axis=axis)

def _gelu(x):
    return jax.nn.gelu(x, approximate=True)

def _silu(x):
    return jax.nn.silu(x)

def _sigmoid(x):
    return jax.nn.sigmoid(x)

def _layernorm(x, axis=-1, eps=1e-05):
    m = jnp.mean(x, axis=axis, keepdims=True)
    v = jnp.var(x, axis=axis, keepdims=True)
    return (x - m) / jnp.sqrt(v + eps)

def _scatter_add(tgt, idx, src, axis=0):
    return tgt.at[idx].add(src)

def _segment_sum(src, seg, n):
    return jax.ops.segment_sum(src, seg, n)
kernel_name = 'mk_seq_preln_d1_jaxref_r4_345135'

def setup_inputs(seed: int=0):
    np.random.seed(seed)
    _w = jnp.asarray

    def _L0_attn_setup():
        import jax, jax.numpy as jnp
        import numpy as np
        EPS = 1e-12

        def _ln(x, g, b):
            m = x.mean(-1, keepdims=True)
            v = x.var(-1, keepdims=True)
            return (x - m) / jnp.sqrt(v + EPS) * g + b

        def _shift(x):
            return jnp.pad(x[:, :-1], ((0, 0), (1, 0), (0, 0)))
        key = jax.random.key(seed)
        ks = jax.random.split(key, 20)
        B, T, H = (4, 512, 512)
        I = 4 * H
        f32 = jnp.float32

        def gamma(k):
            return 1.0 + 0.1 * jax.random.normal(k, (H,), f32)

        def beta(k):
            return 0.1 * jax.random.normal(k, (H,), f32)

        def w(k, i, o):
            return 0.02 * jax.random.normal(k, (i, o), f32)
        return {'x': jax.random.normal(ks[0], (B, T, H), f32), 'ln1_g': gamma(ks[1]), 'ln1_b': beta(ks[2]), 'ln2_g': gamma(ks[3]), 'ln2_b': beta(ks[4]), 'tm_g': gamma(ks[5]), 'tm_b': beta(ks[6]), 'time_decay': -(0.2 + jax.random.uniform(ks[7], (H,), f32)), 'time_first': jax.random.uniform(ks[8], (H,), f32), 'Wk': w(ks[9], H, H), 'Wv': w(ks[10], H, H), 'Wr': w(ks[11], H, H), 'Wo': w(ks[12], H, H), 'bo': jnp.zeros((H,), f32), 'cm_g': gamma(ks[13]), 'cm_b': beta(ks[14]), 'Wck': w(ks[15], H, I), 'Wcv': w(ks[16], I, H), 'Wcr': w(ks[17], H, H)}
    _L0_attn_in = _L0_attn_setup()

    def _L0_ffn_setup():
        import jax, jax.numpy as jnp
        import numpy as np
        B, S, H = (2, 512, 512)
        E, I = (32, 256)
        SI = 1024
        K = 4
        G = 4
        TKG = 2
        SCALE = 2.5

        def _relu2(v):
            r = jax.nn.relu(v)
            return r * r
        key = jax.random.key(seed)
        ks = jax.random.split(key, 7)
        w = 0.02
        return {'x': jax.random.normal(ks[0], (B, S, H), jnp.float32), 'gate_w': jax.random.normal(ks[1], (H, E), jnp.float32) * w, 'e_bias': jax.random.normal(ks[2], (E,), jnp.float32) * 0.01, 'Wu': jax.random.normal(ks[3], (E, H, I), jnp.float32) * w, 'Wd': jax.random.normal(ks[4], (E, I, H), jnp.float32) * w, 'Wsu': jax.random.normal(ks[5], (H, SI), jnp.float32) * w, 'Wsd': jax.random.normal(ks[6], (SI, H), jnp.float32) * w}
    _L0_ffn_in = _L0_ffn_setup()
    _d = {'L0_attn_x': _L0_attn_in['x'], 'L0_attn_ln1_g': _L0_attn_in['ln1_g'], 'L0_attn_ln1_b': _L0_attn_in['ln1_b'], 'L0_attn_ln2_g': _L0_attn_in['ln2_g'], 'L0_attn_ln2_b': _L0_attn_in['ln2_b'], 'L0_attn_tm_g': _L0_attn_in['tm_g'], 'L0_attn_tm_b': _L0_attn_in['tm_b'], 'L0_attn_time_decay': _L0_attn_in['time_decay'], 'L0_attn_time_first': _L0_attn_in['time_first'], 'L0_attn_Wk': _L0_attn_in['Wk'], 'L0_attn_Wv': _L0_attn_in['Wv'], 'L0_attn_Wr': _L0_attn_in['Wr'], 'L0_attn_Wo': _L0_attn_in['Wo'], 'L0_attn_bo': _L0_attn_in['bo'], 'L0_attn_cm_g': _L0_attn_in['cm_g'], 'L0_attn_cm_b': _L0_attn_in['cm_b'], 'L0_attn_Wck': _L0_attn_in['Wck'], 'L0_attn_Wcv': _L0_attn_in['Wcv'], 'L0_attn_Wcr': _L0_attn_in['Wcr'], 'L0_ffn_gate_w': _L0_ffn_in['gate_w'], 'L0_ffn_e_bias': _L0_ffn_in['e_bias'], 'L0_ffn_Wu': _L0_ffn_in['Wu'], 'L0_ffn_Wd': _L0_ffn_in['Wd'], 'L0_ffn_Wsu': _L0_ffn_in['Wsu'], 'L0_ffn_Wsd': _L0_ffn_in['Wsd']}
    _x0 = _d['L0_attn_x']
    _d['L0_attn_x'] = jax.random.normal(jax.random.fold_in(jax.random.key(seed), 1), (1, 2048, 512), dtype=_x0.dtype)
    del _x0
    return _d

def reference(L0_attn_x, L0_attn_ln1_g, L0_attn_ln1_b, L0_attn_ln2_g, L0_attn_ln2_b, L0_attn_tm_g, L0_attn_tm_b, L0_attn_time_decay, L0_attn_time_first, L0_attn_Wk, L0_attn_Wv, L0_attn_Wr, L0_attn_Wo, L0_attn_bo, L0_attn_cm_g, L0_attn_cm_b, L0_attn_Wck, L0_attn_Wcv, L0_attn_Wcr, L0_ffn_gate_w, L0_ffn_e_bias, L0_ffn_Wu, L0_ffn_Wd, L0_ffn_Wsu, L0_ffn_Wsd):

    def _L0_attn_ref(x, ln1_g, ln1_b, ln2_g, ln2_b, tm_g, tm_b, time_decay, time_first, Wk, Wv, Wr, Wo, bo, cm_g, cm_b, Wck, Wcv, Wcr):
        import jax, jax.numpy as jnp
        import numpy as np
        EPS = 1e-12

        def _ln(x, g, b):
            m = x.mean(-1, keepdims=True)
            v = x.var(-1, keepdims=True)
            return (x - m) / jnp.sqrt(v + EPS) * g + b

        def _shift(x):
            return jnp.pad(x[:, :-1], ((0, 0), (1, 0), (0, 0)))
        B, T, H = x.shape
        x1 = _ln(x, ln1_g, ln1_b)
        xln = _ln(x1, tm_g, tm_b)
        xs = _shift(xln)
        mix = xln * time_first + xs * (1.0 - time_first)
        v = xln @ Wv
        r = jax.nn.sigmoid(mix @ Wr)
        dec = jnp.exp(time_decay[None, :] * (T - 1 - jnp.arange(T))[:, None])
        vmix = jnp.einsum('bth,th->bh', v, dec)[:, None, :]
        time_out = r * (vmix @ Wo + bo)
        x2 = x + time_out
        xc = _ln(_ln(x2, ln2_g, ln2_b), cm_g, cm_b)
        xcs = _shift(xc)
        kc = jnp.square(jax.nn.relu(xcs @ Wck))
        vc = kc @ Wcv
        rc = jax.nn.sigmoid(xc @ Wcr)
        return x2 + rc * vc

    def _L0_ffn_ref(x, gate_w, e_bias, Wu, Wd, Wsu, Wsd):
        import jax, jax.numpy as jnp
        import numpy as np
        B, S, H = (2, 512, 512)
        E, I = (32, 256)
        SI = 1024
        K = 4
        G = 4
        TKG = 2
        SCALE = 2.5

        def _relu2(v):
            r = jax.nn.relu(v)
            return r * r
        orig_shape = x.shape
        h = x.reshape(-1, H)
        T = h.shape[0]
        logits = h @ gate_w
        scores = jax.nn.sigmoid(logits)
        sfc = scores + e_bias[None, :]
        per_group = sfc.reshape(T, G, E // G)
        group_scores = jnp.sum(jax.lax.top_k(per_group, 2)[0], axis=-1)
        _, gidx = jax.lax.top_k(group_scores, TKG)
        group_mask = jnp.sum(jax.nn.one_hot(gidx, G, dtype=sfc.dtype), axis=1)
        score_mask = jnp.repeat(group_mask, E // G, axis=-1)
        sfc_masked = jnp.where(score_mask > 0, sfc, 0.0)
        _, topk_idx = jax.lax.top_k(sfc_masked, K)
        topk_w = jnp.take_along_axis(scores, topk_idx, axis=1)
        topk_w = topk_w / (jnp.sum(topk_w, axis=-1, keepdims=True) + 1e-20)
        topk_w = topk_w * SCALE
        combine = jnp.zeros((T, E), scores.dtype).at[jnp.arange(T)[:, None], topk_idx].add(topk_w)
        up = jnp.einsum('th,ehi->tei', h, Wu)
        act = _relu2(up)
        routed = jnp.einsum('tei,te,eih->th', act, combine, Wd)
        shared = _relu2(h @ Wsu) @ Wsd
        out = (routed + shared).reshape(orig_shape)
        return out
    x = L0_attn_x
    x = x + _L0_attn_ref(_layernorm(x, axis=-1), L0_attn_ln1_g, L0_attn_ln1_b, L0_attn_ln2_g, L0_attn_ln2_b, L0_attn_tm_g, L0_attn_tm_b, L0_attn_time_decay, L0_attn_time_first, L0_attn_Wk, L0_attn_Wv, L0_attn_Wr, L0_attn_Wo, L0_attn_bo, L0_attn_cm_g, L0_attn_cm_b, L0_attn_Wck, L0_attn_Wcv, L0_attn_Wcr)
    x = x + _L0_ffn_ref(_layernorm(x, axis=-1), L0_ffn_gate_w, L0_ffn_e_bias, L0_ffn_Wu, L0_ffn_Wd, L0_ffn_Wsu, L0_ffn_Wsd)
    return x

_drawn_inputs = setup_inputs


def setup_inputs(seed=0):
    import zlib

    import numpy as np

    out = dict(_drawn_inputs(seed))
    spreads = {'L0_attn_bo': (0.0, 0.296)}
    factors = {'L0_attn_ln1_g': 6.438,
     'L0_attn_ln1_b': 4.013,
     'L0_attn_ln2_g': 6.96,
     'L0_attn_ln2_b': 7.138,
     'L0_attn_tm_g': 6.871,
     'L0_attn_tm_b': 3.463,
     'L0_attn_time_decay': 2.994,
     'L0_attn_time_first': 7.429,
     'L0_attn_Wr': 4.038,
     'L0_attn_cm_g': 6.785,
     'L0_attn_cm_b': 7.145,
     'L0_attn_Wcr': 4.062,
     'L0_ffn_e_bias': 25.789,
     'L0_ffn_gate_w': 4.668,
     'L0_ffn_Wu': 4.704,
     'L0_ffn_Wd': 4.264,
     'L0_ffn_Wsu': 2.911}
    for name, (base, spread) in spreads.items():
        noise = np.random.default_rng([zlib.crc32(name.encode()), seed]).standard_normal(out[name].shape)
        drawn = base * np.exp(spread * noise) if base else spread * noise
        out[name] = jnp.asarray(drawn.astype(out[name].dtype))
    for name, factor in factors.items():
        out[name] = (out[name] * factor).astype(out[name].dtype)
    return out
```

```python
import concourse.bass as bass
from concourse import mybir
from contextlib import ExitStack

F = mybir.dt.float32
R = mybir.dt.float32r
HALF = mybir.dt.float16
I32 = mybir.dt.int32
U32 = mybir.dt.uint32
ALU = mybir.AluOpType
ACT = mybir.ActivationFunctionType
AX = mybir.AxisListType.X

P = 128
T, H = 2048, 512
NT = T // P
BT = 4
NB = NT // BT
BLK = BT * P
C = H // P
CI = 2048
NCI = CI // P
SI = 1024
NSI = SI // P
E, EI, TOPK, GROUPS = 32, 256, 4, 4
ROUTE_SCALE = 2.5
EPS_OUT, EPS_IN = 1e-5, 1e-12
SLOT_TILES = T * TOPK // P + E
GROUP = 4
OWNER_BITS = 5
KB = 1024
SBUF0 = 16512


class Steps:

    def __init__(self, engine, sem, base=0):
        self.engine, self.sem, self.base, self.k = engine, sem, base, 0

    def do(self, instruction):
        self.k += 1
        instruction.then_inc(self.sem, 1)
        return self.k

    def sync(self, apart=False):
        (wait_apart if apart else type(self.engine).wait_ge)(self.engine, self.sem, self.base + self.k)


def wait_apart(engine, sem, value):
    engine.wait_ge(sem, value)
    engine.nop(nofuse=True)


def program(nc, a, out, scratch):
    ctx = ExitStack()
    sem_names = {}

    def sem(name):
        if name not in sem_names:
            sem_names[name] = ctx.enter_context(nc.semaphore(name))
        return sem_names[name]

    def at(name, shape, dt, kb):
        return nc.alloc_sbuf_tensor_at(name, shape, dt, offset=SBUF0 + int(kb * KB))

    with ctx:
        assert SLOT_TILES - E == NB * NCI
        z_d = scratch("z_d", [T, H])
        wcv_d = scratch("wcv_d", [NCI, P, 2 * H])
        xp_d = scratch("xp_d", [T, H])
        h_d = scratch("h_d", [T, H])
        hT_d = scratch("hT_d", [NB, P, 2, C, BLK])
        z_rows, xp_rows, h_rows = (m.rearrange("(b j p) d -> b p j d", j=BT, p=P) for m in (z_d, xp_d, h_d))
        base_d = scratch("base_d", [T, H])
        y_d = scratch("y_d", [SLOT_TILES * P, H])
        y_spare = y_d.rearrange("(m p) d -> m p d", p=P)[E:]
        base_rows = base_d.rearrange("(b j p) d -> b p j d", j=BT, p=P)
        ident = at("ident", [P, P], F, 200.5)
        onesq = at("onesq", [P, P], F, 201)
        sbc = at("sbc", [P, H], F, 201.5)
        tf = at("tf", [P, C], F, 203.5)
        omtf = at("omtf", [P, C], F, 203.53125)
        ages = at("ages", [P, NT], F, 203.5625)
        mean0 = at("mean0", [P, NT], F, 203.625)
        rstd0 = at("rstd0", [P, NT], F, 203.6875)
        zrow = at("zrow", [P, H], HALF, 203.75)
        nsc = at("nsc", [P, 16, BT], F, 204.75)
        nsci = at("nsci", [P, 2, BT], I32, 205)
        bns = at("bns", [P, BT, 6], F, 205.0625)
        bna = at("bna", [P, BT, 2], F, 205.1875)
        tri = at("tri", [P, P], F, 205.25)
        wck = [at(f"wck_{s}", [P, C, CI], R, 32 * n) for n, s in enumerate(("hi", "lo"))]
        wcr = [at(f"wcr_{s}", [P, C, H], R, 64 + 8 * n) for n, s in enumerate(("hi", "lo"))]
        g1b = at("g1b", [P, 4, H], F, 80)
        tdb = at("tdb", [P, H], F, 88)
        bob = at("bob", [P, H], F, 90)
        xb = at("xb", [P, BT, H], F, 92)
        x1 = at("x1", [P, BT, H], F, 100)
        xln = at("xln", [P, BT, H], F, 108)
        dec = at("dec", [P, BT, H], F, 116)
        xlnT = at("xlnT", [P, C, BLK + 1], F, 124)
        mx = at("mx", [P, C, BLK], F, 132.25)
        mixT = [at(f"mixT_{s}", [P, C, BLK], R, 140.25 + 8 * n) for n, s in enumerate(("hi", "lo"))]
        zo = at("zo", [P, 2, H], F, 156.25)
        wr = [at(f"wr_{s}", [P, C, H], R, 160.25 + 8 * n) for n, s in enumerate(("hi", "lo"))]
        raw = at("raw", [P, C * H], F, 176.25)
        stage = at("stage", [P, C, 2, H], R, 184.25)
        wv = at("wv", [P, C, H], F, 92)
        wo = at("wo", [P, C, H], F, 116)
        pv = at("pv", [P, C, H], F, 100)
        vmb = at("vmb", [P, C, P], F, 132.25)
        vm = at("vm", [P, C], F, 136)

        vring = at("vring", [P, 4, 2 * H], R, 80)
        g2b = at("g2b", [P, 4, H], F, 96)
        f1 = at("f1", [P, 2, BT, H], F, 104)
        f2 = at("f2", [P, BT, H], F, 120)
        hb = at("hb", [P, BT, H], F, 128)
        xcT = [at(f"xcT_{s}", [P, C, BLK + 1], R, 136 + 8.0625 * n) for n, s in enumerate(("hi", "lo"))]
        rc = at("rc", [P, BT, H], F, 152.5)
        ra = at("ra", [P, 2, BLK], F, 160.5)
        ksp = [at(f"ksp_{s}", [P, 2, BLK], R, 164.5 + 4 * n) for n, s in enumerate(("hi", "lo"))]
        hT = at("hT", [P, 2, 2, BLK], R, 172.5)
        gw = [at(f"gw_{s}", [P, C, E], R, 180.5 + 0.5 * n) for n, s in enumerate(("hi", "lo"))]
        gwf = at("gwf", [P, C, E], F, 181.5)
        tmp = at("tmp", [P, BT, H], F, 186)
        scores = at("scores", [P, NT, E], F, 194)

        wsu = [at(f"wsu_{s}", [P, C, SI], R, 16 * n) for n, s in enumerate(("hi", "lo"))]
        wsd = [at(f"wsd_{s}", [P, NSI, H], R, 32 + 16 * n) for n, s in enumerate(("hi", "lo"))]
        hTb = at("hTb", [P, 2, 2, C, BLK], R, 64)
        xps = at("xps", [P, BT, H], F, 104)
        so = at("so", [P, BT, H], F, 112)
        raw3 = [at("raw3a", [P, 2, C * 2 * P], F, 120), at("raw3b", [P, 2, C * 2 * P], F, 96)]
        big = [at(f"big{n}", [P, NT, E], F, kb) for n, kb in enumerate((186, 188, 190, 192, 196, 198))]
        cmp4 = at("cmp4", [P, E, E], F, 186)
        hot_p = at("hot_p", [P, 2, NT, P], HALF, 172.5)
        hot_q = at("hot_q", [P, 2, NT, SLOT_TILES], HALF, 152.5)
        iota_p = at("iota_p", [P, P], F, 180.5)
        iota_q = at("iota_q", [P, SLOT_TILES], F, 181)
        token = at("token", [P, NT], F, 181.375)
        four = at("four", [P, NT], F, 181.4375)
        before = at("before", [P, GROUPS, GROUPS], F, 181.5)
        top8 = at("top8", [P, NT, 8], F, 181.5625)
        ebias = at("ebias", [P, E], F, 182.0625)
        small = at("small", [P, 8, NT * GROUPS], F, 182.1875)
        smi = at("smi", [P, 2, NT * GROUPS], I32, 184.1875)
        slot_i = at("slot_i", [P, TOPK, NT], I32, 184.6875)
        share = at("share", [P, TOPK, NT], F, 184.9375)
        ends_i = at("ends_i", [P, E], I32, 185.1875)
        owner_i = at("owner_i", [P, SLOT_TILES], I32, 185.3125)
        passes_i = at("passes_i", [P, 2], I32, 185.6875)
        ids = at("ids", [P, SLOT_TILES], I32, 206.0)
        wu4 = at("wu4", [P, 4, C * EI], F, 120)
        wd4 = at("wd4", [P, 4, EI // P * H], F, 136)
        xg = at("xg", [P, 2, H], F, 96)
        xT4 = at("xT4", [P, 2, C * P], F, 0)
        a4 = at("a4", [P, 2, EI], F, 8)
        aT4 = at("aT4", [P, 2, 2, EI], R, 10)
        yo = at("yo", [P, 2, H], F, 14)
        wds = at("wds", [P, 2, 2, EI // P * H], R, 34)
        idc = at("idc", [P, 2], I32, 100)
        yg = at("yg", [P, 2, TOPK, H], F, 52)
        acc = at("acc", [P, 2, H], F, 68)
        idc5 = at("idc5", [P, 2, TOPK], I32, 100.0625)

        bank = [ctx.enter_context(nc.psum_tensor(f"bank{i}", [P, 512], F)) for i in range(8)]
        block = ctx.enter_context(nc.Block())

        RSQRT_STEPS = 3 + 9

        def rsqrt(dve, st, v, y):
            half, t = nsci[:, 0], nsc[:, 15]
            st.do(nc.vector.tensor_scalar(half, v.bitcast(I32), 1, None, ALU.logical_shift_right))
            st.sync()
            st.do(nc.vector.tensor_scalar(nsci[:, 1], half, -1.0, float(0x5F3759DF), ALU.mult, ALU.add))
            st.sync()
            st.do(nc.vector.tensor_copy(y, nsci[:, 1].bitcast(F)))
            for _ in range(3):
                st.sync()
                st.do(nc.vector.scalar_tensor_tensor(out=t, in0=y, scalar=-0.5, in1=y, op0=ALU.mult, op1=ALU.mult))
                st.sync()
                st.do(nc.vector.tensor_tensor(t, t, v, ALU.mult))
                st.sync()
                st.do(nc.vector.scalar_tensor_tensor(out=y, in0=t, scalar=1.5, in1=y, op0=ALU.add, op1=ALU.mult))
            st.sync()

        STATS_STEPS = 2 * BT + 1
        S1 = 2 * STATS_STEPS + 3 * RSQRT_STEPS + 6 + 3 * BT - 1

        def stats(dve, st, src, eps):
            for j in range(BT):
                st.do(nc.vector.bn_stats(bns[:, j], src[:, j]))
            st.sync(apart=True)
            for j in range(BT):
                st.do(nc.vector.bn_aggr(bna[:, j], bns[:, j]))
            st.sync()
            st.do(nc.vector.tensor_scalar(nsc[:, 1], bna[:, :, 1], eps, None, ALU.add))
            st.sync()

        def dve_norms1(dve, b):
            st = Steps(dve, sem("s1_dve"), b * S1)
            dve.wait_ge(sem("x_in"), 16 * b + 16)
            stats(dve, st, xb, EPS_OUT)
            rsqrt(dve, st, nsc[:, 1], nsc[:, 2])
            mean_b, rstd_b = mean0[:, bass.ds(b * BT, BT)], rstd0[:, bass.ds(b * BT, BT)]
            st.do(nc.vector.tensor_scalar(mean_b, bna[:, :, 0], 1.0, None, ALU.mult))
            st.do(nc.vector.tensor_scalar(rstd_b, nsc[:, 2], 1.0, None, ALU.mult))
            st.do(nc.vector.tensor_tensor(nsc[:, 3], nsc[:, 2], nsc[:, 2], ALU.mult))
            st.sync()
            st.do(nc.vector.tensor_tensor(nsc[:, 3], nsc[:, 3], bna[:, :, 1], ALU.mult))
            st.sync()
            st.do(nc.vector.tensor_scalar(nsc[:, 3], nsc[:, 3], EPS_IN, None, ALU.add))
            st.sync()
            rsqrt(dve, st, nsc[:, 3], nsc[:, 4])
            st.do(nc.vector.tensor_tensor(nsc[:, 4], nsc[:, 4], nsc[:, 2], ALU.mult))
            st.sync()
            for j in range(BT):
                i = nc.vector.scalar_tensor_tensor(out=x1[:, j], in0=xb[:, j], scalar=bna[:, j, 0:1],
                                                   in1=g1b[:, 0], op0=ALU.subtract, op1=ALU.mult)
                i.then_inc(sem("x_free"), 1) if j == BT - 1 else st.do(i)
            dve.wait_ge(sem("x_free"), b + 2)
            for j in range(BT):
                st.do(nc.vector.scalar_tensor_tensor(out=x1[:, j], in0=x1[:, j], scalar=nsc[:, 4, j:j + 1],
                                                     in1=g1b[:, 1], op0=ALU.mult, op1=ALU.add))
            st.sync()
            stats(dve, st, x1, EPS_IN)
            rsqrt(dve, st, nsc[:, 1], nsc[:, 2])
            for j in range(BT):
                st.do(nc.vector.scalar_tensor_tensor(out=x1[:, j], in0=x1[:, j], scalar=bna[:, j, 0:1],
                                                     in1=g1b[:, 2], op0=ALU.subtract, op1=ALU.mult))
            st.sync()
            dve.wait_ge(sem("m_done"), b + 1)
            for j in range(BT):
                nc.vector.scalar_tensor_tensor(out=xln[:, j], in0=x1[:, j], scalar=nsc[:, 2, j:j + 1],
                                               in1=g1b[:, 3], op0=ALU.mult, op1=ALU.add).then_inc(sem("xln_in"), 1)
            dve.wait_ge(sem("xln_in"), b * BT + BT)
            return st.k

        def dve_mix(dve, b):
            for c in range(C):
                dve.wait_ge(sem("xt_in"), b * C + c + 3)
                nc.vector.scalar_tensor_tensor(out=mx[:, c], in0=xlnT[:, c, 0:BLK], scalar=omtf[:, c:c + 1],
                                               in1=mx[:, c], op0=ALU.mult, op1=ALU.add).then_inc(sem("mix_in"), 1)
            dve.wait_ge(sem("mix_in"), b * C + C)
            nc.vector.tensor_scalar(xlnT[:, :, 0:1], xlnT[:, :, BLK:BLK + 1], 1.0, None,
                                    ALU.mult).then_inc(sem("xt_free"), 1)

        def stage1_vector(dve):
            nc.vector.memset(xlnT[:, :, 0:1], 0.0).then_inc(sem("carry0"), 1)
            dve.wait_ge(sem("par_in"), 16 * 7)
            dve.wait_ge(sem("cst"), 5)
            nc.vector.tensor_scalar(omtf[:], tf[:], -1.0, 1.0, ALU.mult, ALU.add).then_inc(sem("omtf"), 1)
            dve.wait_ge(sem("omtf"), 1)
            dve.wait_ge(sem("carry0"), 1)
            with dve.Fori(0, NB) as b:
                k = dve_norms1(dve, b)
                assert k == S1, (k, S1)
                dve_mix(dve, b)
            dve.wait_ge(sem("m_fin"), 1)
            dve.wait_ge(sem("wv_in"), 16)
            for c in range(C):
                nc.vector.tensor_tensor(pv[:, c], wv[:, c], bank[c][:], ALU.mult).then_inc(sem("pv_in"), 1)
            dve.wait_ge(sem("vm_in"), 1)
            nc.vector.tensor_copy(vm[:], bank[4][:, 0:C]).then_inc(sem("vmc"), 1)
            dve.wait_ge(sem("vmc"), 1)
            dve.wait_ge(sem("mixlo_in"), 4 + NB * C)
            for c in range(C):
                nc.vector.tensor_scalar(vmb[:, c], onesq[:], vm[:, c:c + 1], None, ALU.mult).then_inc(sem("vmb_in"), 1)
            dve.wait_ge(sem("srow_in"), 1)
            nc.vector.tensor_tensor(sbc[:], bank[5][:], bob[:], ALU.add).then_inc(sem("sbc_in"), 1)

        def stage1_scalar(act):
            act.wait_ge(sem("par_in"), 16 * 7)
            act.wait_ge(sem("ages_in"), 1)
            act.wait_ge(sem("raw_in"), 16)
            nc.scalar.activation(wr[0][:].rearrange("p c n -> p (c n)"), raw[:], ACT.Copy).then_inc(sem("whi"), 1)
            act.wait_ge(sem("carry0"), 1)
            with act.Fori(0, NB) as b:
                wait_apart(act, sem("m_done"), b + 1)
                for j in range(BT):
                    nc.scalar.activation(dec[:, j], tdb[:], ACT.Exp,
                                         scale=ages[:, bass.ds(b * BT + j, 1)]).then_inc(sem("dec_in"), 1)
                wait_apart(act, sem("raw_in"), 32 * b + 32)
                nc.scalar.activation(wck[0][:, bass.ds(b, 1)].rearrange("p a n -> p (a n)"), raw[:],
                                     ACT.Copy).then_inc(sem("whi"), 1)
                act.wait_ge(sem("xt_free"), b + 1)
                act.wait_ge(sem("mixlo_in"), b * C + 4)
                for c in range(C):
                    act.wait_ge(sem("tr_in"), b * C + c + 1)
                    nc.scalar.activation(xlnT[:, c, 1:BLK + 1], bank[4 + c % 2][:], ACT.Copy)
                    nc.scalar.activation(mx[:, c], bank[4 + c % 2][:], ACT.Copy,
                                         scale=tf[:, c:c + 1]).then_inc(sem("xt_in"), 1)
                for c in range(C):
                    act.wait_ge(sem("mix_in"), b * C + c + 1)
                    nc.scalar.activation(mixT[0][:, c], mx[:, c], ACT.Copy).then_inc(sem("mixhi_in"), 1)
                act.wait_ge(sem("raw_in"), 32 * b + 48)
                act.wait_ge(sem("wst"), 16 * b + 16)
                nc.scalar.activation(stage[:, :, 0], raw[:].rearrange("p (c n) -> p c n", c=C),
                                     ACT.Copy).then_inc(sem("whi"), 1)
                for j in range(BT):
                    act.wait_ge(sem("z_in"), b * BT + j + 1)
                    act.wait_ge(sem(f"zo_st{j % 2}"), 32 * b + 16 * (j // 2) + 16)
                    nc.scalar.activation(zo[:, j % 2], bank[6 + j % 2][:], ACT.Copy).then_inc(sem("z_free"), 1)
            act.wait_ge(sem("raw_in"), 32 * NB + 32)
            nc.scalar.activation(wcr[0][:].rearrange("p c n -> p (c n)"), raw[:], ACT.Copy).then_inc(sem("whi"), 1)

        def stage1_gpsimd(pool):
            nc.gpsimd.memset(ident[:], 0.0).then_inc(sem("cst"), 1)
            nc.gpsimd.memset(onesq[:], 1.0).then_inc(sem("cst"), 1)
            nc.gpsimd.memset(zrow[:], 0.0).then_inc(sem("cst"), 1)
            pool.wait_ge(sem("cst"), 3)
            nc.gpsimd.affine_select(out=ident[:], in_=ident[:], compare_op=ALU.not_equal, fill=1.0, base=0,
                                    pattern=[[-1, P]], channel_multiplier=1).then_inc(sem("cst"), 1)
            nc.gpsimd.affine_select(out=tri[:], in_=onesq[:], compare_op=ALU.is_gt, fill=0.0, base=0,
                                    pattern=[[1, P]], channel_multiplier=-1).then_inc(sem("cst"), 1)
            nc.gpsimd.iota(ages[:], [[-P, NT]], base=T - 1, channel_multiplier=-1,
                           allow_small_or_imprecise_dtypes=True).then_inc(sem("ages_in"), 1)
            pool.sem_inc(sem("mixlo_in"), 4)
            pool.wait_ge(sem("whi"), 1)
            nc.gpsimd.tensor_tensor(wr[1][:].rearrange("p c n -> p (c n)"), raw[:],
                                    wr[0][:].rearrange("p c n -> p (c n)"), ALU.subtract).then_inc(sem("wlo"), 1)
            with pool.Fori(0, NB) as b:
                wait_apart(pool, sem("whi"), 2 * b + 2)
                nc.gpsimd.tensor_tensor(wck[1][:, bass.ds(b, 1)].rearrange("p a n -> p (a n)"), raw[:],
                                        wck[0][:, bass.ds(b, 1)].rearrange("p a n -> p (a n)"),
                                        ALU.subtract).then_inc(sem("wlo"), 1)
                for c in range(C):
                    pool.wait_ge(sem("mixhi_in"), b * C + c + 1)
                    nc.gpsimd.tensor_tensor(mixT[1][:, c], mx[:, c], mixT[0][:, c],
                                            ALU.subtract).then_inc(sem("mixlo_in"), 1)
                pool.wait_ge(sem("whi"), 2 * b + 3)
                nc.gpsimd.tensor_tensor(stage[:, :, 1], raw[:].rearrange("p (c n) -> p c n", c=C),
                                        stage[:, :, 0], ALU.subtract).then_inc(sem("wlo"), 1)
            pool.wait_ge(sem("whi"), 2 * NB + 2)
            nc.gpsimd.tensor_tensor(wcr[1][:].rearrange("p c n -> p (c n)"), raw[:],
                                    wcr[0][:].rearrange("p c n -> p (c n)"), ALU.subtract).then_inc(sem("wlo"), 1)

        def stage1_tensor(pe):
            pe.sem_inc(sem("m_done"), 1)
            pe.wait_ge(sem("cst"), 5)
            for c in range(C):
                nc.tensor.matmul(bank[c][:], zrow[:, 0:P], zrow[:], start=True, stop=False)
            with pe.Fori(0, NB) as b:
                for c in range(C):
                    for j in range(BT):
                        if c == 0:
                            pe.wait_ge(sem("xln_in"), b * BT + j + 1)
                        if j == 0:
                            pe.wait_ge(sem("xt_in"), b * C + c + 1)
                        i = nc.tensor.transpose(bank[4 + c % 2][:, j * P:(j + 1) * P], xln[:, j, c * P:(c + 1) * P], ident[:])
                    i.then_inc(sem("tr_in"), 1)
                for j in range(BT):
                    pe.wait_ge(sem("dec_in"), b * BT + j + 1)
                    for c in range(C):
                        i = nc.tensor.matmul(bank[c][:], xln[:, j, c * P:(c + 1) * P], dec[:, j], start=False, stop=False)
                i.then_inc(sem("m_done"), 1)
                pe.wait_ge(sem("wlo"), 1)
                pe.wait_ge(sem("mixlo_in"), b * C + C + 4)
                for j in range(BT):
                    pe.wait_ge(sem("z_free"), b * BT + j + 1)
                    i = split_product(bank[6 + j % 2][:], lambda s, c: mixT[s][:, c, j * P:(j + 1) * P],
                                      lambda s, c: wr[s][:, c], C)
                    i.then_inc(sem("z_in"), 1)
            for c in range(C):
                i = nc.tensor.matmul(bank[c][:], zrow[:, 0:P], zrow[:], start=False, stop=True)
            i.then_inc(sem("m_fin"), 1)
            pe.wait_ge(sem("pv_in"), C)
            pe.wait_ge(sem("xt_in"), NB * C + 2)
            for h in range(C):
                for c in range(C):
                    i = nc.tensor.matmul(bank[4][:, h:h + 1], pv[:, c, h * P:(h + 1) * P], onesq[:, 0:1],
                                         start=c == 0, stop=c == C - 1)
            i.then_inc(sem("vm_in"), 1)
            pe.wait_ge(sem("vmb_in"), C)
            pe.wait_ge(sem("wo_in"), 16)
            for h in range(C):
                i = nc.tensor.matmul(bank[5][:], vmb[:, h], wo[:, h], start=h == 0, stop=h == C - 1)
            i.then_inc(sem("srow_in"), 1)

        def split_product(dst, lhs, rhs, n):
            parts = [(0, 0), (0, 1), (1, 0)]
            for c in range(n):
                for k, (l, r) in enumerate(parts):
                    i = nc.tensor.matmul(dst, lhs(l, c), rhs(r, c), start=c == 0 and k == 0,
                                         stop=c == n - 1 and k == 2)
            return i

        def vec(name):
            return a[name].partition_broadcast(P)

        x_rows = a["L0_attn_x"][0].rearrange("(b j p) d -> b p j d", j=BT, p=P)
        wck_rows = a["L0_attn_Wck"].rearrange("(c p) n -> c p n", p=P)
        wcv_rows = a["L0_attn_Wcv"].rearrange("(g c p) n -> g p c n", c=C, p=P)

        def square(name):
            return a[name].rearrange("(c p) n -> p c n", p=P)

        def stage1_sync(sp):
            sp.dma_start(xb[:], x_rows[0]).then_inc(sem("x_in"), 16)
            for n, v in enumerate(("ln1_g", "ln1_b", "tm_g", "tm_b")):
                sp.dma_start(g1b[:, n], vec(f"L0_attn_{v}")).then_inc(sem("par_in"), 16)
            sp.dma_start(tdb[:], vec("L0_attn_time_decay")).then_inc(sem("par_in"), 16)
            sp.dma_start(bob[:], vec("L0_attn_bo")).then_inc(sem("par_in"), 16)
            sp.dma_start(tf[:], a["L0_attn_time_first"].rearrange("(c p) -> p c", p=P),
                         allow_slow_non_contiguous=True).then_inc(sem("par_in"), 16)
            sp.dma_start(raw[:].rearrange("p (c n) -> p c n", c=C), square("L0_attn_Wr")).then_inc(sem("raw_in"), 16)
            for name, credit in (("x_free", 1), ("xt_free", 1), ("xt_in", 2), ("z_free", 2), ("zo_st0", 16),
                                 ("zo_st1", 16), ("wst", 16)):
                sp.sem_inc(sem(name), credit)
            with sp.Fori(0, NB - 1) as b:
                sync_block1(sp, b)
            sync_block1(sp, NB - 1)
            sp.dma_start(raw[:].rearrange("p (c n) -> p c n", c=C), square("L0_attn_Wcr")).then_inc(sem("raw_in"), 16)
            sp.wait_ge(sem("x_free"), NB + 1)
            sp.dma_start(wv[:], square("L0_attn_Wv")).then_inc(sem("wv_in"), 16)
            sp.wait_ge(sem("m_fin"), 1)
            sp.dma_start(wo[:], square("L0_attn_Wo")).then_inc(sem("wo_in"), 16)

        def sync_block1(sp, b):
            wait_apart(sp, sem("wlo"), 2 * b + 1)
            sp.dma_start(raw[:], wck_rows[bass.ds(b, 1)].rearrange("a p n -> p (a n)")).then_inc(sem("raw_in"), 16)
            if not isinstance(b, int):
                wait_apart(sp, sem("x_free"), b + 2)
                sp.dma_start(xb[:], x_rows[bass.ds(b + 1, 1)].rearrange("a p j d -> p (a j) d")).then_inc(sem("x_in"), 16)
            wait_apart(sp, sem("wlo"), 2 * b + 2)
            sp.dma_start(raw[:].rearrange("p (c n) -> p c n", c=C),
                         wcv_rows[bass.ds(b, 1)].rearrange("a p c n -> p (a c) n")).then_inc(sem("raw_in"), 16)
            wait_apart(sp, sem("wlo"), 2 * b + 3)
            sp.dma_start(wcv_d[bass.ds(b * C, C)].rearrange("c p m -> p c m"),
                         stage[:].bitcast(F).rearrange("p c s n -> p c (s n)")).then_inc(sem("wst"), 16)
            for j in range(BT):
                wait_apart(sp, sem("z_free"), b * BT + j + 3)
                sp.dma_start(z_d[bass.ds((b * BT + j) * P, P)], zo[:, j % 2]).then_inc(sem(f"zo_st{j % 2}"), 16)

        TH_AT = 2
        FRONT, TAIL = 4 * BT + 2 * (STATS_STEPS + RSQRT_STEPS) + 3 * BT, STATS_STEPS + RSQRT_STEPS

        def wait_pos(engine, s, value):
            if not isinstance(value, int) or value > 0:
                engine.wait_ge(s, value)

        def dve_front(dve, b):
            st = Steps(dve, sem("front_dve"), b * FRONT)
            xx = lambda j: f1[:, bass.ds(b & 1, 1), j].rearrange("p a d -> p (a d)")
            wait_apart(dve, sem("x2_in"), 16 * b + 16)
            for j in range(BT):
                st.do(nc.vector.tensor_scalar(tmp[:, j], xx(j), mean0[:, bass.ds(b * BT + j, 1)],
                                              rstd0[:, bass.ds(b * BT + j, 1)], ALU.subtract, ALU.mult))
            for j in range(BT):
                dve.wait_ge(sem("zs_in"), b * BT + j + 1)
                st.do(nc.vector.tensor_tensor(f2[:, j], f2[:, j], sbc[:], ALU.mult))
            st.sync()
            for j in range(BT):
                st.do(nc.vector.tensor_tensor(f2[:, j], f2[:, j], tmp[:, j], ALU.add))
            st.sync()
            for j in range(BT):
                st.do(nc.vector.tensor_tensor(xx(j), xx(j), f2[:, j], ALU.add))
            for n in (0, 2):
                stats(dve, st, f2, EPS_IN)
                rsqrt(dve, st, nsc[:, 1], nsc[:, 2])
                for j in range(BT):
                    st.do(nc.vector.scalar_tensor_tensor(out=f2[:, j], in0=f2[:, j], scalar=bna[:, j, 0:1],
                                                         in1=g2b[:, n], op0=ALU.subtract, op1=ALU.mult))
                st.sync()
                for j in range(BT):
                    i = nc.vector.scalar_tensor_tensor(out=f2[:, j], in0=f2[:, j], scalar=nsc[:, 2, j:j + 1],
                                                       in1=g2b[:, n + 1], op0=ALU.mult, op1=ALU.add)
                    st.do(i) if n == 0 else i.then_inc(sem("xc_in"), 1)
                if n == 0:
                    st.sync()
            dve.wait_ge(sem("xc_in"), b * BT + BT)
            assert st.k == FRONT, (st.k, FRONT)

        def dve_lo_xc(dve, b):
            for c in range(C):
                dve.wait_ge(sem("hiT_in"), b * C + c + 1)
                nc.vector.tensor_tensor(xcT[1][:, c, 1:BLK + 1], bank[6 + c % 2][:], xcT[0][:, c, 1:BLK + 1],
                                        ALU.subtract).then_inc(sem("loT_in"), 1)

        def dve_tail_a(dve, b):
            dve.wait_ge(sem("vc_done"), 2 + NCI * (b + 1))
            dve.wait_ge(sem("h_st"), 16 * b + 16)
            for j in range(BT):
                nc.vector.tensor_tensor(hb[:, j], rc[:, j], bank[j][:], ALU.mult).then_inc(sem("u_in"), 1)

        def dve_tail_b(dve, b):
            st = Steps(dve, sem("tail_dve"), b * TAIL)
            xx = lambda j: f1[:, bass.ds(b & 1, 1), j].rearrange("p a d -> p (a d)")
            dve.wait_ge(sem("u_in"), 4 + b * BT + BT)
            for j in range(BT):
                nc.vector.tensor_tensor(xx(j), xx(j), hb[:, j], ALU.add).then_inc(sem("xp_in"), 1)
            wait_apart(dve, sem("xp_in"), b * BT + BT)
            stats(dve, st, f1[:, bass.ds(b & 1, 1)].rearrange("p a j d -> p (a j) d"), EPS_OUT)
            rsqrt(dve, st, nsc[:, 1], nsc[:, 2])
            for j in range(BT):
                nc.vector.tensor_scalar(hb[:, j], xx(j), bna[:, j, 0:1], nsc[:, 2, j:j + 1],
                                        ALU.subtract, ALU.mult).then_inc(sem("h_in"), 1)
            dve.wait_ge(sem("h_in"), b * BT + BT)
            assert st.k == TAIL, (st.k, TAIL)

        def dve_lo_h(dve, b):
            for c in range(C):
                dve.wait_ge(sem("hiTH_in"), b * C + c + 1)
                nc.vector.tensor_tensor(hT[:, c % 2, 1], bank[6 + c % 2][:], hT[:, c % 2, 0],
                                        ALU.subtract).then_inc(sem("loTH_in"), 1)

        def stage2_vector(dve):
            for s in range(2):
                nc.vector.memset(xcT[s][:, :, 0:1].bitcast(F), 0.0).then_inc(sem("carry2"), 1)
            dve.wait_ge(sem("par2_in"), 16 * 5)
            dve.wait_ge(sem("gwhi"), 1)
            nc.vector.tensor_tensor(gw[1][:], gwf[:], gw[0][:], ALU.subtract).then_inc(sem("gwlo"), 1)
            dve_front(dve, 0)
            dve_lo_xc(dve, 0)
            dve_front(dve, 1)
            with dve.Fori(1, NB - 1) as b:
                dve_tail_a(dve, b - 1)
                dve_lo_xc(dve, b)
                dve_tail_b(dve, b - 1)
                dve_lo_h(dve, b - 1)
                dve_front(dve, b + 1)
            dve_tail_a(dve, NB - 2)
            dve_lo_xc(dve, NB - 1)
            dve_tail_b(dve, NB - 2)
            dve_lo_h(dve, NB - 2)
            dve_tail_a(dve, NB - 1)
            dve_tail_b(dve, NB - 1)
            dve_lo_h(dve, NB - 1)

        def act_receptance(act, b):
            act.wait_ge(sem("zl_in"), 16 * b + 16)
            for j in range(BT):
                nc.scalar.activation(f2[:, j], f2[:, j], ACT.Sigmoid).then_inc(sem("zs_in"), 1)

        def act_hi_xc(act, b, first=False):
            act.wait_ge(sem("trT_in"), b * C + 1)
            if first:
                act.wait_ge(sem("carry2"), 2)
            else:
                for s in range(2):
                    nc.scalar.activation(xcT[s][:, :, 0:1], xcT[s][:, :, BLK:BLK + 1], ACT.Copy).then_inc(sem("carry2"), 1)
                act.wait_ge(sem("carry2"), 2 + 2 * b)
            for c in range(C):
                act.wait_ge(sem("trT_in"), b * C + c + 1)
                nc.scalar.activation(xcT[0][:, c, 1:BLK + 1], bank[6 + c % 2][:], ACT.Copy).then_inc(sem("hiT_in"), 1)

        def act_rc(act, b):
            act.wait_ge(sem("u_in"), b * BT + 4)
            for j in range(BT):
                act.wait_ge(sem("rcp_in"), b * BT + j + 1)
                nc.scalar.activation(rc[:, j], bank[6 + j % 2][:], ACT.Sigmoid).then_inc(sem("rc_in"), 1)

        def act_inner(act, n, i):
            act.wait_ge(sem("kc_in"), n + 1)
            act.wait_ge(sem("klo_in"), n + 1)
            nc.scalar.activation(ra[:, i % 2], bank[4 + i % 2][:], ACT.Relu).then_inc(sem("kc_free"), 1)
            act.wait_ge(sem("kc_free"), n + 3)
            nc.scalar.activation(ra[:, i % 2], ra[:, i % 2], ACT.Square).then_inc(sem("sq"), 1)
            act.wait_ge(sem("sq"), n + 1)
            act.wait_ge(sem("vc_done"), n + 1)
            nc.scalar.activation(ksp[0][:, i % 2], ra[:, i % 2], ACT.Copy).then_inc(sem("khi_in"), 1)

        def act_hi_h(act, b):
            for c in range(C):
                act.wait_ge(sem("trH_in"), b * C + c + 1)
                act.wait_ge(sem(f"ht_st{c % 2}"), 32 * b + 16 * (c // 2) + 16)
                nc.scalar.activation(hT[:, c % 2, 0], bank[6 + c % 2][:], ACT.Copy).then_inc(sem("hiTH_in"), 1)
            wait_apart(act, sem("lg_in"), b + 1)
            nc.scalar.activation(scores[:, bass.ds(b * BT, BT)].rearrange("p j e -> p (j e)"), bank[5][:, 0:BT * E],
                                 ACT.Sigmoid).then_inc(sem("sc_in"), 1)

        def act_block2(act, b, first=False, last=False):
            act_hi_xc(act, b, first)
            act_rc(act, b)
            for i in range(NCI):
                act_inner(act, b * NCI + i, i)
                if i == 1 and not last:
                    act_receptance(act, b + 1)
                if i == TH_AT and not first:
                    act_hi_h(act, b - 1)

        def stage2_scalar(act):
            act.wait_ge(sem("par2_in"), 16 * 5)
            nc.scalar.activation(gw[0][:], gwf[:], ACT.Copy).then_inc(sem("gwhi"), 1)
            act_receptance(act, 0)
            act_block2(act, 0, first=True)
            with act.Fori(1, NB - 1) as b:
                act_block2(act, b)
            act_block2(act, NB - 1, last=True)

        def pool_inner(pool, n, i):
            pool.wait_ge(sem("khi_in"), n + 1)
            nc.gpsimd.tensor_tensor(ksp[1][:, i % 2], ra[:, i % 2], ksp[0][:, i % 2],
                                    ALU.subtract).then_inc(sem("klo_in"), 1)

        def stage2_gpsimd(pool):
            with pool.Fori(0, NB) as b:
                for i in range(NCI):
                    pool_inner(pool, b * NCI + i, i)

        def pe_inner_up(pe, n, i, weights, rhs):
            pe.wait_ge(sem("kc_free"), n + 1)
            split_product(bank[4 + i % 2][:], lambda s, c: weights[s][:, c, i * P:(i + 1) * P],
                          rhs, C).then_inc(sem("kc_in"), 1)

        def pe_inner_down(pe, n, i, last, rhs):
            pe.wait_ge(sem("klo_in"), n + 3)
            for j in range(BT):
                for k, (l, r) in enumerate(((0, 0), (0, 1), (1, 0))):
                    m = nc.tensor.matmul(bank[j][:], ksp[l][:, i % 2, j * P:(j + 1) * P], rhs(r),
                                         start=i == 0 and k == 0, stop=i == last and k == 2)
            m.then_inc(sem("vc_done"), 1)

        def pe_router(pe, b):
            def logits(c):
                pe.wait_ge(sem("loTH_in"), 8 + b * C + c + 1)
                for j in range(BT):
                    for k, (l, r) in enumerate(((0, 0), (0, 1), (1, 0))):
                        m = nc.tensor.matmul(bank[5][:, j * E:(j + 1) * E], hT[:, c % 2, l, j * P:(j + 1) * P],
                                             gw[r][:, c], start=False, stop=c == C - 1 and j == BT - 1 and k == 2)
                return m
            pe.wait_ge(sem("h_in"), b * BT + BT)
            nc.tensor.matmul(bank[5][:, 0:P], zrow[:, 0:P], zrow[:, 0:P], start=True, stop=False)
            for c in range(C):
                if c >= 2:
                    pe.wait_ge(sem("loTH_in"), 8 + b * C + c - 1)
                for j in range(BT):
                    m = nc.tensor.transpose(bank[6 + c % 2][:, j * P:(j + 1) * P], hb[:, j, c * P:(c + 1) * P], ident[:])
                m.then_inc(sem("trH_in"), 1)
                if c:
                    logits(c - 1)
            logits(C - 1).then_inc(sem("lg_in"), 1)

        def pe_block2(pe, b, first=False):
            pe.wait_ge(sem("xc_in"), b * BT + BT)
            pe.wait_ge(sem("loTH_in"), 4 + b * C)
            for c in range(C):
                if c >= 2:
                    pe.wait_ge(sem("loT_in"), b * C + c - 1)
                for j in range(BT):
                    m = nc.tensor.transpose(bank[6 + c % 2][:, j * P:(j + 1) * P], f2[:, j, c * P:(c + 1) * P], ident[:])
                m.then_inc(sem("trT_in"), 1)
            pe.wait_ge(sem("loT_in"), b * C + C)
            for j in range(BT):
                if j >= 2:
                    pe.wait_ge(sem("rc_in"), b * BT + j - 1)
                split_product(bank[6 + j % 2][:], lambda s, c: xcT[s][:, c, 1 + j * P:1 + (j + 1) * P],
                              lambda s, c: wcr[s][:, c], C).then_inc(sem("rcp_in"), 1)

            def down(i):
                if i == 0:
                    pe.wait_ge(sem("u_in"), b * BT + 4)
                pe.wait_ge(sem(f"vr_in{i % 4}"), 64 * b + 16 * (i // 4) + 16)
                pe_inner_down(pe, b * NCI + i, i, NCI - 1, lambda s: vring[:, i % 4, s * H:(s + 1) * H])

            for i in range(NCI):
                if i == TH_AT + 1 and not first:
                    pe.wait_ge(sem("sc_in"), b)
                pe_inner_up(pe, b * NCI + i, i, wck, lambda s, c: xcT[s][:, c, 0:BLK])
                if i >= 2:
                    down(i - 2)
                if i == TH_AT and not first:
                    pe.wait_ge(sem("rc_in"), b * BT + BT)
                    pe.wait_ge(sem("kc_free"), b * NCI + TH_AT + 2)
                    pe_router(pe, b - 1)
            down(NCI - 2)
            down(NCI - 1)

        def stage2_tensor(pe):
            pe.wait_ge(sem("wlo"), 2 * NB + 2)
            pe.wait_ge(sem("gwlo"), 1)
            pe_block2(pe, 0, first=True)
            with pe.Fori(1, NB) as b:
                pe_block2(pe, b)

        hT_rows = hT_d.rearrange("b p s c t -> b c p s t")

        def sp_tail2(sp, b):
            wait_apart(sp, sem("xp_in"), b * BT + BT)
            sp.dma_start(xp_rows[bass.ds(b, 1)].rearrange("a p j d -> p (a j) d"),
                         f1[:, bass.ds(b & 1, 1)].rearrange("p a j d -> p (a j) d")).then_inc(sem("xp_st"), 16)
            wait_apart(sp, sem("h_in"), b * BT + BT)
            sp.dma_start(h_rows[bass.ds(b, 1)].rearrange("a p j d -> p (a j) d"), hb[:]).then_inc(sem("h_st"), 16)

        def sp_hT(sp, b):
            for c in range(C):
                wait_apart(sp, sem("loTH_in"), 8 + b * C + c + 1)
                sp.dma_start(hT_rows[bass.ds(b, 1), c].rearrange("a p s t -> p (a s) t"),
                             hT[:, c % 2].bitcast(F)).then_inc(sem(f"ht_st{c % 2}"), 16)

        def sp_block2(sp, b, first=False, last=False):
            def ring(i):
                n = b * NCI + i
                if not (first and i < 4):
                    wait_apart(sp, sem("vc_done"), n - 1)
                sp.dma_start(vring[:, i % 4].bitcast(F), wcv_d[i]).then_inc(sem(f"vr_in{i % 4}"), 16)
                sp.dma_start(y_spare[bass.ds(n, 1)].rearrange("a p (s n) -> (a p) s n", s=2),
                             zrow[:].bitcast(F).unsqueeze(1).to_broadcast([P, 2, H // 2])).then_inc(sem("y_fill"), 16)
            if not last:
                wait_apart(sp, sem("trT_in"), b * C + C)
                sp.dma_start(f2[:], z_rows[bass.ds(b + 1, 1)].rearrange("a p j d -> p (a j) d")).then_inc(sem("zl_in"), 16)
            for i in range(4):
                ring(i)
            if not first:
                sp_tail2(sp, b - 1)
                if not last:
                    wait_apart(sp, sem("xp_st"), 16 * b)
                    sp.dma_start(f1[:, bass.ds((b + 1) & 1, 1)].rearrange("p a j d -> p (a j) d"),
                                 x_rows[bass.ds(b + 1, 1)].rearrange("a p j d -> p (a j) d")).then_inc(sem("x2_in"), 16)
            ring(4)
            if not first:
                sp_hT(sp, b - 1)
            for i in range(5, NCI):
                ring(i)

        def stage2_sync(sp):
            for name, credit in (("u_in", 4), ("h_st", 16), ("kc_free", 2), ("klo_in", 2), ("vc_done", 2),
                                 ("loTH_in", 8), ("ht_st0", 16), ("ht_st1", 16),
                                 ("bs_st", 16), ("xt4", 2), ("u4", 2), ("r4", 2), ("at4", 2), ("al4", 2),
                                 ("d4", 2), ("y4", 2), ("y_st0", 16), ("y_st1", 16)):
                sp.sem_inc(sem(name), credit)
            sp.wait_ge(sem("sbc_in"), 1)
            sp.wait_ge(sem("wst"), 16 * NB + 16)
            sp.wait_ge(sem("wlo"), 2 * NB + 2)
            for n, v in enumerate(("ln2_g", "ln2_b", "cm_g", "cm_b")):
                sp.dma_start(g2b[:, n], vec(f"L0_attn_{v}")).then_inc(sem("par2_in"), 16)
            sp.dma_start(gwf[:], square("L0_ffn_gate_w")).then_inc(sem("par2_in"), 16)
            sp.wait_ge(sem("zo_st0"), 32 * NB + 16)
            sp.wait_ge(sem("zo_st1"), 32 * NB + 16)
            sp.dma_start(f2[:], z_rows[0]).then_inc(sem("zl_in"), 16)
            sp.dma_start(f1[:, 0], x_rows[0]).then_inc(sem("x2_in"), 16)
            sp.wait_ge(sem("x2_in"), 16)
            sp.dma_start(f1[:, 1], x_rows[1]).then_inc(sem("x2_in"), 16)
            sp_block2(sp, 0, first=True)
            with sp.Fori(1, NB - 1) as b:
                sp_block2(sp, b)
            sp_block2(sp, NB - 1, last=True)

        N3 = NB * NCI

        def pe_block3(pe, b, router=False, between=None):
            pe.wait_ge(sem("hb_in"), 16 * b + 16)

            def down(i):
                if i == 0:
                    if b == 0:
                        pe.wait_ge(sem("u_in"), NB * BT + 4)
                    else:
                        pe.wait_ge(sem("sh_in"), b * BT)
                pe_inner_down(pe, N3 + b * NSI + i, i, NSI - 1, lambda s: wsd[s][:, i])

            rhs = lambda s, c: hTb[:, bass.ds(b & 1, 1), s, c].rearrange("p a t -> p (a t)")
            for i in range(NSI):
                if i == TH_AT + 1 and router:
                    pe.wait_ge(sem("sc_in"), NB)
                pe.wait_ge(sem("w3lo"), 2 * (i // 2) + 2)
                pe_inner_up(pe, N3 + b * NSI + i, i, wsu, rhs)
                if i >= 2:
                    down(i - 2)
                if i == TH_AT and router:
                    pe.wait_ge(sem("rc_in"), NB * BT)
                    pe.wait_ge(sem("kc_free"), N3 + TH_AT + 2)
                    pe_router(pe, NB - 1)
                if i == 4 and between:
                    between(pe)
            down(NSI - 2)
            down(NSI - 1)

        def pe_counts(pe):
            pe.wait_ge(sem("sel_in"), 1)
            sel = big[3][:].rearrange("p n e -> p (n e)")
            nc.tensor.matmul(bank[6][:], tri[:], sel, start=True, stop=True)
            nc.tensor.matmul(bank[7][:], onesq[:], sel, start=True, stop=True).then_inc(sem("cnt_in"), 1)

        def pe_ids(pe):
            for k in range(TOPK):
                pe.wait_ge(sem("hot_in"), k + 1)
                for n in range(NT):
                    m = nc.tensor.matmul(bank[6][:, 0:SLOT_TILES], hot_p[:, k % 2, n], hot_q[:, k % 2, n],
                                         start=k == 0 and n == 0, stop=k == TOPK - 1 and n == NT - 1)
                m.then_inc(sem("ids_mm"), 1)

        def stage3_tensor(pe):
            pe_block3(pe, 0, router=True)
            pe_block3(pe, 1, between=pe_counts)
            pe_block3(pe, 2)
            pe_block3(pe, 3, between=pe_ids)

        def act_hi3(act, k):
            act.wait_ge(sem(f"raw3_in{k % 2}"), 32 * (k // 2) + 32)
            act.wait_ge(sem("kc_in"), N3)
            nc.scalar.activation(wsu[0][:, :, 2 * k * P:2 * (k + 1) * P],
                                 raw3[k % 2][:, 0].rearrange("p (c n) -> p c n", c=C), ACT.Copy).then_inc(sem("w3hi"), 1)
            nc.scalar.activation(wsd[0][:, 2 * k:2 * k + 2],
                                 raw3[k % 2][:, 1].rearrange("p (c n) -> p c n", c=2), ACT.Copy).then_inc(sem("w3hi"), 1)

        def act_block3(act, b, router=False):
            for i in range(NSI):
                act_inner(act, N3 + b * NSI + i, i)
                if i == TH_AT and router:
                    act_hi_h(act, NB - 1)
            act.wait_ge(sem("vc_done"), 2 + N3 + (b + 1) * NSI)
            act.wait_ge(sem("bs_st"), 16 * b + 16)
            for j in range(BT):
                nc.scalar.activation(so[:, j], bank[j][:], ACT.Copy).then_inc(sem("sh_in"), 1)

        def stage3_scalar(act):
            for k in range(4):
                act_hi3(act, k)
            act.wait_ge(sem("xp_st"), 16 * NB)
            act_block3(act, 0, router=True)
            with act.Fori(1, NB) as b:
                act_block3(act, b)

        def pool_numbers(pool):
            pool.wait_ge(sem("sc_in"), NB)
            nc.gpsimd.iota(iota_p[:], [[1, P]], base=0, channel_multiplier=0, allow_small_or_imprecise_dtypes=True)
            nc.gpsimd.iota(iota_q[:], [[1, SLOT_TILES]], base=0, channel_multiplier=0, allow_small_or_imprecise_dtypes=True)
            nc.gpsimd.iota(token[:], [[P, NT]], base=0, channel_multiplier=1, allow_small_or_imprecise_dtypes=True)
            nc.gpsimd.iota(four[:], [[TOPK, NT]], base=0, channel_multiplier=0, allow_small_or_imprecise_dtypes=True)
            nc.gpsimd.memset(before[:], 1.0).then_inc(sem("num_in"), 1)
            pool.wait_ge(sem("num_in"), 1)
            nc.gpsimd.affine_select(out=before[:], in_=before[:], compare_op=ALU.is_gt, fill=0.0, base=0,
                                    pattern=[[1, GROUPS], [-1, GROUPS]], channel_multiplier=0).then_inc(sem("num_in"), 1)

        def pool_block3(pool, b, numbers=False):
            for i in range(NSI):
                pool_inner(pool, N3 + b * NSI + i, i)
                if numbers and i == TH_AT + 1:
                    pool_numbers(pool)
            wait_apart(pool, sem("xps_in"), 16 * b + 16)
            for j in range(BT):
                pool.wait_ge(sem("sh_in"), b * BT + j + 1)
                nc.gpsimd.tensor_tensor(so[:, j], so[:, j], xps[:, j], ALU.add).then_inc(sem("bs_in"), 1)

        def stage3_gpsimd(pool):
            for k in range(4):
                for s, w in enumerate((wsu[0][:, :, 2 * k * P:2 * (k + 1) * P], wsd[0][:, 2 * k:2 * k + 2])):
                    lo = wsu[1][:, :, 2 * k * P:2 * (k + 1) * P] if s == 0 else wsd[1][:, 2 * k:2 * k + 2]
                    pool.wait_ge(sem("w3hi"), 2 * k + s + 1)
                    nc.gpsimd.tensor_tensor(lo, raw3[k % 2][:, s].rearrange("p (c n) -> p c n", c=(C, 2)[s]), w,
                                            ALU.subtract).then_inc(sem("w3lo"), 1)
            pool_block3(pool, 0, numbers=True)
            with pool.Fori(1, NB) as b:
                pool_block3(pool, b)

        def sp_raw3(sp, k):
            if k >= 2:
                sp.wait_ge(sem("w3lo"), 2 * (k - 2) + 2)
            sp.dma_start(raw3[k % 2][:, 0].rearrange("p (c n) -> p c n", c=C),
                         square("L0_ffn_Wsu")[:, :, 2 * k * P:2 * (k + 1) * P]).then_inc(sem(f"raw3_in{k % 2}"), 16)
            sp.dma_start(raw3[k % 2][:, 1].rearrange("p (c n) -> p c n", c=2),
                         square("L0_ffn_Wsd")[:, 2 * k:2 * k + 2]).then_inc(sem(f"raw3_in{k % 2}"), 16)

        def sp_hTb(sp, b):
            sp.dma_start(hTb[:, b % 2].bitcast(F), hT_d[b]).then_inc(sem("hb_in"), 16)

        def stage3_sync(sp):
            sp.wait_ge(sem("trT_in"), NB * C)
            sp_raw3(sp, 0)
            sp_raw3(sp, 1)
            sp.wait_ge(sem("ht_st0"), 32 + 16)
            sp.wait_ge(sem("ht_st1"), 32 + 16)
            sp.wait_ge(sem("rcp_in"), NB * BT)
            sp_hTb(sp, 0)
            sp.wait_ge(sem("xp_st"), 16 * (NB - 1))
            sp.dma_start(xps[:], xp_rows[0]).then_inc(sem("xps_in"), 16)
            sp_raw3(sp, 2)
            sp_raw3(sp, 3)
            sp.wait_ge(sem("hb_in"), 16)
            sp.wait_ge(sem("vc_done"), 2 + N3)
            sp_hTb(sp, 1)
            sp_tail2(sp, NB - 1)
            sp_hT(sp, NB - 1)
            sp.wait_ge(sem("sc_in"), NB)
            sp.dma_start(ebias[:], a["L0_ffn_e_bias"].partition_broadcast(P)).then_inc(sem("eb_in"), 16)
            for b in range(NB):
                if b + 2 < NB:
                    sp.wait_ge(sem("kc_in"), N3 + (b + 1) * NSI)
                    sp.wait_ge(sem("hb_in"), 16 * (b + 2))
                    if b + 2 == NB - 1:
                        sp.wait_ge(sem("ht_st0"), 32 * NB + 16)
                        sp.wait_ge(sem("ht_st1"), 32 * NB + 16)
                    sp_hTb(sp, b + 2)
                sp.wait_ge(sem("bs_in"), (b + 1) * BT)
                sp.dma_start(base_rows[b], so[:]).then_inc(sem("bs_st"), 16)
                if b + 1 < NB:
                    if b + 1 == NB - 1:
                        sp.wait_ge(sem("xp_st"), 16 * NB)
                    sp.dma_start(xps[:], xp_rows[b + 1]).then_inc(sem("xps_in"), 16)

        def routing_vector(dve):
            st = Steps(dve, sem("route"))
            v = nc.vector

            def run(instruction):
                st.do(instruction)
                st.sync()
            tt = lambda o, x, y, op: run(v.tensor_tensor(o, x, y, op))
            dve.wait_ge(sem("eb_in"), 16)
            dve.wait_ge(sem("num_in"), 2)
            sfc, wa, wb, sel, wc, wd = (m[:] for m in big)
            sc = scores[:]
            per_tile = lambda m: m.unsqueeze(2).to_broadcast([P, NT, E])
            tt(sfc, sc, ebias[:].unsqueeze(1).to_broadcast([P, NT, E]), ALU.add)
            g8 = sfc.rearrange("p n (g k) -> p (n g) k", k=8)
            hi, lo = (m.rearrange("p n e -> p (n e)")[:, 0:256].rearrange("p (g k) -> p g k", k=4) for m in (wa, wb))
            t, u = (m.rearrange("p n e -> p (n e)")[:, 256:384].rearrange("p (g k) -> p g k", k=2) for m in (wa, wb))
            tt(hi, g8[:, :, 0:4], g8[:, :, 4:8], ALU.max)
            tt(lo, g8[:, :, 0:4], g8[:, :, 4:8], ALU.min)
            for w in (2, 1):
                a0, a1, b0, b1 = hi[:, :, 0:w], hi[:, :, w:2 * w], lo[:, :, 0:w], lo[:, :, w:2 * w]
                tt(t[:, :, 0:w], a0, a1, ALU.min)
                tt(u[:, :, 0:w], b0, b1, ALU.max)
                tt(a0, a0, a1, ALU.max)
                tt(b0, t[:, :, 0:w], u[:, :, 0:w], ALU.max)
            gs = small[:, 0].rearrange("p (n g) -> p n g", g=GROUPS)
            tt(gs, hi[:, :, 0].rearrange("p (n g) -> p n g", g=GROUPS), lo[:, :, 0].rearrange("p (n g) -> p n g", g=GROUPS), ALU.add)
            shape4 = [P, NT, GROUPS, GROUPS]
            other, own = gs.unsqueeze(2).to_broadcast(shape4), gs.unsqueeze(3).to_broadcast(shape4)
            gt4, eq4 = (m.rearrange("p n e -> p (n e)")[:, 0:256].rearrange("p (n g j) -> p n g j", g=GROUPS, j=GROUPS)
                        for m in (wc, wd))
            tt(gt4, other, own, ALU.is_gt)
            tt(eq4, other, own, ALU.is_equal)
            tt(eq4, eq4, before[:].unsqueeze(1).to_broadcast(shape4), ALU.mult)
            tt(gt4, gt4, eq4, ALU.add)
            gm = small[:, 1].rearrange("p (n g) -> p n g", g=GROUPS)
            run(v.tensor_reduce(gm, gt4, AX, ALU.add))
            run(v.tensor_scalar(gm, gm, 1.5, None, ALU.is_lt))
            tt(g8, g8, small[:, 1].unsqueeze(2).to_broadcast([P, NT * GROUPS, 8]), ALU.mult)
            for n in range(NT):
                st.do(v.max(top8[:, n], sfc[:, n]))
            st.sync()
            fourth = per_tile(top8[:, :, TOPK - 1])
            tt(wa, sfc, fourth, ALU.is_gt)
            tt(wb, sfc, fourth, ALU.is_equal)
            flat = lambda m: m.rearrange("p n e -> p (n e)")
            ones_row = onesq[:, 0:1].to_broadcast([P, NT * E])
            run(v.tensor_tensor_scan(flat(wc), ones_row, flat(wb), 0.0, ALU.mult, ALU.add))
            room = small[:, 2, 0:NT]
            st.do(v.memset(small[:, 3, 0:1], 0.0))
            run(v.tensor_copy(small[:, 3, 1:NT], wc[:, 0:NT - 1, E - 1]))
            run(v.tensor_reduce(room, wa, AX, ALU.add))
            tt(room, small[:, 3, 0:NT], room, ALU.subtract)
            run(v.tensor_scalar(room, room, float(TOPK), None, ALU.add))
            tt(wc, wc, per_tile(room), ALU.is_le)
            tt(wb, wb, wc, ALU.mult)
            st.do(v.tensor_tensor(sel, wa, wb, ALU.add))
            st.sync()
            v.tensor_scalar(small[:, 4, 0:1], small[:, 3, 0:1], 1.0, None, ALU.mult).then_inc(sem("sel_in"), 1)
            tt(wa, sc, sel, ALU.mult)
            den = small[:, 5, 0:NT]
            run(v.tensor_reduce(den, wa, AX, ALU.add))
            run(v.tensor_scalar(den, den, 1e-20, None, ALU.add))
            run(v.reciprocal(den, den))
            tt(wa, wa, per_tile(den), ALU.mult)
            run(v.tensor_scalar(wa, wa, ROUTE_SCALE, None, ALU.mult))
            run(v.tensor_tensor_scan(flat(wb), ones_row, flat(sel), 0.0, ALU.mult, ALU.add))
            tt(wb, wb, per_tile(four[:]), ALU.subtract)
            tt(wb, wb, sel, ALU.mult)
            dve.wait_ge(sem("cnt_in"), 1)
            run(v.tensor_copy(flat(wd), bank[7][:]))
            st.do(v.memset(wc[:, 0], 0.0))
            st.sync()
            for n in range(1, NT):
                tt(wc[:, n], wc[:, n - 1], wd[:, n - 1], ALU.add)
            cnt = small[:, 6, 0:E]
            tiles_of = small[:, 6, E:2 * E]
            tt(cnt, wc[:, NT - 1], wd[:, NT - 1], ALU.add)
            run(v.tensor_scalar(cnt, cnt, float(P - 1), None, ALU.add))
            run(v.tensor_copy(smi[:, 0, 0:E], cnt))
            run(v.tensor_scalar(smi[:, 1, 0:E], smi[:, 0, 0:E], 7, None, ALU.arith_shift_right))
            run(v.tensor_copy(tiles_of, smi[:, 1, 0:E]))
            run(v.tensor_scalar(tiles_of, tiles_of, 1.0, None, ALU.max))
            ends, first = small[:, 7, 0:E], small[:, 7, E:2 * E]
            run(v.tensor_tensor_scan(ends, onesq[:, 0:E], tiles_of, 0.0, ALU.mult, ALU.add))
            tt(first, ends, tiles_of, ALU.subtract)
            run(v.tensor_scalar(first, first, float(P), None, ALU.mult))
            run(v.tensor_copy(ends_i[:], ends))
            tt(flat(wc), flat(wc), bank[6][:], ALU.add)
            tt(wc, wc, first.unsqueeze(1).to_broadcast([P, NT, E]), ALU.add)
            slot_f = small[:, 0]
            for k in range(TOPK):
                st.do(v.scalar_tensor_tensor(out=wd, in0=wb, scalar=float(k + 1), in1=wc, op0=ALU.is_equal, op1=ALU.mult))
                run(v.scalar_tensor_tensor(out=sfc, in0=wb, scalar=float(k + 1), in1=wa, op0=ALU.is_equal, op1=ALU.mult))
                st.do(v.tensor_reduce(slot_f[:, k * NT:(k + 1) * NT], wd, AX, ALU.add))
                run(v.tensor_reduce(share[:, k], sfc, AX, ALU.add))
            slot_flat = slot_i[:].rearrange("p k n -> p (k n)")
            run(v.tensor_copy(slot_flat, slot_f))
            st.do(v.tensor_scalar(smi[:, 0], slot_flat, 7, None, ALU.arith_shift_right))
            run(v.tensor_scalar(smi[:, 1], slot_flat, P - 1, None, ALU.bitwise_and))
            q, r = small[:, 1], small[:, 2]
            st.do(v.tensor_copy(q, smi[:, 0]))
            run(v.tensor_copy(r, smi[:, 1]))
            for k in range(TOPK):
                if k >= 2:
                    dve.wait_ge(sem("ids_mm"), k - 1)
                col = lambda m: m[:, k * NT:(k + 1) * NT]
                st.do(v.tensor_tensor(hot_p[:, k % 2], iota_p[:].unsqueeze(1).to_broadcast([P, NT, P]),
                                      col(r).unsqueeze(2).to_broadcast([P, NT, P]), ALU.is_equal))
                shape_q = [P, NT, SLOT_TILES]
                run(v.tensor_tensor(hot_q[:, k % 2], iota_q[:].unsqueeze(1).to_broadcast(shape_q),
                                    col(q).unsqueeze(2).to_broadcast(shape_q), ALU.is_equal))
                v.tensor_tensor(hot_q[:, k % 2], hot_q[:, k % 2], token[:].unsqueeze(2).to_broadcast(shape_q),
                                ALU.mult).then_inc(sem("hot_in"), 1)
            for m in range(SLOT_TILES // E):
                sh = [P, E, E]
                run(v.tensor_tensor(cmp4[:], ends.unsqueeze(1).to_broadcast(sh),
                                    iota_q[:, m * E:(m + 1) * E].unsqueeze(2).to_broadcast(sh), ALU.is_le))
                run(v.tensor_reduce(small[:, 3 + m // 2, (m % 2) * E:(m % 2) * E + E], cmp4[:], AX, ALU.add))
            owner = small[:, 3:5].rearrange("p a b -> p (a b)")[:, 0:SLOT_TILES]
            run(v.tensor_scalar(owner, owner, float(E - 1), None, ALU.min))
            packed = small[:, 6:8].rearrange("p a b -> p (a b)")[:, 0:SLOT_TILES]
            run(v.tensor_copy(packed, owner))
            for k in range(1, GROUP):
                run(v.scalar_tensor_tensor(out=packed[:, 0:SLOT_TILES - k], in0=owner[:, k:], scalar=float(1 << OWNER_BITS * k),
                                           in1=packed[:, 0:SLOT_TILES - k], op0=ALU.mult, op1=ALU.add))
            run(v.tensor_scalar(passes_i[:, 1:2], ends_i[:, E - 1:E], 1, None, ALU.subtract))
            run(v.tensor_scalar(passes_i[:, 0:1], passes_i[:, 1:2], 2, None, ALU.arith_shift_right))
            v.tensor_copy(owner_i[:], packed).then_inc(sem("owner_in"), 1)
            dve.wait_ge(sem("ids_mm"), TOPK)
            v.tensor_copy(ids[:], bank[6][:, 0:SLOT_TILES]).then_inc(sem("ids_in"), 1)

        N4 = N3 + NB * NSI
        def passes_of(engine):
            return engine.value_load(passes_i[0:1, 0:1], min_val=E // GROUP - 1, max_val=SLOT_TILES // GROUP - 1)

        def owners(engine, g, n=GROUP):
            word = engine.value_load(owner_i[0:1, bass.ds(g, 1)], min_val=0, max_val=(1 << OWNER_BITS * GROUP) - 1)
            return [(word >> OWNER_BITS * k) & E - 1 for k in range(n)]

        def slot_of(ring, e):
            return ring[:, bass.ds(e & 3, 1)].rearrange("p a n -> p (a n)")

        def stage4_tensor(pe):
            def tin(g, u):
                pe.wait_ge(sem(f"xg_in{u}"), (g - u) * 8 + 16)
                pe.wait_ge(sem("xt4"), g + 1)
                for c in range(C):
                    m = nc.tensor.transpose(bank[u][:, c * P:(c + 1) * P], xg[:, u, c * P:(c + 1) * P], ident[:])
                m.then_inc(sem("t4"), 1)

            def up(g, u, e):
                pe.wait_ge(sem("win"), e + 1)
                pe.wait_ge(sem("xt4"), g + 3)
                pe.wait_ge(sem("r4"), g + 1)
                for c in range(C):
                    m = nc.tensor.matmul(bank[2 + u][:, 0:EI], xT4[:, u, c * P:(c + 1) * P],
                                         slot_of(wu4[:, :, c * EI:(c + 1) * EI], e), start=c == 0, stop=c == C - 1)
                m.then_inc(sem("u4"), 1)

            def turn(g, u):
                pe.wait_ge(sem("s4"), g + 1)
                pe.wait_ge(sem("al4"), g + 1)
                for c in range(EI // P):
                    m = nc.tensor.transpose(bank[4 + u][:, c * P:(c + 1) * P], a4[:, u, c * P:(c + 1) * P], ident[:])
                m.then_inc(sem("at4"), 1)

            def down(g, u):
                pe.wait_ge(sem("al4"), g + 3)
                pe.wait_ge(sem("wl4"), g + 1)
                pe.wait_ge(sem("wlb4"), g + 1)
                pe.wait_ge(sem("y4"), g + 1)
                split_product(bank[6 + u][:], lambda s, c: aT4[:, u, s, c * P:(c + 1) * P],
                              lambda s, c: wds[:, u, s, c * H:(c + 1) * H], EI // P).then_inc(sem("d4"), 1)

            def step(g, u, e):
                up(g, u, e)
                tin(g + 1, 1 - u)
                down(g - 1, 1 - u)
                turn(g, u)

            pe.wait_ge(sem("bs_in"), NB * BT)
            pe.wait_ge(sem("owner_in"), 1)
            passes = passes_of(pe)
            tin(0, 0)
            up(0, 0, owners(pe, 0)[0])
            tin(1, 1)
            turn(0, 0)
            with pe.Fori(0, passes) as i:
                for k, e in enumerate(owners(pe, GROUP * i + 1)):
                    step(GROUP * i + 1 + k, (1 + k) % 2, e)
            last = GROUP * passes + GROUP - 1
            e0, e1, e2 = owners(pe, last - 2, 3)
            step(last - 2, 1, e0)
            step(last - 1, 0, e1)
            up(last, 1, e2)
            down(last - 1, 0)
            turn(last, 1)
            down(last, 1)

        def stage4_scalar(act):
            def x_in(g, u):
                act.wait_ge(sem("t4"), g + 1)
                act.wait_ge(sem("u4"), g + 1)
                nc.scalar.activation(xT4[:, u], bank[u][:], ACT.Copy).then_inc(sem("xt4"), 1)

            def relu(g, u):
                act.wait_ge(sem("u4"), g + 3)
                act.wait_ge(sem("at4"), g + 1)
                nc.scalar.activation(a4[:, u], bank[2 + u][:, 0:EI], ACT.Relu).then_inc(sem("r4"), 1)

            def a_hi(g, u):
                act.wait_ge(sem("at4"), g + 3)
                act.wait_ge(sem("d4"), g + 1)
                nc.scalar.activation(aT4[:, u, 0], bank[4 + u][:, 0:EI], ACT.Copy).then_inc(sem("ah4"), 1)

            def w_hi(g, u, e):
                act.wait_ge(sem("d4"), g + 1)
                wait_apart(act, sem("win"), e + 1)
                nc.scalar.activation(wds[:, u, 0], slot_of(wd4, e), ACT.Copy).then_inc(sem("wh4"), 1)

            def store(g, u):
                wait_apart(act, sem("y4"), g + 3)
                act.dma_start(y_d[bass.ds(g * P, P)], yo[:, u]).then_inc(sem(f"y_st{u}"), 16)

            def step(g, u, e, stores=True, more=True):
                a_hi(g - 1, 1 - u)
                w_hi(g, u, e)
                relu(g, u)
                if more:
                    x_in(g + 1, 1 - u)
                if stores:
                    store(g - 2, u)

            act.wait_ge(sem("vc_done"), 2 + N4)
            act.wait_ge(sem("owner_in"), 1)
            passes = passes_of(act)
            act.wait_ge(sem("y_fill"), 16 * NB * NCI)
            e0, e1 = owners(act, 0, 2)
            w_hi(0, 0, e0)
            x_in(0, 0)
            relu(0, 0)
            x_in(1, 1)
            step(1, 1, e1, stores=False)
            with act.Fori(0, passes) as i:
                for k, e in enumerate(owners(act, GROUP * i + 2)):
                    step(GROUP * i + 2 + k, k % 2, e)
            last = GROUP * passes + GROUP - 1
            e0, e1 = owners(act, last - 1, 2)
            step(last - 1, 0, e0)
            step(last, 1, e1, more=False)
            a_hi(last, 1)
            store(last - 1, 0)
            store(last, 1)

        HALF_W = EI // P * H // 2

        def stage4_vector(dve):
            def square4(g, u):
                dve.wait_ge(sem("r4"), g + 3)
                nc.vector.tensor_tensor(a4[:, u], a4[:, u], a4[:, u], ALU.mult).then_inc(sem("s4"), 1)

            def a_lo(g, u):
                dve.wait_ge(sem("ah4"), g + 1)
                nc.vector.tensor_tensor(aT4[:, u, 1], bank[4 + u][:, 0:EI], aT4[:, u, 0],
                                        ALU.subtract).then_inc(sem("al4"), 1)

            def w_lo(g, u, e):
                dve.wait_ge(sem("wh4"), g + 1)
                nc.vector.tensor_tensor(wds[:, u, 1, 0:HALF_W], slot_of(wd4[:, :, 0:HALF_W], e),
                                        wds[:, u, 0, 0:HALF_W], ALU.subtract).then_inc(sem("wl4"), 1)

            def take_y(g, u):
                dve.wait_ge(sem("d4"), g + 3)
                dve.wait_ge(sem(f"y_st{u}"), (g - u) * 8 + 16)
                nc.vector.tensor_copy(yo[:, u], bank[6 + u][:]).then_inc(sem("y4"), 1)

            def step(g, u, e):
                a_lo(g - 1, 1 - u)
                w_lo(g, u, e)
                square4(g, u)
                take_y(g - 1, 1 - u)

            dve.wait_ge(sem("owner_in"), 1)
            passes = passes_of(dve)
            w_lo(0, 0, owners(dve, 0)[0])
            square4(0, 0)
            with dve.Fori(0, passes) as i:
                for k, e in enumerate(owners(dve, GROUP * i + 1)):
                    step(GROUP * i + 1 + k, (1 + k) % 2, e)
            last = GROUP * passes + GROUP - 1
            for k, e in enumerate(owners(dve, last - 2, 3)):
                step(last - 2 + k, (1 + k) % 2, e)
            a_lo(last, 1)
            take_y(last, 1)

        def stage4_gpsimd(pool):
            def gather(g, u):
                nc.gpsimd.tensor_copy(idc[:, u:u + 1], ids[:, bass.ds(g, 1)]).then_inc(sem("idc_in"), 1)
                wait_apart(pool, sem("idc_in"), g + 1)
                pool.indirect_dma_start(out=xg[:, u], out_offset=None, in_=h_d,
                                        in_offset=bass.IndirectOffsetOnAxis(ap=idc[:, u:u + 1].bitcast(U32), axis=0)
                                        ).then_inc(sem(f"xg_in{u}"), 16)

            def w_lo(g, u, e):
                wait_apart(pool, sem("wh4"), g + 1)
                nc.gpsimd.tensor_tensor(wds[:, u, 1, HALF_W:], slot_of(wd4[:, :, HALF_W:], e),
                                        wds[:, u, 0, HALF_W:], ALU.subtract).then_inc(sem("wlb4"), 1)

            def step(g, u, e):
                wait_apart(pool, sem("t4"), g + 1)
                gather(g + 2, u)
                w_lo(g, u, e)

            pool.wait_ge(sem("owner_in"), 1)
            pool.wait_ge(sem("ids_in"), 1)
            pool.wait_ge(sem("h_st"), 16 * NB + 16)
            passes = passes_of(pool)
            gather(0, 0)
            gather(1, 1)
            with pool.Fori(0, passes) as i:
                for k, e in enumerate(owners(pool, GROUP * i)):
                    step(GROUP * i + k, k % 2, e)
            last = GROUP * passes + GROUP - 1
            e0, e1, e2, e3 = owners(pool, last - 3)
            step(last - 3, 0, e0)
            step(last - 2, 1, e1)
            w_lo(last - 1, 0, e2)
            w_lo(last, 1, e3)

        def stage4_sync(sp):
            wu_rows = a["L0_ffn_Wu"].rearrange("e (c p) i -> e p c i", p=P)
            wd_rows = a["L0_ffn_Wd"].rearrange("e (c p) i -> e p c i", p=P)

            def load(e, s):
                sp.dma_start(wu4[:, s].rearrange("p (c n) -> p c n", c=C),
                             wu_rows[bass.ds(e, 1)].rearrange("a p c i -> p (a c) i")).then_inc(sem(f"w4_in{s}"), 16)
                sp.dma_start(wd4[:, s].rearrange("p (c n) -> p c n", n=H),
                             wd_rows[bass.ds(e, 1)].rearrange("a p c i -> p (a c) i")).then_inc(sem(f"w4_in{s}"), 16)

            def landed(r, s):
                wait_apart(sp, sem(f"w4_in{s}"), 32 * r + 32)
                sp.sem_inc(sem("win"), 1)

            sp.wait_ge(sem("w3lo"), 8)
            sp.wait_ge(sem("lg_in"), NB)
            for s in range(4):
                load(s, s)
                if s:
                    landed(0, s - 1)
            sp.wait_ge(sem("owner_in"), 1)
            with sp.Fori(1, E // 4) as r:
                for s in range(4):
                    end = sp.value_load(ends_i[0:1, bass.ds(4 * r + s - 4, 1)], min_val=1, max_val=SLOT_TILES)
                    wait_apart(sp, sem("d4"), end + 2)
                    load(4 * r + s, s)
                    landed(r if s else r - 1, (s - 1) % 4)
            landed(E // 4 - 1, 3)

        def stage5_gpsimd(pool):
            passes = passes_of(pool)
            for u in range(2):
                wait_apart(pool, sem(f"y_st{u}"), 8 * GROUP * passes + 8 * GROUP + 16)

            def fetch(n, u):
                nc.gpsimd.tensor_copy(idc5[:, u], slot_i[:, :, bass.ds(n, 1)].rearrange("p k a -> p (k a)")).then_inc(sem("idc5_in"), 1)
                wait_apart(pool, sem("idc5_in"), n + 1)
                for k in range(TOPK):
                    pool.indirect_dma_start(out=yg[:, u, k], out_offset=None, in_=y_d,
                                            in_offset=bass.IndirectOffsetOnAxis(ap=idc5[:, u, k:k + 1].bitcast(U32), axis=0)
                                            ).then_inc(sem(f"yg_in{u}{k}"), 16)
            fetch(0, 0)
            fetch(1, 1)
            with pool.Fori(1, NT // 2) as i:
                for n, u in ((2 * i, 0), (2 * i + 1, 1)):
                    wait_apart(pool, sem("o5"), TOPK * (n - 1))
                    fetch(n, u)

        def stage5_vector(dve):
            with dve.Fori(0, NT // 2) as i:
                for n, u in ((2 * i, 0), (2 * i + 1, 1)):
                    wait_apart(dve, sem(f"acc_in{u}"), 16 * i + 16)
                    for k in range(TOPK):
                        wait_apart(dve, sem(f"yg_in{u}{k}"), 16 * i + 16)
                        nc.vector.scalar_tensor_tensor(out=acc[:, u], in0=yg[:, u, k],
                                                       scalar=share[:, k, bass.ds(n, 1)], in1=acc[:, u],
                                                       op0=ALU.mult, op1=ALU.add).then_inc(sem("o5"), 1)
                        wait_apart(dve, sem("o5"), TOPK * n + k + 1)

        def stage5_sync(sp):
            sp.wait_ge(sem("bs_st"), 16 * NB + 16)
            for u in range(2):
                sp.dma_start(acc[:, u], base_d[u * P:(u + 1) * P]).then_inc(sem(f"acc_in{u}"), 16)
            def emit(n, u, i, more=True):
                wait_apart(sp, sem("o5"), TOPK * (n + 1))
                sp.dma_start(out[0, bass.ds(n * P, P)], acc[:, u]).then_inc(sem(f"o_st{u}"), 16)
                if more:
                    wait_apart(sp, sem(f"o_st{u}"), 16 * i + 16)
                    sp.dma_start(acc[:, u], base_d[bass.ds((n + 2) * P, P)]).then_inc(sem(f"acc_in{u}"), 16)
            with sp.Fori(0, NT // 2 - 1) as i:
                emit(2 * i, 0, i)
                emit(2 * i + 1, 1, i)
            emit(NT - 2, 0, NT // 2 - 1, more=False)
            emit(NT - 1, 1, NT // 2 - 1, more=False)
            for u in range(2):
                sp.wait_ge(sem(f"o_st{u}"), 16 * (NT // 2))

        @block.sync
        def _(sp):
            stage1_sync(sp)
            stage2_sync(sp)
            stage3_sync(sp)
            stage4_sync(sp)
            stage5_sync(sp)

        @block.gpsimd
        def _(pool):
            stage1_gpsimd(pool)
            stage2_gpsimd(pool)
            stage3_gpsimd(pool)
            stage4_gpsimd(pool)
            stage5_gpsimd(pool)

        @block.scalar
        def _(act):
            stage1_scalar(act)
            stage2_scalar(act)
            stage3_scalar(act)
            stage4_scalar(act)

        @block.vector
        def _(dve):
            stage1_vector(dve)
            stage2_vector(dve)
            routing_vector(dve)
            stage4_vector(dve)
            stage5_vector(dve)

        @block.tensor
        def _(pe):
            stage1_tensor(pe)
            stage2_tensor(pe)
            stage3_tensor(pe)
            stage4_tensor(pe)


def kernel(**inputs):
    import numpy as _np
    import concourse.bacc as _bacc
    from concourse import mybir as _mybir
    from concourse.bass_utils import run_bass_kernel_spmd as _run

    nc = _bacc.Bacc("TRN2", target_bir_lowering=False, num_devices=1)
    arrays, args = {}, {}
    for name, value in inputs.items():
        v = _np.ascontiguousarray(value)
        arrays[f"in_{name}"] = v
        args[name] = nc.dram_tensor(f"in_{name}", v.shape, _mybir.dt.from_np(v.dtype), kind="ExternalInput").ap()
    out = nc.dram_tensor("out", (1, T, H), _mybir.dt.float32, kind="ExternalOutput").ap()
    program(nc, args, out, lambda name, shape: nc.dram_tensor(name, shape, F).ap())
    r = _run(nc, [arrays], core_ids=[0])
    return r.results[0]["out"]
```

```python
import concourse.bass as bass
from concourse import mybir
from contextlib import ExitStack

F = mybir.dt.float32
R = mybir.dt.float32r
HALF = mybir.dt.float16
I32 = mybir.dt.int32
U32 = mybir.dt.uint32
ALU = mybir.AluOpType
ACT = mybir.ActivationFunctionType
AX = mybir.AxisListType.X

P = 128
T, H = 2048, 512
NT = T // P
BT = 4
NB = NT // BT
BLK = BT * P
C = H // P
CI = 2048
NCI = CI // P
SI = 1024
NSI = SI // P
E, EI, TOPK, GROUPS = 32, 256, 4, 4
ROUTE_SCALE = 2.5
EPS_OUT, EPS_IN = 1e-5, 1e-12
SLOT_TILES = T * TOPK // P + E
GROUP = 8
GROUP_BITS = 3
PACK = 4
OWNER_BITS = 5
assert E == 1 << OWNER_BITS and GROUP == 1 << GROUP_BITS and SLOT_TILES % GROUP == 0
KB = 1024
SBUF0 = 16512


class Steps:

    def __init__(self, engine, sem, base=0):
        self.engine, self.sem, self.base, self.k = engine, sem, base, 0

    def do(self, instruction):
        self.k += 1
        instruction.then_inc(self.sem, 1)
        return self.k

    def sync(self, apart=False):
        (wait_apart if apart else type(self.engine).wait_ge)(self.engine, self.sem, self.base + self.k)


def wait_apart(engine, sem, value):
    engine.wait_ge(sem, value)
    engine.nop(nofuse=True)


def program(nc, a, out, scratch):
    ctx = ExitStack()
    sem_names = {}

    def sem(name):
        if name not in sem_names:
            sem_names[name] = ctx.enter_context(nc.semaphore(name))
        return sem_names[name]

    def at(name, shape, dt, kb):
        return nc.alloc_sbuf_tensor_at(name, shape, dt, offset=SBUF0 + int(kb * KB))

    with ctx:
        assert SLOT_TILES - E == NB * NCI
        z_d = scratch("z_d", [T, H])
        wcv_d = scratch("wcv_d", [NCI, P, 2 * H])
        xp_d = scratch("xp_d", [T, H])
        h_d = scratch("h_d", [T, H])
        hT_d = scratch("hT_d", [NB, P, 2, C, BLK])
        z_rows, xp_rows, h_rows = (m.rearrange("(b j p) d -> b p j d", j=BT, p=P) for m in (z_d, xp_d, h_d))
        base_d = scratch("base_d", [T, H])
        y_d = scratch("y_d", [SLOT_TILES * P, H])
        y_spare = y_d.rearrange("(m p) d -> m p d", p=P)[E:]
        base_rows = base_d.rearrange("(b j p) d -> b p j d", j=BT, p=P)
        ident = at("ident", [P, P], F, 200.5)
        onesq = at("onesq", [P, P], F, 201)
        sbc = at("sbc", [P, H], F, 201.5)
        tf = at("tf", [P, C], F, 203.5)
        omtf = at("omtf", [P, C], F, 203.53125)
        ages = at("ages", [P, NT], F, 203.5625)
        mean0 = at("mean0", [P, NT], F, 203.625)
        rstd0 = at("rstd0", [P, NT], F, 203.6875)
        zrow = at("zrow", [P, H], HALF, 203.75)
        nsc = at("nsc", [P, 16, BT], F, 204.75)
        nsci = at("nsci", [P, 2, BT], I32, 205)
        bns = at("bns", [P, BT, 6], F, 205.0625)
        bna = at("bna", [P, BT, 2], F, 205.1875)
        tri = at("tri", [P, P], F, 205.25)
        wck = [at(f"wck_{s}", [P, C, CI], R, 32 * n) for n, s in enumerate(("hi", "lo"))]
        wcr = [at(f"wcr_{s}", [P, C, H], R, 64 + 8 * n) for n, s in enumerate(("hi", "lo"))]
        g1b = at("g1b", [P, 4, H], F, 80)
        tdb = at("tdb", [P, H], F, 88)
        bob = at("bob", [P, H], F, 90)
        xb = at("xb", [P, BT, H], F, 92)
        x1 = at("x1", [P, BT, H], F, 100)
        xln = at("xln", [P, BT, H], F, 108)
        dec = at("dec", [P, BT, H], F, 116)
        xlnT = at("xlnT", [P, C, BLK + 1], F, 124)
        mx = at("mx", [P, C, BLK], F, 132.25)
        mixT = [at(f"mixT_{s}", [P, C, BLK], R, 140.25 + 8 * n) for n, s in enumerate(("hi", "lo"))]
        zo = at("zo", [P, 2, H], F, 156.25)
        wr = [at(f"wr_{s}", [P, C, H], R, 160.25 + 8 * n) for n, s in enumerate(("hi", "lo"))]
        raw = at("raw", [P, C * H], F, 176.25)
        stage = at("stage", [P, C, 2, H], R, 184.25)
        wv = at("wv", [P, C, H], F, 92)
        wo = at("wo", [P, C, H], F, 116)
        pv = at("pv", [P, C, H], F, 100)
        vmb = at("vmb", [P, C, P], F, 132.25)
        vm = at("vm", [P, C], F, 136)

        vring = at("vring", [P, 4, 2 * H], R, 80)
        g2b = at("g2b", [P, 4, H], F, 96)
        f1 = at("f1", [P, 2, BT, H], F, 104)
        f2 = at("f2", [P, BT, H], F, 120)
        hb = at("hb", [P, BT, H], F, 128)
        xcT = [at(f"xcT_{s}", [P, C, BLK + 1], R, 136 + 8.0625 * n) for n, s in enumerate(("hi", "lo"))]
        rc = at("rc", [P, BT, H], F, 152.5)
        ra = at("ra", [P, 2, BLK], F, 160.5)
        ksp = [at(f"ksp_{s}", [P, 2, BLK], R, 164.5 + 4 * n) for n, s in enumerate(("hi", "lo"))]
        hT = [at(f"hT_{c}", [P, 2, BLK], R, kb) for c, kb in enumerate((172.5, 176.5, 196, 186))]
        gw = [at(f"gw_{s}", [P, C, E], R, 180.5 + 0.5 * n) for n, s in enumerate(("hi", "lo"))]
        gwf = at("gwf", [P, C, E], F, 181.5)
        sgT = at("sgT", [E, BLK], F, 182)
        tmp = at("tmp", [P, BT, H], F, 186)
        scores = at("scores", [P, NT, E], F, 194)

        wsu = [at(f"wsu_{s}", [P, C, SI], R, 16 * n) for n, s in enumerate(("hi", "lo"))]
        wsd = [at(f"wsd_{s}", [P, NSI, H], R, 32 + 16 * n) for n, s in enumerate(("hi", "lo"))]
        hTb = at("hTb", [P, 2, 2, C, BLK], R, 64)
        xps = at("xps", [P, BT, H], F, 104)
        so = at("so", [P, BT, H], F, 112)
        raw3 = [at("raw3a", [P, 2, C * 2 * P], F, 120), at("raw3b", [P, 2, C * 2 * P], F, 96)]
        big = [at(f"big{n}", [P, NT, E], F, kb) for n, kb in enumerate((186, 188, 190, 192, 196, 198))]
        cmp4 = at("cmp4", [P, E, E], F, 186)
        hot_p = at("hot_p", [P, 2, NT, P], HALF, 172.5)
        hot_q = at("hot_q", [P, 2, NT, SLOT_TILES], HALF, 152.5)
        iota_p = at("iota_p", [P, P], F, 180.5)
        iota_q = at("iota_q", [P, SLOT_TILES], F, 181)
        token = at("token", [P, NT], F, 181.375)
        four = at("four", [P, NT], F, 181.4375)
        before = at("before", [P, GROUPS, GROUPS], F, 181.5)
        top8 = at("top8", [P, NT, 8], F, 181.5625)
        ebias = at("ebias", [P, E], F, 182.0625)
        small = at("small", [P, 8, NT * GROUPS], F, 182.1875)
        smi = at("smi", [P, 2, NT * GROUPS], I32, 184.1875)
        slot_i = at("slot_i", [P, TOPK, NT], I32, 184.6875)
        share = at("share", [P, TOPK, NT], F, 184.9375)
        ends_i = at("ends_i", [P, E], I32, 185.1875)
        owner_i = at("owner_i", [P, SLOT_TILES], I32, 185.3125)
        passes_i = at("passes_i", [P, 2], I32, 185.6875)
        ids = at("ids", [P, SLOT_TILES], I32, 206.0)
        wu4 = at("wu4", [P, 4, C * EI], F, 120)
        wd4 = at("wd4", [P, 4, EI // P * H], F, 136)
        xg = at("xg", [P, 2, H], F, 96)
        xT4 = at("xT4", [P, 2, C * P], F, 0)
        a4 = at("a4", [P, 2, EI], F, 8)
        aT4 = at("aT4", [P, 2, 2, EI], R, 10)
        yo = at("yo", [P, 2, H], F, 14)
        wds = at("wds", [P, 2, 2, EI // P * H], R, 34)
        idc = at("idc", [P, 2], I32, 100)
        yg = at("yg", [P, 2, TOPK, H], F, 52)
        acc = at("acc", [P, 2, H], F, 68)
        idc5 = at("idc5", [P, 2, TOPK], I32, 100.0625)

        bank = [ctx.enter_context(nc.psum_tensor(f"bank{i}", [P, 512], F)) for i in range(8)]
        block = ctx.enter_context(nc.Block())

        RSQRT_STEPS = 3 + 9

        def rsqrt(dve, st, v, y):
            half, t = nsci[:, 0], nsc[:, 15]
            st.do(nc.vector.tensor_scalar(half, v.bitcast(I32), 1, None, ALU.logical_shift_right))
            st.sync()
            st.do(nc.vector.tensor_scalar(nsci[:, 1], half, -1.0, float(0x5F3759DF), ALU.mult, ALU.add))
            st.sync()
            st.do(nc.vector.tensor_copy(y, nsci[:, 1].bitcast(F)))
            for _ in range(3):
                st.sync()
                st.do(nc.vector.scalar_tensor_tensor(out=t, in0=y, scalar=-0.5, in1=y, op0=ALU.mult, op1=ALU.mult))
                st.sync()
                st.do(nc.vector.tensor_tensor(t, t, v, ALU.mult))
                st.sync()
                st.do(nc.vector.scalar_tensor_tensor(out=y, in0=t, scalar=1.5, in1=y, op0=ALU.add, op1=ALU.mult))
            st.sync()

        STATS_STEPS = 2 * BT + 1
        S1 = 2 * STATS_STEPS + 3 * RSQRT_STEPS + 6 + 3 * BT - 1

        def stats(dve, st, src, eps):
            for j in range(BT):
                st.do(nc.vector.bn_stats(bns[:, j], src[:, j]))
            st.sync(apart=True)
            for j in range(BT):
                st.do(nc.vector.bn_aggr(bna[:, j], bns[:, j]))
            st.sync()
            st.do(nc.vector.tensor_scalar(nsc[:, 1], bna[:, :, 1], eps, None, ALU.add))
            st.sync()

        def dve_norms1(dve, b):
            st = Steps(dve, sem("s1_dve"), b * S1)
            dve.wait_ge(sem("x_in"), 16 * b + 16)
            stats(dve, st, xb, EPS_OUT)
            rsqrt(dve, st, nsc[:, 1], nsc[:, 2])
            mean_b, rstd_b = mean0[:, bass.ds(b * BT, BT)], rstd0[:, bass.ds(b * BT, BT)]
            st.do(nc.vector.tensor_scalar(mean_b, bna[:, :, 0], 1.0, None, ALU.mult))
            st.do(nc.vector.tensor_scalar(rstd_b, nsc[:, 2], 1.0, None, ALU.mult))
            st.do(nc.vector.tensor_tensor(nsc[:, 3], nsc[:, 2], nsc[:, 2], ALU.mult))
            st.sync()
            st.do(nc.vector.tensor_tensor(nsc[:, 3], nsc[:, 3], bna[:, :, 1], ALU.mult))
            st.sync()
            st.do(nc.vector.tensor_scalar(nsc[:, 3], nsc[:, 3], EPS_IN, None, ALU.add))
            st.sync()
            rsqrt(dve, st, nsc[:, 3], nsc[:, 4])
            st.do(nc.vector.tensor_tensor(nsc[:, 4], nsc[:, 4], nsc[:, 2], ALU.mult))
            st.sync()
            for j in range(BT):
                i = nc.vector.scalar_tensor_tensor(out=x1[:, j], in0=xb[:, j], scalar=bna[:, j, 0:1],
                                                   in1=g1b[:, 0], op0=ALU.subtract, op1=ALU.mult)
                i.then_inc(sem("x_free"), 1) if j == BT - 1 else st.do(i)
            dve.wait_ge(sem("x_free"), b + 2)
            for j in range(BT):
                st.do(nc.vector.scalar_tensor_tensor(out=x1[:, j], in0=x1[:, j], scalar=nsc[:, 4, j:j + 1],
                                                     in1=g1b[:, 1], op0=ALU.mult, op1=ALU.add))
            st.sync()
            stats(dve, st, x1, EPS_IN)
            rsqrt(dve, st, nsc[:, 1], nsc[:, 2])
            for j in range(BT):
                st.do(nc.vector.scalar_tensor_tensor(out=x1[:, j], in0=x1[:, j], scalar=bna[:, j, 0:1],
                                                     in1=g1b[:, 2], op0=ALU.subtract, op1=ALU.mult))
            st.sync()
            dve.wait_ge(sem("m_done"), b + 1)
            for j in range(BT):
                nc.vector.scalar_tensor_tensor(out=xln[:, j], in0=x1[:, j], scalar=nsc[:, 2, j:j + 1],
                                               in1=g1b[:, 3], op0=ALU.mult, op1=ALU.add).then_inc(sem("xln_in"), 1)
            dve.wait_ge(sem("xln_in"), b * BT + BT)
            return st.k

        def dve_mix(dve, b):
            for c in range(C):
                dve.wait_ge(sem("xt_in"), b * C + c + 3)
                nc.vector.scalar_tensor_tensor(out=mx[:, c], in0=xlnT[:, c, 0:BLK], scalar=omtf[:, c:c + 1],
                                               in1=mx[:, c], op0=ALU.mult, op1=ALU.add).then_inc(sem("mix_in"), 1)
            dve.wait_ge(sem("mix_in"), b * C + C)
            nc.vector.tensor_scalar(xlnT[:, :, 0:1], xlnT[:, :, BLK:BLK + 1], 1.0, None,
                                    ALU.mult).then_inc(sem("xt_free"), 1)

        def stage1_vector(dve):
            nc.vector.memset(xlnT[:, :, 0:1], 0.0).then_inc(sem("carry0"), 1)
            dve.wait_ge(sem("par_in"), 16 * 7)
            dve.wait_ge(sem("cst"), 5)
            nc.vector.tensor_scalar(omtf[:], tf[:], -1.0, 1.0, ALU.mult, ALU.add).then_inc(sem("omtf"), 1)
            dve.wait_ge(sem("omtf"), 1)
            dve.wait_ge(sem("carry0"), 1)
            with dve.Fori(0, NB) as b:
                k = dve_norms1(dve, b)
                assert k == S1, (k, S1)
                dve_mix(dve, b)
            dve.wait_ge(sem("m_fin"), 1)
            dve.wait_ge(sem("wv_in"), 16)
            for c in range(C):
                nc.vector.tensor_tensor(pv[:, c], wv[:, c], bank[c][:], ALU.mult).then_inc(sem("pv_in"), 1)
            dve.wait_ge(sem("vm_in"), 1)
            nc.vector.tensor_copy(vm[:], bank[4][:, 0:C]).then_inc(sem("vmc"), 1)
            dve.wait_ge(sem("vmc"), 1)
            dve.wait_ge(sem("mixlo_in"), 4 + NB * C)
            for c in range(C):
                nc.vector.tensor_scalar(vmb[:, c], onesq[:], vm[:, c:c + 1], None, ALU.mult).then_inc(sem("vmb_in"), 1)
            dve.wait_ge(sem("srow_in"), 1)
            nc.vector.tensor_tensor(sbc[:], bank[5][:], bob[:], ALU.add).then_inc(sem("sbc_in"), 1)

        def stage1_scalar(act):
            act.wait_ge(sem("par_in"), 16 * 7)
            act.wait_ge(sem("ages_in"), 1)
            act.wait_ge(sem("raw_in"), 16)
            nc.scalar.activation(wr[0][:].rearrange("p c n -> p (c n)"), raw[:], ACT.Copy).then_inc(sem("whi"), 1)
            act.wait_ge(sem("carry0"), 1)
            with act.Fori(0, NB) as b:
                wait_apart(act, sem("m_done"), b + 1)
                for j in range(BT):
                    nc.scalar.activation(dec[:, j], tdb[:], ACT.Exp,
                                         scale=ages[:, bass.ds(b * BT + j, 1)]).then_inc(sem("dec_in"), 1)
                wait_apart(act, sem("raw_in"), 32 * b + 32)
                nc.scalar.activation(wck[0][:, bass.ds(b, 1)].rearrange("p a n -> p (a n)"), raw[:],
                                     ACT.Copy).then_inc(sem("whi"), 1)
                act.wait_ge(sem("xt_free"), b + 1)
                act.wait_ge(sem("mixlo_in"), b * C + 4)
                for c in range(C):
                    act.wait_ge(sem("tr_in"), b * C + c + 1)
                    nc.scalar.activation(xlnT[:, c, 1:BLK + 1], bank[4 + c % 2][:], ACT.Copy)
                    nc.scalar.activation(mx[:, c], bank[4 + c % 2][:], ACT.Copy,
                                         scale=tf[:, c:c + 1]).then_inc(sem("xt_in"), 1)
                for c in range(C):
                    act.wait_ge(sem("mix_in"), b * C + c + 1)
                    nc.scalar.activation(mixT[0][:, c], mx[:, c], ACT.Copy).then_inc(sem("mixhi_in"), 1)
                act.wait_ge(sem("raw_in"), 32 * b + 48)
                act.wait_ge(sem("wst"), 16 * b + 16)
                nc.scalar.activation(stage[:, :, 0], raw[:].rearrange("p (c n) -> p c n", c=C),
                                     ACT.Copy).then_inc(sem("whi"), 1)
                for j in range(BT):
                    act.wait_ge(sem("z_in"), b * BT + j + 1)
                    act.wait_ge(sem(f"zo_st{j % 2}"), 32 * b + 16 * (j // 2) + 16)
                    nc.scalar.activation(zo[:, j % 2], bank[6 + j % 2][:], ACT.Copy).then_inc(sem("z_free"), 1)
            act.wait_ge(sem("raw_in"), 32 * NB + 32)
            nc.scalar.activation(wcr[0][:].rearrange("p c n -> p (c n)"), raw[:], ACT.Copy).then_inc(sem("whi"), 1)

        def stage1_gpsimd(pool):
            nc.gpsimd.memset(ident[:], 0.0).then_inc(sem("cst"), 1)
            nc.gpsimd.memset(onesq[:], 1.0).then_inc(sem("cst"), 1)
            nc.gpsimd.memset(zrow[:], 0.0).then_inc(sem("cst"), 1)
            pool.wait_ge(sem("cst"), 3)
            nc.gpsimd.affine_select(out=ident[:], in_=ident[:], compare_op=ALU.not_equal, fill=1.0, base=0,
                                    pattern=[[-1, P]], channel_multiplier=1).then_inc(sem("cst"), 1)
            nc.gpsimd.affine_select(out=tri[:], in_=onesq[:], compare_op=ALU.is_gt, fill=0.0, base=0,
                                    pattern=[[1, P]], channel_multiplier=-1).then_inc(sem("cst"), 1)
            nc.gpsimd.iota(ages[:], [[-P, NT]], base=T - 1, channel_multiplier=-1,
                           allow_small_or_imprecise_dtypes=True).then_inc(sem("ages_in"), 1)
            pool.sem_inc(sem("mixlo_in"), 4)
            pool.wait_ge(sem("whi"), 1)
            nc.gpsimd.tensor_tensor(wr[1][:].rearrange("p c n -> p (c n)"), raw[:],
                                    wr[0][:].rearrange("p c n -> p (c n)"), ALU.subtract).then_inc(sem("wlo"), 1)
            with pool.Fori(0, NB) as b:
                wait_apart(pool, sem("whi"), 2 * b + 2)
                nc.gpsimd.tensor_tensor(wck[1][:, bass.ds(b, 1)].rearrange("p a n -> p (a n)"), raw[:],
                                        wck[0][:, bass.ds(b, 1)].rearrange("p a n -> p (a n)"),
                                        ALU.subtract).then_inc(sem("wlo"), 1)
                for c in range(C):
                    pool.wait_ge(sem("mixhi_in"), b * C + c + 1)
                    nc.gpsimd.tensor_tensor(mixT[1][:, c], mx[:, c], mixT[0][:, c],
                                            ALU.subtract).then_inc(sem("mixlo_in"), 1)
                pool.wait_ge(sem("whi"), 2 * b + 3)
                nc.gpsimd.tensor_tensor(stage[:, :, 1], raw[:].rearrange("p (c n) -> p c n", c=C),
                                        stage[:, :, 0], ALU.subtract).then_inc(sem("wlo"), 1)
            pool.wait_ge(sem("whi"), 2 * NB + 2)
            nc.gpsimd.tensor_tensor(wcr[1][:].rearrange("p c n -> p (c n)"), raw[:],
                                    wcr[0][:].rearrange("p c n -> p (c n)"), ALU.subtract).then_inc(sem("wlo"), 1)

        def stage1_tensor(pe):
            pe.sem_inc(sem("m_done"), 1)
            pe.wait_ge(sem("cst"), 5)
            for c in range(C):
                nc.tensor.matmul(bank[c][:], zrow[:, 0:P], zrow[:], start=True, stop=False)
            with pe.Fori(0, NB) as b:
                for c in range(C):
                    for j in range(BT):
                        if c == 0:
                            pe.wait_ge(sem("xln_in"), b * BT + j + 1)
                        if j == 0:
                            pe.wait_ge(sem("xt_in"), b * C + c + 1)
                        i = nc.tensor.transpose(bank[4 + c % 2][:, j * P:(j + 1) * P], xln[:, j, c * P:(c + 1) * P], ident[:])
                    i.then_inc(sem("tr_in"), 1)
                for j in range(BT):
                    pe.wait_ge(sem("dec_in"), b * BT + j + 1)
                    for c in range(C):
                        i = nc.tensor.matmul(bank[c][:], xln[:, j, c * P:(c + 1) * P], dec[:, j], start=False, stop=False)
                i.then_inc(sem("m_done"), 1)
                pe.wait_ge(sem("wlo"), 1)
                pe.wait_ge(sem("mixlo_in"), b * C + C + 4)
                for j in range(BT):
                    pe.wait_ge(sem("z_free"), b * BT + j + 1)
                    i = split_product(bank[6 + j % 2][:], lambda s, c: mixT[s][:, c, j * P:(j + 1) * P],
                                      lambda s, c: wr[s][:, c], C)
                    i.then_inc(sem("z_in"), 1)
            for c in range(C):
                i = nc.tensor.matmul(bank[c][:], zrow[:, 0:P], zrow[:], start=False, stop=True)
            i.then_inc(sem("m_fin"), 1)
            pe.wait_ge(sem("pv_in"), C)
            pe.wait_ge(sem("xt_in"), NB * C + 2)
            for h in range(C):
                for c in range(C):
                    i = nc.tensor.matmul(bank[4][:, h:h + 1], pv[:, c, h * P:(h + 1) * P], onesq[:, 0:1],
                                         start=c == 0, stop=c == C - 1)
            i.then_inc(sem("vm_in"), 1)
            pe.wait_ge(sem("vmb_in"), C)
            pe.wait_ge(sem("wo_in"), 16)
            for h in range(C):
                i = nc.tensor.matmul(bank[5][:], vmb[:, h], wo[:, h], start=h == 0, stop=h == C - 1)
            i.then_inc(sem("srow_in"), 1)

        def split_product(dst, lhs, rhs, n):
            parts = [(0, 0), (0, 1), (1, 0)]
            for c in range(n):
                for k, (l, r) in enumerate(parts):
                    i = nc.tensor.matmul(dst, lhs(l, c), rhs(r, c), start=c == 0 and k == 0,
                                         stop=c == n - 1 and k == 2)
            return i

        def vec(name):
            return a[name].partition_broadcast(P)

        x_rows = a["L0_attn_x"][0].rearrange("(b j p) d -> b p j d", j=BT, p=P)
        wck_rows = a["L0_attn_Wck"].rearrange("(c p) n -> c p n", p=P)
        wcv_rows = a["L0_attn_Wcv"].rearrange("(g c p) n -> g p c n", c=C, p=P)

        def square(name):
            return a[name].rearrange("(c p) n -> p c n", p=P)

        def stage1_sync(sp):
            sp.dma_start(xb[:], x_rows[0]).then_inc(sem("x_in"), 16)
            for n, v in enumerate(("ln1_g", "ln1_b", "tm_g", "tm_b")):
                sp.dma_start(g1b[:, n], vec(f"L0_attn_{v}")).then_inc(sem("par_in"), 16)
            sp.dma_start(tdb[:], vec("L0_attn_time_decay")).then_inc(sem("par_in"), 16)
            sp.dma_start(bob[:], vec("L0_attn_bo")).then_inc(sem("par_in"), 16)
            sp.dma_start(tf[:], a["L0_attn_time_first"].rearrange("(c p) -> p c", p=P),
                         allow_slow_non_contiguous=True).then_inc(sem("par_in"), 16)
            sp.dma_start(raw[:].rearrange("p (c n) -> p c n", c=C), square("L0_attn_Wr")).then_inc(sem("raw_in"), 16)
            for name, credit in (("x_free", 1), ("xt_free", 1), ("xt_in", 2), ("z_free", 2), ("zo_st0", 16),
                                 ("zo_st1", 16), ("wst", 16)):
                sp.sem_inc(sem(name), credit)
            with sp.Fori(0, NB - 1) as b:
                sync_block1(sp, b)
            sync_block1(sp, NB - 1)
            sp.dma_start(raw[:].rearrange("p (c n) -> p c n", c=C), square("L0_attn_Wcr")).then_inc(sem("raw_in"), 16)
            sp.wait_ge(sem("x_free"), NB + 1)
            sp.dma_start(wv[:], square("L0_attn_Wv")).then_inc(sem("wv_in"), 16)
            sp.wait_ge(sem("m_fin"), 1)
            sp.dma_start(wo[:], square("L0_attn_Wo")).then_inc(sem("wo_in"), 16)

        def sync_block1(sp, b):
            wait_apart(sp, sem("wlo"), 2 * b + 1)
            sp.dma_start(raw[:], wck_rows[bass.ds(b, 1)].rearrange("a p n -> p (a n)")).then_inc(sem("raw_in"), 16)
            if not isinstance(b, int):
                wait_apart(sp, sem("x_free"), b + 2)
                sp.dma_start(xb[:], x_rows[bass.ds(b + 1, 1)].rearrange("a p j d -> p (a j) d")).then_inc(sem("x_in"), 16)
            wait_apart(sp, sem("wlo"), 2 * b + 2)
            sp.dma_start(raw[:].rearrange("p (c n) -> p c n", c=C),
                         wcv_rows[bass.ds(b, 1)].rearrange("a p c n -> p (a c) n")).then_inc(sem("raw_in"), 16)
            wait_apart(sp, sem("wlo"), 2 * b + 3)
            sp.dma_start(wcv_d[bass.ds(b * C, C)].rearrange("c p m -> p c m"),
                         stage[:].bitcast(F).rearrange("p c s n -> p c (s n)")).then_inc(sem("wst"), 16)
            for j in range(BT):
                wait_apart(sp, sem("z_free"), b * BT + j + 3)
                sp.dma_start(z_d[bass.ds((b * BT + j) * P, P)], zo[:, j % 2]).then_inc(sem(f"zo_st{j % 2}"), 16)

        TH_AT = 3
        FRONT, TAIL = 4 * BT + 2 * (STATS_STEPS + RSQRT_STEPS) + 3 * BT, STATS_STEPS + RSQRT_STEPS

        def wait_pos(engine, s, value):
            if not isinstance(value, int) or value > 0:
                engine.wait_ge(s, value)

        def dve_front(dve, b):
            st = Steps(dve, sem("front_dve"), b * FRONT)
            xx = lambda j: f1[:, bass.ds(b & 1, 1), j].rearrange("p a d -> p (a d)")
            wait_apart(dve, sem("x2_in"), 16 * b + 16)
            if not isinstance(b, int):
                wait_apart(dve, sem("ht_st"), 16 * C * (b - 1) + 16)
                wait_apart(dve, sem("lg_in"), b - 1)
            for j in range(BT):
                st.do(nc.vector.tensor_scalar(tmp[:, j], xx(j), mean0[:, bass.ds(b * BT + j, 1)],
                                              rstd0[:, bass.ds(b * BT + j, 1)], ALU.subtract, ALU.mult))
            for j in range(BT):
                dve.wait_ge(sem("zs_in"), b * BT + j + 1)
                st.do(nc.vector.tensor_tensor(f2[:, j], f2[:, j], sbc[:], ALU.mult))
            st.sync()
            for j in range(BT):
                st.do(nc.vector.tensor_tensor(f2[:, j], f2[:, j], tmp[:, j], ALU.add))
            st.sync()
            for j in range(BT):
                st.do(nc.vector.tensor_tensor(xx(j), xx(j), f2[:, j], ALU.add))
            for n in (0, 2):
                stats(dve, st, f2, EPS_IN)
                rsqrt(dve, st, nsc[:, 1], nsc[:, 2])
                for j in range(BT):
                    st.do(nc.vector.scalar_tensor_tensor(out=f2[:, j], in0=f2[:, j], scalar=bna[:, j, 0:1],
                                                         in1=g2b[:, n], op0=ALU.subtract, op1=ALU.mult))
                st.sync()
                for j in range(BT):
                    i = nc.vector.scalar_tensor_tensor(out=f2[:, j], in0=f2[:, j], scalar=nsc[:, 2, j:j + 1],
                                                       in1=g2b[:, n + 1], op0=ALU.mult, op1=ALU.add)
                    st.do(i) if n == 0 else i.then_inc(sem("xc_in"), 1)
                if n == 0:
                    st.sync()
            dve.wait_ge(sem("xc_in"), b * BT + BT)
            assert st.k == FRONT, (st.k, FRONT)

        def dve_lo_xc(dve, b):
            for c in range(C):
                dve.wait_ge(sem("hiT_in"), b * C + c + 1)
                nc.vector.tensor_tensor(xcT[1][:, c, 1:BLK + 1], bank[6 + c % 2][:], xcT[0][:, c, 1:BLK + 1],
                                        ALU.subtract).then_inc(sem("loT_in"), 1)

        def dve_tail_a(dve, b):
            dve.wait_ge(sem("vc_done"), 2 + NCI * (b + 1))
            dve.wait_ge(sem("h_st"), 16 * b + 16)
            for j in range(BT):
                nc.vector.tensor_tensor(hb[:, j], rc[:, j], bank[j][:], ALU.mult).then_inc(sem("u_in"), 1)

        def dve_tail_b(dve, b):
            st = Steps(dve, sem("tail_dve"), b * TAIL)
            xx = lambda j: f1[:, bass.ds(b & 1, 1), j].rearrange("p a d -> p (a d)")
            dve.wait_ge(sem("u_in"), 4 + b * BT + BT)
            for j in range(BT):
                nc.vector.tensor_tensor(xx(j), xx(j), hb[:, j], ALU.add).then_inc(sem("xp_in"), 1)
            wait_apart(dve, sem("xp_in"), b * BT + BT)
            stats(dve, st, f1[:, bass.ds(b & 1, 1)].rearrange("p a j d -> p (a j) d"), EPS_OUT)
            rsqrt(dve, st, nsc[:, 1], nsc[:, 2])
            for j in range(BT):
                nc.vector.tensor_scalar(hb[:, j], xx(j), bna[:, j, 0:1], nsc[:, 2, j:j + 1],
                                        ALU.subtract, ALU.mult).then_inc(sem("h_in"), 1)
            dve.wait_ge(sem("h_in"), b * BT + BT)
            assert st.k == TAIL, (st.k, TAIL)

        def dve_lo_h(dve, b):
            for c in range(C):
                dve.wait_ge(sem("hiTH_in"), b * C + c + 1)
                nc.vector.tensor_tensor(hT[c][:, 1], bank[6 + c % 2][:], hT[c][:, 0],
                                        ALU.subtract).then_inc(sem("loTH_in"), 1)

        def stage2_vector(dve):
            for s in range(2):
                nc.vector.memset(xcT[s][:, :, 0:1].bitcast(F), 0.0).then_inc(sem("carry2"), 1)
            dve.wait_ge(sem("par2_in"), 16 * 5)
            dve.wait_ge(sem("gwhi"), 1)
            nc.vector.tensor_tensor(gw[1][:], gwf[:], gw[0][:], ALU.subtract).then_inc(sem("gwlo"), 1)
            dve_front(dve, 0)
            dve_lo_xc(dve, 0)
            dve_front(dve, 1)
            with dve.Fori(1, NB - 1) as b:
                dve_tail_a(dve, b - 1)
                dve_lo_xc(dve, b)
                dve_tail_b(dve, b - 1)
                dve_lo_h(dve, b - 1)
                dve_front(dve, b + 1)
            dve_tail_a(dve, NB - 2)
            dve_lo_xc(dve, NB - 1)
            dve_tail_b(dve, NB - 2)
            dve_lo_h(dve, NB - 2)
            lo3(dve, nc.vector, *ORDER3[:3])
            dve_tail_a(dve, NB - 1)
            lo3(dve, nc.vector, ORDER3[3])
            dve_tail_b(dve, NB - 1)
            dve_lo_h(dve, NB - 1)

        def act_receptance(act, b):
            act.wait_ge(sem("zl_in"), 16 * b + 16)
            for j in range(BT):
                nc.scalar.activation(f2[:, j], f2[:, j], ACT.Sigmoid).then_inc(sem("zs_in"), 1)

        def act_hi_xc(act, b, first=False):
            act.wait_ge(sem("trT_in"), b * C + 1)
            if first:
                act.wait_ge(sem("carry2"), 2)
            else:
                for s in range(2):
                    nc.scalar.activation(xcT[s][:, :, 0:1], xcT[s][:, :, BLK:BLK + 1], ACT.Copy).then_inc(sem("carry2"), 1)
                act.wait_ge(sem("carry2"), 2 + 2 * b)
            for c in range(C):
                act.wait_ge(sem("trT_in"), b * C + c + 1)
                nc.scalar.activation(xcT[0][:, c, 1:BLK + 1], bank[6 + c % 2][:], ACT.Copy).then_inc(sem("hiT_in"), 1)

        def act_rc(act, b):
            act.wait_ge(sem("u_in"), b * BT + 4)
            for j in range(BT):
                act.wait_ge(sem("rcp_in"), b * BT + j + 1)
                nc.scalar.activation(rc[:, j], bank[6 + j % 2][:], ACT.Sigmoid).then_inc(sem("rc_in"), 1)

        def act_inner(act, n, i):
            act.wait_ge(sem("kc_in"), n + 1)
            act.wait_ge(sem("klo_in"), n + 1)
            nc.scalar.activation(ra[:, i % 2], bank[4 + i % 2][:], ACT.Relu).then_inc(sem("kc_free"), 1)
            act.wait_ge(sem("kc_free"), n + 3)
            nc.scalar.activation(ra[:, i % 2], ra[:, i % 2], ACT.Square).then_inc(sem("sq"), 1)
            act.wait_ge(sem("sq"), n + 1)
            act.wait_ge(sem("vc_done"), n + 1)
            nc.scalar.activation(ksp[0][:, i % 2], ra[:, i % 2], ACT.Copy).then_inc(sem("khi_in"), 1)

        def act_router(act, b, i):
            if i == TH_AT:
                act_hi_h(act, b)
            if i == TH_AT + 1:
                act.wait_ge(sem("lg_in"), b + 1)
                nc.scalar.activation(sgT[:], bank[5][0:E], ACT.Sigmoid).then_inc(sem("sg_in"), 1)
            if i == TH_AT + 2:
                wait_apart(act, sem("tsc_in"), b + 1)
                nc.scalar.activation(scores[:, bass.ds(b * BT, BT)].rearrange("p j e -> p (j e)"), bank[6][:, 0:BT * E],
                                     ACT.Copy).then_inc(sem("sc_in"), 1)

        def act_hi_h(act, b):
            for c in range(C):
                act.wait_ge(sem("trH_in"), b * C + c + 1)
                act.wait_ge(sem("ht_st"), 16 * C * b + 16)
                nc.scalar.activation(hT[c][:, 0], bank[6 + c % 2][:], ACT.Copy).then_inc(sem("hiTH_in"), 1)

        def act_block2(act, b, first=False, last=False):
            act_hi_xc(act, b, first)
            act_rc(act, b)
            for i in range(NCI):
                act_inner(act, b * NCI + i, i)
                if i == 1 and not last:
                    act_receptance(act, b + 1)
                if not first:
                    act_router(act, b - 1, i)

        def stage2_scalar(act):
            act.wait_ge(sem("par2_in"), 16 * 5)
            nc.scalar.activation(gw[0][:], gwf[:], ACT.Copy).then_inc(sem("gwhi"), 1)
            act_receptance(act, 0)
            act_block2(act, 0, first=True)
            with act.Fori(1, NB - 1) as b:
                act_block2(act, b)
            act_block2(act, NB - 1, last=True)

        def pool_inner(pool, n, i):
            pool.wait_ge(sem("khi_in"), n + 1)
            nc.gpsimd.tensor_tensor(ksp[1][:, i % 2], ra[:, i % 2], ksp[0][:, i % 2],
                                    ALU.subtract).then_inc(sem("klo_in"), 1)

        def stage2_gpsimd(pool):
            with pool.Fori(0, NB) as b:
                for i in range(NCI):
                    pool_inner(pool, b * NCI + i, i)

        def pe_inner_up(pe, n, i, weights, rhs):
            pe.wait_ge(sem("kc_free"), n + 1)
            split_product(bank[4 + i % 2][:], lambda s, c: weights[s][:, c, i * P:(i + 1) * P],
                          rhs, C).then_inc(sem("kc_in"), 1)

        def pe_inner_down(pe, n, i, last, rhs):
            pe.wait_ge(sem("klo_in"), n + 3)
            for j in range(BT):
                for k, (l, r) in enumerate(((0, 0), (0, 1), (1, 0))):
                    m = nc.tensor.matmul(bank[j][:], ksp[l][:, i % 2, j * P:(j + 1) * P], rhs(r),
                                         start=i == 0 and k == 0, stop=i == last and k == 2)
            m.then_inc(sem("vc_done"), 1)

        def pe_logits(pe, b, c):
            pe.wait_ge(sem("loTH_in"), 8 + b * C + c + 1)
            for k, (l, r) in enumerate(((0, 0), (0, 1), (1, 0))):
                m = nc.tensor.matmul(bank[5][0:E], gw[l][:, c], hT[c][:, r], start=c == 0 and k == 0,
                                     stop=c == C - 1 and k == 2)
            if c == C - 1:
                m.then_inc(sem("lg_in"), 1)

        def pe_turn_norm(pe, b, c):
            if c >= 2:
                pe.wait_ge(sem("loTH_in"), 8 + b * C + c - 1)
            for j in range(BT):
                m = nc.tensor.transpose(bank[6 + c % 2][:, j * P:(j + 1) * P], hb[:, j, c * P:(c + 1) * P], ident[:])
            m.then_inc(sem("trH_in"), 1)

        def pe_inner(pe, b, i, n, up, down, router, rc_done=None):
            if router and i == TH_AT + 2:
                pe.wait_ge(sem("sg_in"), b + 1)
            up(i)
            if router and i == TH_AT:
                pe.wait_ge(sem("h_in"), b * BT + BT)
                pe.wait_ge(sem("rc_in"), rc_done)
                pe_turn_norm(pe, b, 0)
                pe_turn_norm(pe, b, 1)
            if router and i == TH_AT + 1:
                pe_logits(pe, b, 2)
                pe_logits(pe, b, 3)
            if i >= 2:
                down(i - 2)
            if router and i == TH_AT:
                pe.wait_ge(sem("kc_free"), n + 3)
                pe_logits(pe, b, 0)
                pe_turn_norm(pe, b, 2)
                pe_logits(pe, b, 1)
                pe_turn_norm(pe, b, 3)
            if router and i == TH_AT + 2:
                pe_scores(pe, b)

        def pe_scores(pe, b):
            wait_apart(pe, sem("sg_in"), b + 1)
            for j in range(BT):
                m = nc.tensor.transpose(bank[6][:, j * E:(j + 1) * E], sgT[:, j * P:(j + 1) * P], ident[0:E, 0:E])
            m.then_inc(sem("tsc_in"), 1)

        def pe_block2(pe, b, first=False):
            pe.wait_ge(sem("xc_in"), b * BT + BT)
            pe.wait_ge(sem("loTH_in"), 4 + b * C)
            for c in range(C):
                if c >= 2:
                    pe.wait_ge(sem("loT_in"), b * C + c - 1)
                for j in range(BT):
                    m = nc.tensor.transpose(bank[6 + c % 2][:, j * P:(j + 1) * P], f2[:, j, c * P:(c + 1) * P], ident[:])
                m.then_inc(sem("trT_in"), 1)
            pe.wait_ge(sem("loT_in"), b * C + C)
            for j in range(BT):
                if j >= 2:
                    pe.wait_ge(sem("rc_in"), b * BT + j - 1)
                split_product(bank[6 + j % 2][:], lambda s, c: xcT[s][:, c, 1 + j * P:1 + (j + 1) * P],
                              lambda s, c: wcr[s][:, c], C).then_inc(sem("rcp_in"), 1)

            def down(i):
                if i == 0:
                    pe.wait_ge(sem("u_in"), b * BT + 4)
                pe.wait_ge(sem(f"vr_in{i % 4}"), 64 * b + 16 * (i // 4) + 16)
                pe_inner_down(pe, b * NCI + i, i, NCI - 1, lambda s: vring[:, i % 4, s * H:(s + 1) * H])

            def up(i):
                pe_inner_up(pe, b * NCI + i, i, wck, lambda s, c: xcT[s][:, c, 0:BLK])

            for i in range(NCI):
                pe_inner(pe, b - 1, i, b * NCI + i, up, down, not first, b * BT + BT)
            down(NCI - 2)
            down(NCI - 1)

        def stage2_tensor(pe):
            pe.wait_ge(sem("wlo"), 2 * NB + 2)
            pe.wait_ge(sem("gwlo"), 1)
            pe_block2(pe, 0, first=True)
            with pe.Fori(1, NB) as b:
                pe_block2(pe, b)

        hT_rows = hT_d.rearrange("b p s c t -> b c p s t")

        def sp_tail2(sp, b):
            wait_apart(sp, sem("xp_in"), b * BT + BT)
            sp.dma_start(xp_rows[bass.ds(b, 1)].rearrange("a p j d -> p (a j) d"),
                         f1[:, bass.ds(b & 1, 1)].rearrange("p a j d -> p (a j) d")).then_inc(sem("xp_st"), 16)
            wait_apart(sp, sem("h_in"), b * BT + BT)
            sp.dma_start(h_rows[bass.ds(b, 1)].rearrange("a p j d -> p (a j) d"), hb[:]).then_inc(sem("h_st"), 16)

        def sp_hT(sp, b):
            for c in range(C):
                wait_apart(sp, sem("loTH_in"), 8 + b * C + c + 1)
                sp.dma_start(hT_rows[bass.ds(b, 1), c].rearrange("a p s t -> p (a s) t"),
                             hT[c][:].bitcast(F)).then_inc(sem("ht_st"), 16)

        def sp_block2(sp, b, first=False, last=False):
            def ring(i):
                n = b * NCI + i
                if not (first and i < 4):
                    wait_apart(sp, sem("vc_done"), n - 1)
                sp.dma_start(vring[:, i % 4].bitcast(F), wcv_d[i]).then_inc(sem(f"vr_in{i % 4}"), 16)
                sp.dma_start(y_spare[bass.ds(n, 1)].rearrange("a p (s n) -> (a p) s n", s=2),
                             zrow[:].bitcast(F).unsqueeze(1).to_broadcast([P, 2, H // 2])).then_inc(sem("y_fill"), 16)
            if not last:
                wait_apart(sp, sem("trT_in"), b * C + C)
                sp.dma_start(f2[:], z_rows[bass.ds(b + 1, 1)].rearrange("a p j d -> p (a j) d")).then_inc(sem("zl_in"), 16)
            for i in range(4):
                ring(i)
            if not first:
                sp_tail2(sp, b - 1)
                if not last:
                    wait_apart(sp, sem("xp_st"), 16 * b)
                    sp.dma_start(f1[:, bass.ds((b + 1) & 1, 1)].rearrange("p a j d -> p (a j) d"),
                                 x_rows[bass.ds(b + 1, 1)].rearrange("a p j d -> p (a j) d")).then_inc(sem("x2_in"), 16)
            ring(4)
            if not first:
                sp_hT(sp, b - 1)
            for i in range(5, NCI):
                ring(i)

        def stage2_sync(sp):
            for name, credit in (("u_in", 4), ("h_st", 16), ("kc_free", 2), ("klo_in", 2), ("vc_done", 2),
                                 ("loTH_in", 8), ("ht_st", 16),
                                 ("bs_st", 16), ("xt4", 2), ("u4", 2), ("r4", 2), ("at4", 2), ("al4", 2),
                                 ("d4", 2), ("y4", 2), ("y_st0", 16), ("y_st1", 16)):
                sp.sem_inc(sem(name), credit)
            sp.wait_ge(sem("sbc_in"), 1)
            sp.wait_ge(sem("wst"), 16 * NB + 16)
            sp.wait_ge(sem("wlo"), 2 * NB + 2)
            for n, v in enumerate(("ln2_g", "ln2_b", "cm_g", "cm_b")):
                sp.dma_start(g2b[:, n], vec(f"L0_attn_{v}")).then_inc(sem("par2_in"), 16)
            sp.dma_start(gwf[:], square("L0_ffn_gate_w")).then_inc(sem("par2_in"), 16)
            sp.wait_ge(sem("zo_st0"), 32 * NB + 16)
            sp.wait_ge(sem("zo_st1"), 32 * NB + 16)
            sp.dma_start(f2[:], z_rows[0]).then_inc(sem("zl_in"), 16)
            sp.dma_start(f1[:, 0], x_rows[0]).then_inc(sem("x2_in"), 16)
            sp.wait_ge(sem("x2_in"), 16)
            sp.dma_start(f1[:, 1], x_rows[1]).then_inc(sem("x2_in"), 16)
            sp_block2(sp, 0, first=True)
            with sp.Fori(1, NB - 1) as b:
                sp_block2(sp, b)
            sp_block2(sp, NB - 1, last=True)

        N3 = NB * NCI

        BETWEEN_AT = 2

        def pe_block3(pe, b, router=False, between=None):
            pe.wait_ge(sem("hb_in"), 16 * b + 16)

            def down(i):
                if i == 0:
                    if b == 0:
                        pe.wait_ge(sem("u_in"), NB * BT + 4)
                    else:
                        pe.wait_ge(sem("sh_in"), b * BT)
                pe.wait_ge(sem(f"wsd_lo{i // 4}"), i % 4 // 2 + 1)
                pe_inner_down(pe, N3 + b * NSI + i, i, NSI - 1, lambda s: wsd[s][:, i])

            rhs = lambda s, c: hTb[:, bass.ds(b & 1, 1), s, c].rearrange("p a t -> p (a t)")

            def up(i):
                pe.wait_ge(sem(f"wsu_lo{i // 4}"), i % 4 // 2 + 1)
                pe_inner_up(pe, N3 + b * NSI + i, i, wsu, rhs)

            for i in range(NSI):
                pe_inner(pe, NB - 1, i, N3 + b * NSI + i, up, down, router, NB * BT)
                if i == BETWEEN_AT and between:
                    between(pe)
            down(NSI - 2)
            down(NSI - 1)

        def pe_counts(pe):
            pe.wait_ge(sem("sel_in"), 1)
            sel = big[3][:].rearrange("p n e -> p (n e)")
            nc.tensor.matmul(bank[6][:], tri[:], sel, start=True, stop=True)
            nc.tensor.matmul(bank[7][:], onesq[:], sel, start=True, stop=True).then_inc(sem("cnt_in"), 1)

        def pe_ids(pe, choices):
            for k in choices:
                pe.wait_ge(sem("hot_in"), k + 1)
                for n in range(NT):
                    m = nc.tensor.matmul(bank[6][:, 0:SLOT_TILES], hot_p[:, k % 2, n], hot_q[:, k % 2, n],
                                         start=k == 0 and n == 0, stop=k == TOPK - 1 and n == NT - 1)
                m.then_inc(sem("ids_mm"), 1)

        def stage3_tensor(pe):
            pe_block3(pe, 0, router=True)
            pe_block3(pe, 1, between=pe_counts)
            pe_block3(pe, 2, between=lambda pe: pe_ids(pe, (0, 1)))
            pe_block3(pe, 3, between=lambda pe: pe_ids(pe, (2, 3)))

        ORDER3 = (("u", 0), ("u", 1), ("d", 0), ("d", 1), ("u", 2), ("d", 2), ("u", 3), ("d", 3))

        def part3(m, which, k):
            if which == "u":
                return wsu[m][:, :, 2 * k * P:2 * (k + 1) * P], raw3[k % 2][:, 0].rearrange("p (c n) -> p c n", c=C)
            return wsd[m][:, 2 * k:2 * k + 2], raw3[k % 2][:, 1].rearrange("p (c n) -> p c n", c=2)

        def act_hi3(act, *parts):
            for which, k in parts:
                act.wait_ge(sem(f"raw3_in{k % 2}"), 32 * (k // 2) + 32)
                act.wait_ge(sem("kc_in"), N3)
                dst, src = part3(0, which, k)
                nc.scalar.activation(dst, src, ACT.Copy).then_inc(sem("w3hi"), 1)

        def lo3(engine, ops, *parts):
            for which, k in parts:
                engine.wait_ge(sem("w3hi"), ORDER3.index((which, k)) + 1)
                hi, src = part3(0, which, k)
                ops.tensor_tensor(part3(1, which, k)[0], src, hi, ALU.subtract).then_inc(sem(f"ws{which}_lo{k // 2}"), 1)

        def act_block3(act, b, router=False):
            for i in range(NSI):
                act_inner(act, N3 + b * NSI + i, i)
                if router and i < 3:
                    act_hi3(act, *((("u", 2),), (("d", 2), ("u", 3)), (("d", 3),))[i])
                if i == 3 and router:
                    act.wait_ge(sem("xp_st"), 16 * NB)
                if router:
                    act_router(act, NB - 1, i)
            act.wait_ge(sem("vc_done"), 2 + N3 + (b + 1) * NSI)
            act.wait_ge(sem("bs_st"), 16 * b + 16)
            for j in range(BT):
                nc.scalar.activation(so[:, j], bank[j][:], ACT.Copy).then_inc(sem("sh_in"), 1)

        def stage3_scalar(act):
            act_hi3(act, *ORDER3[:4])
            act_block3(act, 0, router=True)
            with act.Fori(1, NB) as b:
                act_block3(act, b)

        def pool_numbers(pool):
            pool.wait_ge(sem("sc_in"), NB)
            nc.gpsimd.iota(iota_p[:], [[1, P]], base=0, channel_multiplier=0, allow_small_or_imprecise_dtypes=True)
            nc.gpsimd.iota(iota_q[:], [[1, SLOT_TILES]], base=0, channel_multiplier=0, allow_small_or_imprecise_dtypes=True)
            nc.gpsimd.iota(token[:], [[P, NT]], base=0, channel_multiplier=1, allow_small_or_imprecise_dtypes=True)
            nc.gpsimd.iota(four[:], [[TOPK, NT]], base=0, channel_multiplier=0, allow_small_or_imprecise_dtypes=True)
            nc.gpsimd.memset(before[:], 1.0).then_inc(sem("num_in"), 1)
            pool.wait_ge(sem("num_in"), 1)
            nc.gpsimd.affine_select(out=before[:], in_=before[:], compare_op=ALU.is_gt, fill=0.0, base=0,
                                    pattern=[[1, GROUPS], [-1, GROUPS]], channel_multiplier=0).then_inc(sem("num_in"), 1)

        def pool_block3(pool, b, first=False, last=False):
            for i in range(NSI):
                pool_inner(pool, N3 + b * NSI + i, i)
                if first and i < 4:
                    lo3(pool, nc.gpsimd, ORDER3[4 + i])
                if first and i == TH_AT + 2:
                    pool_numbers(pool)
            if last:
                first_gathers(pool)
            wait_apart(pool, sem("xps_in"), 16 * b + 16)
            for j in range(BT):
                pool.wait_ge(sem("sh_in"), b * BT + j + 1)
                nc.gpsimd.tensor_tensor(so[:, j], so[:, j], xps[:, j], ALU.add).then_inc(sem("bs_in"), 1)

        def stage3_gpsimd(pool):
            pool_block3(pool, 0, first=True)
            with pool.Fori(1, NB - 1) as b:
                pool_block3(pool, b)
            pool_block3(pool, NB - 1, last=True)

        def sp_raw3(sp, k):
            if k >= 2:
                sp.wait_ge(sem("wsu_lo0"), k - 1)
                sp.wait_ge(sem("wsd_lo0"), k - 1)
            sp.dma_start(raw3[k % 2][:, 0].rearrange("p (c n) -> p c n", c=C),
                         square("L0_ffn_Wsu")[:, :, 2 * k * P:2 * (k + 1) * P]).then_inc(sem(f"raw3_in{k % 2}"), 16)
            sp.dma_start(raw3[k % 2][:, 1].rearrange("p (c n) -> p c n", c=2),
                         square("L0_ffn_Wsd")[:, 2 * k:2 * k + 2]).then_inc(sem(f"raw3_in{k % 2}"), 16)

        def sp_hTb(sp, b):
            sp.dma_start(hTb[:, b % 2].bitcast(F), hT_d[b]).then_inc(sem("hb_in"), 16)

        wu_rows = a["L0_ffn_Wu"].rearrange("e (c p) i -> e p c i", p=P)
        wd_rows = a["L0_ffn_Wd"].rearrange("e (c p) i -> e p c i", p=P)

        def load(sp, e, s):
            sp.dma_start(wu4[:, s].rearrange("p (c n) -> p c n", c=C),
                         wu_rows[bass.ds(e, 1)].rearrange("a p c i -> p (a c) i")).then_inc(sem(f"w4_in{s}"), 16)
            sp.dma_start(wd4[:, s].rearrange("p (c n) -> p c n", n=H),
                         wd_rows[bass.ds(e, 1)].rearrange("a p c i -> p (a c) i")).then_inc(sem(f"w4_in{s}"), 16)

        def landed(sp, r, s):
            wait_apart(sp, sem(f"w4_in{s}"), 32 * r + 32)
            sp.sem_inc(sem("win"), 1)

        def first_experts(sp):
            sp.wait_ge(sem("wsu_lo1"), 2)
            sp.wait_ge(sem("wsd_lo1"), 2)
            sp.wait_ge(sem("lg_in"), NB)
            for s in range(4):
                load(sp, s, s)

        def stage3_sync(sp):
            sp.wait_ge(sem("trT_in"), NB * C)
            sp_raw3(sp, 0)
            sp_raw3(sp, 1)
            sp.wait_ge(sem("ht_st"), 16 * C + 16)
            sp.wait_ge(sem("rcp_in"), NB * BT)
            sp_hTb(sp, 0)
            sp.wait_ge(sem("xp_st"), 16 * (NB - 1))
            sp.dma_start(xps[:], xp_rows[0]).then_inc(sem("xps_in"), 16)
            sp_raw3(sp, 2)
            sp_raw3(sp, 3)
            sp.wait_ge(sem("hb_in"), 16)
            sp.wait_ge(sem("vc_done"), 2 + N3)
            sp_hTb(sp, 1)
            sp_tail2(sp, NB - 1)
            sp_hT(sp, NB - 1)
            sp.wait_ge(sem("sc_in"), NB)
            sp.dma_start(ebias[:], a["L0_ffn_e_bias"].partition_broadcast(P)).then_inc(sem("eb_in"), 16)
            for b in range(NB):
                if b + 2 < NB:
                    sp.wait_ge(sem("kc_in"), N3 + (b + 1) * NSI)
                    sp.wait_ge(sem("hb_in"), 16 * (b + 2))
                    if b + 2 == NB - 1:
                        sp.wait_ge(sem("ht_st"), 16 * C * NB + 16)
                    sp_hTb(sp, b + 2)
                if b == 1:
                    first_experts(sp)
                sp.wait_ge(sem("bs_in"), (b + 1) * BT)
                sp.dma_start(base_rows[b], so[:]).then_inc(sem("bs_st"), 16)
                if b + 1 < NB:
                    if b + 1 == NB - 1:
                        sp.wait_ge(sem("xp_st"), 16 * NB)
                    sp.dma_start(xps[:], xp_rows[b + 1]).then_inc(sem("xps_in"), 16)

        def routing_vector(dve):
            st = Steps(dve, sem("route"))
            v = nc.vector

            def run(instruction):
                st.do(instruction)
                st.sync()
            tt = lambda o, x, y, op: run(v.tensor_tensor(o, x, y, op))
            dve.wait_ge(sem("eb_in"), 16)
            dve.wait_ge(sem("num_in"), 2)
            sfc, wa, wb, sel, wc, wd = (m[:] for m in big)
            sc = scores[:]
            per_tile = lambda m: m.unsqueeze(2).to_broadcast([P, NT, E])
            tt(sfc, sc, ebias[:].unsqueeze(1).to_broadcast([P, NT, E]), ALU.add)
            g8 = sfc.rearrange("p n (g k) -> p (n g) k", k=8)
            hi, lo = (m.rearrange("p n e -> p (n e)")[:, 0:256].rearrange("p (g k) -> p g k", k=4) for m in (wa, wb))
            t, u = (m.rearrange("p n e -> p (n e)")[:, 256:384].rearrange("p (g k) -> p g k", k=2) for m in (wa, wb))
            tt(hi, g8[:, :, 0:4], g8[:, :, 4:8], ALU.max)
            tt(lo, g8[:, :, 0:4], g8[:, :, 4:8], ALU.min)
            for w in (2, 1):
                a0, a1, b0, b1 = hi[:, :, 0:w], hi[:, :, w:2 * w], lo[:, :, 0:w], lo[:, :, w:2 * w]
                tt(t[:, :, 0:w], a0, a1, ALU.min)
                tt(u[:, :, 0:w], b0, b1, ALU.max)
                tt(a0, a0, a1, ALU.max)
                tt(b0, t[:, :, 0:w], u[:, :, 0:w], ALU.max)
            gs = small[:, 0].rearrange("p (n g) -> p n g", g=GROUPS)
            tt(gs, hi[:, :, 0].rearrange("p (n g) -> p n g", g=GROUPS), lo[:, :, 0].rearrange("p (n g) -> p n g", g=GROUPS), ALU.add)
            shape4 = [P, NT, GROUPS, GROUPS]
            other, own = gs.unsqueeze(2).to_broadcast(shape4), gs.unsqueeze(3).to_broadcast(shape4)
            gt4, eq4 = (m.rearrange("p n e -> p (n e)")[:, 0:256].rearrange("p (n g j) -> p n g j", g=GROUPS, j=GROUPS)
                        for m in (wc, wd))
            tt(gt4, other, own, ALU.is_gt)
            tt(eq4, other, own, ALU.is_equal)
            tt(eq4, eq4, before[:].unsqueeze(1).to_broadcast(shape4), ALU.mult)
            tt(gt4, gt4, eq4, ALU.add)
            gm = small[:, 1].rearrange("p (n g) -> p n g", g=GROUPS)
            run(v.tensor_reduce(gm, gt4, AX, ALU.add))
            run(v.tensor_scalar(gm, gm, 1.5, None, ALU.is_lt))
            tt(g8, g8, small[:, 1].unsqueeze(2).to_broadcast([P, NT * GROUPS, 8]), ALU.mult)
            for n in range(NT):
                st.do(v.max(top8[:, n], sfc[:, n]))
            st.sync()
            fourth = per_tile(top8[:, :, TOPK - 1])
            tt(wa, sfc, fourth, ALU.is_gt)
            tt(wb, sfc, fourth, ALU.is_equal)
            flat = lambda m: m.rearrange("p n e -> p (n e)")
            ones_row = onesq[:, 0:1].to_broadcast([P, NT * E])
            run(v.tensor_tensor_scan(flat(wc), ones_row, flat(wb), 0.0, ALU.mult, ALU.add))
            room = small[:, 2, 0:NT]
            st.do(v.memset(small[:, 3, 0:1], 0.0))
            run(v.tensor_copy(small[:, 3, 1:NT], wc[:, 0:NT - 1, E - 1]))
            run(v.tensor_reduce(room, wa, AX, ALU.add))
            tt(room, small[:, 3, 0:NT], room, ALU.subtract)
            run(v.tensor_scalar(room, room, float(TOPK), None, ALU.add))
            tt(wc, wc, per_tile(room), ALU.is_le)
            tt(wb, wb, wc, ALU.mult)
            st.do(v.tensor_tensor(sel, wa, wb, ALU.add))
            st.sync()
            v.tensor_scalar(small[:, 4, 0:1], small[:, 3, 0:1], 1.0, None, ALU.mult).then_inc(sem("sel_in"), 1)
            tt(wa, sc, sel, ALU.mult)
            den = small[:, 5, 0:NT]
            run(v.tensor_reduce(den, wa, AX, ALU.add))
            run(v.tensor_scalar(den, den, 1e-20, None, ALU.add))
            run(v.reciprocal(den, den))
            tt(wa, wa, per_tile(den), ALU.mult)
            run(v.tensor_scalar(wa, wa, ROUTE_SCALE, None, ALU.mult))
            run(v.tensor_tensor_scan(flat(wb), ones_row, flat(sel), 0.0, ALU.mult, ALU.add))
            tt(wb, wb, per_tile(four[:]), ALU.subtract)
            tt(wb, wb, sel, ALU.mult)
            dve.wait_ge(sem("cnt_in"), 1)
            run(v.tensor_copy(flat(wd), bank[7][:]))
            st.do(v.memset(wc[:, 0], 0.0))
            st.sync()
            for n in range(1, NT):
                tt(wc[:, n], wc[:, n - 1], wd[:, n - 1], ALU.add)
            cnt = small[:, 6, 0:E]
            tiles_of = small[:, 6, E:2 * E]
            tt(cnt, wc[:, NT - 1], wd[:, NT - 1], ALU.add)
            run(v.tensor_scalar(cnt, cnt, float(P - 1), None, ALU.add))
            run(v.tensor_copy(smi[:, 0, 0:E], cnt))
            run(v.tensor_scalar(smi[:, 1, 0:E], smi[:, 0, 0:E], 7, None, ALU.arith_shift_right))
            run(v.tensor_copy(tiles_of, smi[:, 1, 0:E]))
            run(v.tensor_scalar(tiles_of, tiles_of, 1.0, None, ALU.max))
            ends, first = small[:, 7, 0:E], small[:, 7, E:2 * E]
            run(v.tensor_tensor_scan(ends, onesq[:, 0:E], tiles_of, 0.0, ALU.mult, ALU.add))
            tt(first, ends, tiles_of, ALU.subtract)
            run(v.tensor_scalar(first, first, float(P), None, ALU.mult))
            run(v.tensor_copy(ends_i[:], ends))
            tt(flat(wc), flat(wc), bank[6][:], ALU.add)
            tt(wc, wc, first.unsqueeze(1).to_broadcast([P, NT, E]), ALU.add)
            slot_f = small[:, 0]
            for k in range(TOPK):
                st.do(v.scalar_tensor_tensor(out=wd, in0=wb, scalar=float(k + 1), in1=wc, op0=ALU.is_equal, op1=ALU.mult))
                run(v.scalar_tensor_tensor(out=sfc, in0=wb, scalar=float(k + 1), in1=wa, op0=ALU.is_equal, op1=ALU.mult))
                st.do(v.tensor_reduce(slot_f[:, k * NT:(k + 1) * NT], wd, AX, ALU.add))
                run(v.tensor_reduce(share[:, k], sfc, AX, ALU.add))
            slot_flat = slot_i[:].rearrange("p k n -> p (k n)")
            run(v.tensor_copy(slot_flat, slot_f))
            st.do(v.tensor_scalar(smi[:, 0], slot_flat, 7, None, ALU.arith_shift_right))
            run(v.tensor_scalar(smi[:, 1], slot_flat, P - 1, None, ALU.bitwise_and))
            q, r = small[:, 1], small[:, 2]
            st.do(v.tensor_copy(q, smi[:, 0]))
            run(v.tensor_copy(r, smi[:, 1]))
            for k in range(TOPK):
                if k >= 2:
                    dve.wait_ge(sem("ids_mm"), k - 1)
                col = lambda m: m[:, k * NT:(k + 1) * NT]
                st.do(v.tensor_tensor(hot_p[:, k % 2], iota_p[:].unsqueeze(1).to_broadcast([P, NT, P]),
                                      col(r).unsqueeze(2).to_broadcast([P, NT, P]), ALU.is_equal))
                shape_q = [P, NT, SLOT_TILES]
                run(v.tensor_tensor(hot_q[:, k % 2], iota_q[:].unsqueeze(1).to_broadcast(shape_q),
                                    col(q).unsqueeze(2).to_broadcast(shape_q), ALU.is_equal))
                v.tensor_tensor(hot_q[:, k % 2], hot_q[:, k % 2], token[:].unsqueeze(2).to_broadcast(shape_q),
                                ALU.mult).then_inc(sem("hot_in"), 1)
            for m in range(SLOT_TILES // E):
                sh = [P, E, E]
                run(v.tensor_tensor(cmp4[:], ends.unsqueeze(1).to_broadcast(sh),
                                    iota_q[:, m * E:(m + 1) * E].unsqueeze(2).to_broadcast(sh), ALU.is_le))
                run(v.tensor_reduce(small[:, 3 + m // 2, (m % 2) * E:(m % 2) * E + E], cmp4[:], AX, ALU.add))
            owner = small[:, 3:5].rearrange("p a b -> p (a b)")[:, 0:SLOT_TILES]
            run(v.tensor_scalar(owner, owner, float(E - 1), None, ALU.min))
            packed = small[:, 6:8].rearrange("p a b -> p (a b)")[:, 0:SLOT_TILES]
            run(v.tensor_copy(packed, owner))
            for k in range(1, PACK):
                run(v.scalar_tensor_tensor(out=packed[:, 0:SLOT_TILES - k], in0=owner[:, k:], scalar=float(1 << OWNER_BITS * k),
                                           in1=packed[:, 0:SLOT_TILES - k], op0=ALU.mult, op1=ALU.add))
            run(v.tensor_scalar(passes_i[:, 1:2], ends_i[:, E - 1:E], 1, None, ALU.subtract))
            run(v.tensor_scalar(passes_i[:, 0:1], passes_i[:, 1:2], GROUP_BITS, None, ALU.arith_shift_right))
            v.tensor_copy(owner_i[:], packed).then_inc(sem("owner_in"), 1)
            dve.wait_ge(sem("ids_mm"), TOPK)
            v.tensor_copy(ids[:], bank[6][:, 0:SLOT_TILES]).then_inc(sem("ids_in"), 1)

        N4 = N3 + NB * NSI
        def passes_of(engine):
            return engine.value_load(passes_i[0:1, 0:1], min_val=E // GROUP - 1, max_val=PASSES - 1)

        PASSES = SLOT_TILES // GROUP

        def owners(engine, g, n=GROUP):
            for k in range(n):
                if k % PACK == 0:
                    word = engine.value_load(owner_i[0:1, bass.ds(g + k, 1)], min_val=0,
                                             max_val=(1 << OWNER_BITS * PACK) - 1)
                yield k, (word >> OWNER_BITS * (k % PACK)) & E - 1

        def first_owners(engine, n):
            return [e for _, e in owners(engine, 0, n)]

        def slot_of(ring, e):
            return ring[:, bass.ds(e & 3, 1)].rearrange("p a n -> p (a n)")

        def stage4_tensor(pe):
            def tin(g, u):
                pe.wait_ge(sem(f"xg_in{u}"), (g - u) * 8 + 16)
                pe.wait_ge(sem("xt4"), g + 1)
                for c in range(C):
                    m = nc.tensor.transpose(bank[u][:, c * P:(c + 1) * P], xg[:, u, c * P:(c + 1) * P], ident[:])
                m.then_inc(sem("t4"), 1)

            def up(g, u, e):
                pe.wait_ge(sem("win"), e + 1)
                pe.wait_ge(sem("xt4"), g + 3)
                pe.wait_ge(sem("r4"), g + 1)
                for c in range(C):
                    m = nc.tensor.matmul(bank[2 + u][:, 0:EI], xT4[:, u, c * P:(c + 1) * P],
                                         slot_of(wu4[:, :, c * EI:(c + 1) * EI], e), start=c == 0, stop=c == C - 1)
                m.then_inc(sem("u4"), 1)

            def turn(g, u):
                pe.wait_ge(sem("s4"), g + 1)
                pe.wait_ge(sem("al4"), g + 1)
                for c in range(EI // P):
                    m = nc.tensor.transpose(bank[4 + u][:, c * P:(c + 1) * P], a4[:, u, c * P:(c + 1) * P], ident[:])
                m.then_inc(sem("at4"), 1)

            def down(g, u):
                pe.wait_ge(sem("al4"), g + 3)
                pe.wait_ge(sem("wl4"), g + 1)
                pe.wait_ge(sem("wlb4"), g + 1)
                pe.wait_ge(sem("y4"), g + 1)
                split_product(bank[6 + u][:], lambda s, c: aT4[:, u, s, c * P:(c + 1) * P],
                              lambda s, c: wds[:, u, s, c * H:(c + 1) * H], EI // P).then_inc(sem("d4"), 1)

            def step(g, u, e):
                up(g, u, e)
                tin(g + 1, 1 - u)
                down(g - 1, 1 - u)
                turn(g, u)

            pe.wait_ge(sem("sh_in"), NB * BT)
            pe.wait_ge(sem("owner_in"), 1)
            passes = passes_of(pe)
            tin(0, 0)
            up(0, 0, first_owners(pe, 1)[0])
            tin(1, 1)
            turn(0, 0)
            with pe.Fori(0, PASSES - 1) as i, pe.If(i < passes):
                for k, e in owners(pe, GROUP * i + 1):
                    step(GROUP * i + 1 + k, (1 + k) % 2, e)
            rest = GROUP * passes
            last = rest + GROUP - 1
            for k, e in owners(pe, rest + 1, GROUP - 1):
                if k < GROUP - 2:
                    step(rest + 1 + k, (1 + k) % 2, e)
            up(last, 1, e)
            down(last - 1, 0)
            turn(last, 1)
            down(last, 1)

        def stage4_scalar(act):
            def x_in(g, u):
                act.wait_ge(sem("t4"), g + 1)
                act.wait_ge(sem("u4"), g + 1)
                nc.scalar.activation(xT4[:, u], bank[u][:], ACT.Copy).then_inc(sem("xt4"), 1)

            def relu(g, u):
                act.wait_ge(sem("u4"), g + 3)
                act.wait_ge(sem("at4"), g + 1)
                nc.scalar.activation(a4[:, u], bank[2 + u][:, 0:EI], ACT.Relu).then_inc(sem("r4"), 1)

            def a_hi(g, u):
                act.wait_ge(sem("at4"), g + 3)
                act.wait_ge(sem("d4"), g + 1)
                nc.scalar.activation(aT4[:, u, 0], bank[4 + u][:, 0:EI], ACT.Copy).then_inc(sem("ah4"), 1)

            def w_hi(g, u, e):
                act.wait_ge(sem("d4"), g + 1)
                wait_apart(act, sem("win"), e + 1)
                nc.scalar.activation(wds[:, u, 0], slot_of(wd4, e), ACT.Copy).then_inc(sem("wh4"), 1)

            def store(g, u):
                wait_apart(act, sem("y4"), g + 3)
                act.dma_start(y_d[bass.ds(g * P, P)], yo[:, u]).then_inc(sem(f"y_st{u}"), 16)

            def step(g, u, e, stores=True, more=True):
                a_hi(g - 1, 1 - u)
                w_hi(g, u, e)
                relu(g, u)
                if more:
                    x_in(g + 1, 1 - u)
                if stores:
                    store(g - 2, u)

            act.wait_ge(sem("vc_done"), 2 + N4)
            act.wait_ge(sem("owner_in"), 1)
            passes = passes_of(act)
            act.wait_ge(sem("y_fill"), 16 * NB * NCI)
            e0, e1 = first_owners(act, 2)
            w_hi(0, 0, e0)
            x_in(0, 0)
            relu(0, 0)
            x_in(1, 1)
            step(1, 1, e1, stores=False)
            with act.Fori(0, PASSES - 1) as i, act.If(i < passes):
                for k, e in owners(act, GROUP * i + 2):
                    step(GROUP * i + 2 + k, k % 2, e)
            rest = GROUP * passes
            last = rest + GROUP - 1
            for k, e in owners(act, rest + 2, GROUP - 2):
                step(rest + 2 + k, k % 2, e, more=k < GROUP - 3)
            a_hi(last, 1)
            store(last - 1, 0)
            store(last, 1)

        HALF_W = EI // P * H // 2

        def stage4_vector(dve):
            def square4(g, u):
                dve.wait_ge(sem("r4"), g + 3)
                nc.vector.tensor_tensor(a4[:, u], a4[:, u], a4[:, u], ALU.mult).then_inc(sem("s4"), 1)

            def a_lo(g, u):
                dve.wait_ge(sem("ah4"), g + 1)
                nc.vector.tensor_tensor(aT4[:, u, 1], bank[4 + u][:, 0:EI], aT4[:, u, 0],
                                        ALU.subtract).then_inc(sem("al4"), 1)

            def w_lo(g, u, e):
                dve.wait_ge(sem("wh4"), g + 1)
                nc.vector.tensor_tensor(wds[:, u, 1, 0:HALF_W], slot_of(wd4[:, :, 0:HALF_W], e),
                                        wds[:, u, 0, 0:HALF_W], ALU.subtract).then_inc(sem("wl4"), 1)

            def take_y(g, u):
                dve.wait_ge(sem("d4"), g + 3)
                dve.wait_ge(sem(f"y_st{u}"), (g - u) * 8 + 16)
                nc.vector.tensor_copy(yo[:, u], bank[6 + u][:]).then_inc(sem("y4"), 1)

            def step(g, u, e):
                a_lo(g - 1, 1 - u)
                w_lo(g, u, e)
                square4(g, u)
                take_y(g - 1, 1 - u)

            dve.wait_ge(sem("owner_in"), 1)
            passes = passes_of(dve)
            w_lo(0, 0, first_owners(dve, 1)[0])
            square4(0, 0)
            with dve.Fori(0, PASSES - 1) as i, dve.If(i < passes):
                for k, e in owners(dve, GROUP * i + 1):
                    step(GROUP * i + 1 + k, (1 + k) % 2, e)
            rest = GROUP * passes
            last = rest + GROUP - 1
            for k, e in owners(dve, rest + 1, GROUP - 1):
                step(rest + 1 + k, (1 + k) % 2, e)
            a_lo(last, 1)
            take_y(last, 1)

        def gather(pool, g, u):
            nc.gpsimd.tensor_copy(idc[:, u:u + 1], ids[:, bass.ds(g, 1)]).then_inc(sem("idc_in"), 1)
            wait_apart(pool, sem("idc_in"), g + 1)
            pool.indirect_dma_start(out=xg[:, u], out_offset=None, in_=h_d,
                                    in_offset=bass.IndirectOffsetOnAxis(ap=idc[:, u:u + 1].bitcast(U32), axis=0)
                                    ).then_inc(sem(f"xg_in{u}"), 16)

        def first_gathers(pool):
            pool.wait_ge(sem("ids_in"), 1)
            pool.wait_ge(sem("h_st"), 16 * NB + 16)
            gather(pool, 0, 0)
            gather(pool, 1, 1)

        def stage4_gpsimd(pool):
            def w_lo(g, u, e):
                wait_apart(pool, sem("wh4"), g + 1)
                nc.gpsimd.tensor_tensor(wds[:, u, 1, HALF_W:], slot_of(wd4[:, :, HALF_W:], e),
                                        wds[:, u, 0, HALF_W:], ALU.subtract).then_inc(sem("wlb4"), 1)

            def step(g, u, e):
                wait_apart(pool, sem("t4"), g + 1)
                gather(pool, g + 2, u)
                w_lo(g, u, e)

            pool.wait_ge(sem("owner_in"), 1)
            passes = passes_of(pool)
            with pool.Fori(0, PASSES - 1) as i, pool.If(i < passes):
                for k, e in owners(pool, GROUP * i):
                    step(GROUP * i + k, k % 2, e)
            rest = GROUP * passes
            for k, e in owners(pool, rest):
                if k < GROUP - 2:
                    step(rest + k, k % 2, e)
                else:
                    w_lo(rest + k, k % 2, e)

        def stage4_sync(sp):
            for s in range(3):
                landed(sp, 0, s)
            sp.wait_ge(sem("owner_in"), 1)
            with sp.Fori(1, E // 4) as r:
                for s in range(4):
                    end = sp.value_load(ends_i[0:1, bass.ds(4 * r + s - 4, 1)], min_val=1, max_val=SLOT_TILES)
                    wait_apart(sp, sem("d4"), end + 2)
                    load(sp, 4 * r + s, s)
                    landed(sp, r if s else r - 1, (s - 1) % 4)
            landed(sp, E // 4 - 1, 3)

        def stage5_gpsimd(pool):
            passes = passes_of(pool)
            for u in range(2):
                wait_apart(pool, sem(f"y_st{u}"), 8 * GROUP * passes + 8 * GROUP + 16)

            def fetch(n, u):
                nc.gpsimd.tensor_copy(idc5[:, u], slot_i[:, :, bass.ds(n, 1)].rearrange("p k a -> p (k a)")).then_inc(sem("idc5_in"), 1)
                wait_apart(pool, sem("idc5_in"), n + 1)
                for k in range(TOPK):
                    pool.indirect_dma_start(out=yg[:, u, k], out_offset=None, in_=y_d,
                                            in_offset=bass.IndirectOffsetOnAxis(ap=idc5[:, u, k:k + 1].bitcast(U32), axis=0)
                                            ).then_inc(sem(f"yg_in{u}{k}"), 16)
            fetch(0, 0)
            fetch(1, 1)
            with pool.Fori(1, NT // 2) as i:
                for n, u in ((2 * i, 0), (2 * i + 1, 1)):
                    wait_apart(pool, sem("o5"), TOPK * (n - 1))
                    fetch(n, u)

        def stage5_vector(dve):
            with dve.Fori(0, NT // 2) as i:
                for n, u in ((2 * i, 0), (2 * i + 1, 1)):
                    wait_apart(dve, sem(f"acc_in{u}"), 16 * i + 16)
                    for k in range(TOPK):
                        wait_apart(dve, sem(f"yg_in{u}{k}"), 16 * i + 16)
                        nc.vector.scalar_tensor_tensor(out=acc[:, u], in0=yg[:, u, k],
                                                       scalar=share[:, k, bass.ds(n, 1)], in1=acc[:, u],
                                                       op0=ALU.mult, op1=ALU.add).then_inc(sem("o5"), 1)
                        wait_apart(dve, sem("o5"), TOPK * n + k + 1)

        def stage5_sync(sp):
            sp.wait_ge(sem("bs_st"), 16 * NB + 16)
            for u in range(2):
                sp.dma_start(acc[:, u], base_d[u * P:(u + 1) * P]).then_inc(sem(f"acc_in{u}"), 16)
            def emit(n, u, i, more=True):
                wait_apart(sp, sem("o5"), TOPK * (n + 1))
                sp.dma_start(out[0, bass.ds(n * P, P)], acc[:, u]).then_inc(sem(f"o_st{u}"), 16)
                if more:
                    wait_apart(sp, sem(f"o_st{u}"), 16 * i + 16)
                    sp.dma_start(acc[:, u], base_d[bass.ds((n + 2) * P, P)]).then_inc(sem(f"acc_in{u}"), 16)
            with sp.Fori(0, NT // 2 - 1) as i:
                emit(2 * i, 0, i)
                emit(2 * i + 1, 1, i)
            emit(NT - 2, 0, NT // 2 - 1, more=False)
            emit(NT - 1, 1, NT // 2 - 1, more=False)
            for u in range(2):
                sp.wait_ge(sem(f"o_st{u}"), 16 * (NT // 2))

        @block.sync
        def _(sp):
            stage1_sync(sp)
            stage2_sync(sp)
            stage3_sync(sp)
            stage4_sync(sp)
            stage5_sync(sp)

        @block.gpsimd
        def _(pool):
            stage1_gpsimd(pool)
            stage2_gpsimd(pool)
            stage3_gpsimd(pool)
            stage4_gpsimd(pool)
            stage5_gpsimd(pool)

        @block.scalar
        def _(act):
            stage1_scalar(act)
            stage2_scalar(act)
            stage3_scalar(act)
            stage4_scalar(act)

        @block.vector
        def _(dve):
            stage1_vector(dve)
            stage2_vector(dve)
            routing_vector(dve)
            stage4_vector(dve)
            stage5_vector(dve)

        @block.tensor
        def _(pe):
            stage1_tensor(pe)
            stage2_tensor(pe)
            stage3_tensor(pe)
            stage4_tensor(pe)


def kernel(**inputs):
    import numpy as _np
    import concourse.bacc as _bacc
    from concourse import mybir as _mybir
    from concourse.bass_utils import run_bass_kernel_spmd as _run

    nc = _bacc.Bacc("TRN2", target_bir_lowering=False, num_devices=1)
    arrays, args = {}, {}
    for name, value in inputs.items():
        v = _np.ascontiguousarray(value)
        arrays[f"in_{name}"] = v
        args[name] = nc.dram_tensor(f"in_{name}", v.shape, _mybir.dt.from_np(v.dtype), kind="ExternalInput").ap()
    out = nc.dram_tensor("out", (1, T, H), _mybir.dt.float32, kind="ExternalOutput").ap()
    program(nc, args, out, lambda name, shape: nc.dram_tensor(name, shape, F).ap())
    r = _run(nc, [arrays], core_ids=[0])
    return r.results[0]["out"]
```

```python
import concourse.bass as bass
from concourse import mybir
from contextlib import ExitStack

F = mybir.dt.float32
R = mybir.dt.float32r
HALF = mybir.dt.float16
I32 = mybir.dt.int32
U32 = mybir.dt.uint32
ALU = mybir.AluOpType
ACT = mybir.ActivationFunctionType
AX = mybir.AxisListType.X

P = 128
T, H = 2048, 512
NT = T // P
BT = 4
NB = NT // BT
BLK = BT * P
C = H // P
CI = 2048
NCI = CI // P
SI = 1024
NSI = SI // P
E, EI, TOPK, GROUPS = 32, 256, 4, 4
ROUTE_SCALE = 2.5
EPS_OUT, EPS_IN = 1e-5, 1e-12
SLOT_TILES = T * TOPK // P + E
GROUP = 12
GROUP_MUL, GROUP_SHIFT = (1 << 17) // GROUP + 1, 17
PACK = 6
OWNER_BITS = 5
assert E == 1 << OWNER_BITS and SLOT_TILES % GROUP == 0 and GROUP % 4 == 0
assert all(n * GROUP_MUL >> GROUP_SHIFT == n // GROUP and n * GROUP_MUL < 1 << 24 for n in range(SLOT_TILES))
KB = 1024
SBUF0 = 16512


class Steps:

    def __init__(self, engine, sem, base=0):
        self.engine, self.sem, self.base, self.k = engine, sem, base, 0

    def do(self, instruction):
        self.k += 1
        instruction.then_inc(self.sem, 1)
        return self.k

    def sync(self, apart=False):
        (wait_apart if apart else type(self.engine).wait_ge)(self.engine, self.sem, self.base + self.k)


def wait_apart(engine, sem, value):
    engine.wait_ge(sem, value)
    engine.nop(nofuse=True)


def program(nc, a, out, scratch):
    ctx = ExitStack()
    sem_names = {}

    def sem(name):
        if name not in sem_names:
            sem_names[name] = ctx.enter_context(nc.semaphore(name))
        return sem_names[name]

    def at(name, shape, dt, kb):
        return nc.alloc_sbuf_tensor_at(name, shape, dt, offset=SBUF0 + int(kb * KB))

    with ctx:
        z_d = scratch("z_d", [T, H])
        wcv_d = scratch("wcv_d", [NCI, P, 2 * H])
        xp_d = scratch("xp_d", [T, H])
        h_d = scratch("h_d", [T, H])
        hT_d = scratch("hT_d", [NB, P, 2, C, BLK])
        z_rows, xp_rows, h_rows = (m.rearrange("(b j p) d -> b p j d", j=BT, p=P) for m in (z_d, xp_d, h_d))
        base_d = scratch("base_d", [T, H])
        y_d = scratch("y_d", [T * TOPK + 2 * P, H])
        y_rows = y_d[0:T * TOPK].rearrange("(n p k) d -> n p (k d)", p=P, k=TOPK)
        base_rows = base_d.rearrange("(b j p) d -> b p j d", j=BT, p=P)
        ident = at("ident", [P, P], F, 200.5)
        onesq = at("onesq", [P, P], F, 201)
        sbc = at("sbc", [P, H], F, 201.5)
        tf = at("tf", [P, C], F, 203.5)
        omtf = at("omtf", [P, C], F, 203.53125)
        ages = at("ages", [P, NT], F, 203.5625)
        mean0 = at("mean0", [P, NT], F, 203.625)
        rstd0 = at("rstd0", [P, NT], F, 203.6875)
        zrow = at("zrow", [P, H], HALF, 203.75)
        nsc = at("nsc", [P, 16, BT], F, 204.75)
        nsci = at("nsci", [P, 2, BT], I32, 205)
        bns = at("bns", [P, BT, 6], F, 205.0625)
        bna = at("bna", [P, BT, 2], F, 205.1875)
        tri = at("tri", [P, P], F, 205.25)
        wck = [at(f"wck_{s}", [P, C, CI], R, 32 * n) for n, s in enumerate(("hi", "lo"))]
        wcr = [at(f"wcr_{s}", [P, C, H], R, 64 + 8 * n) for n, s in enumerate(("hi", "lo"))]
        g1b = at("g1b", [P, 4, H], F, 80)
        tdb = at("tdb", [P, H], F, 88)
        bob = at("bob", [P, H], F, 205.75)
        xb = at("xb", [P, BT, H], F, 92)
        x1 = at("x1", [P, BT, H], F, 100)
        xln = at("xln", [P, BT, H], F, 108)
        dec = at("dec", [P, BT, H], F, 116)
        xlnT = at("xlnT", [P, C, BLK + 1], F, 124)
        mx = at("mx", [P, C, BLK], F, 132.25)
        mixT = [at(f"mixT_{s}", [P, C, BLK], R, 140.25 + 8 * n) for n, s in enumerate(("hi", "lo"))]
        zo = at("zo", [P, 2, H], F, 156.25)
        wr = [at(f"wr_{s}", [P, C, H], R, 160.25 + 8 * n) for n, s in enumerate(("hi", "lo"))]
        raw = at("raw", [P, C * H], F, 176.25)
        stage = at("stage", [P, C, 2, H], R, 184.25)
        wv = at("wv", [P, C, H], F, 80)
        wo = at("wo", [P, C, H], F, 88)
        pv = at("pv", [P, C, H], F, 128)
        vmb = at("vmb", [P, C, P], F, 136)
        vm = at("vm", [P, C], F, 138)

        vring = at("vring", [P, 4, 2 * H], R, 80)
        g2b = at("g2b", [P, 4, H], F, 96)
        f1 = at("f1", [P, 2, BT, H], F, 104)
        f2 = at("f2", [P, BT, H], F, 120)
        hb = at("hb", [P, BT, H], F, 128)
        xcT = [at(f"xcT_{s}", [P, C, BLK + 1], R, 136 + 8.0625 * n) for n, s in enumerate(("hi", "lo"))]
        rc = at("rc", [P, BT, H], F, 152.5)
        ra = at("ra", [P, 2, BLK], F, 160.5)
        ksp = [at(f"ksp_{s}", [P, 2, BLK], R, 164.5 + 4 * n) for n, s in enumerate(("hi", "lo"))]
        hT = [at(f"hT_{c}", [P, 2, BLK], R, kb) for c, kb in enumerate((172.5, 176.5, 196, 186))]
        gw = [at(f"gw_{s}", [P, C, E], R, 180.5 + 0.5 * n) for n, s in enumerate(("hi", "lo"))]
        gwf = at("gwf", [P, C, E], F, 181.5)
        sgT = at("sgT", [E, BLK], F, 182)
        tmp = at("tmp", [P, BT, H], F, 186)
        scores = at("scores", [P, NT, E], F, 194)

        wsu = [at(f"wsu_{s}", [P, C, SI], R, 16 * n) for n, s in enumerate(("hi", "lo"))]
        wsd = [at(f"wsd_{s}", [P, NSI, H], R, 32 + 16 * n) for n, s in enumerate(("hi", "lo"))]
        hTb = at("hTb", [P, 2, 2, C, BLK], R, 64)
        xps = at("xps", [P, BT, H], F, 104)
        so = at("so", [P, BT, H], F, 112)
        raw3 = [at("raw3a", [P, 2, C * 2 * P], F, 120), at("raw3b", [P, 2, C * 2 * P], F, 96)]
        big = [at(f"big{n}", [P, NT, E], F, kb) for n, kb in enumerate((186, 188, 190, 192, 196, 198))]
        cmp4 = at("cmp4", [P, E, E], F, 186)
        hot_p = at("hot_p", [P, 2, NT, P], HALF, 172.5)
        hot_q = at("hot_q", [P, 2, NT, SLOT_TILES], HALF, 152.5)
        iota_p = at("iota_p", [P, P], F, 180.5)
        iota_q = at("iota_q", [P, SLOT_TILES], F, 181)
        token = at("token", [P, NT], F, 181.375)
        four = at("four", [P, NT], F, 181.4375)
        before = at("before", [P, GROUPS, GROUPS], F, 181.5)
        top8 = at("top8", [P, NT, 8], F, 181.5625)
        ebias = at("ebias", [P, E], F, 182.0625)
        small = at("small", [P, 8, NT * GROUPS], F, 182.1875)
        smi = at("smi", [P, 2, NT * GROUPS], I32, 184.1875)
        slot_i = at("slot_i", [P, TOPK, NT], I32, 184.6875)
        share = at("share", [P, TOPK, NT], F, 184.9375)
        ends_i = at("ends_i", [P, E], I32, 185.1875)
        owner_i = at("owner_i", [P, SLOT_TILES], I32, 185.3125)
        passes_i = at("passes_i", [P, 2], I32, 185.6875)
        ids = at("ids", [P, SLOT_TILES], I32, 206.0)
        rows_i = at("rows_i", [P, SLOT_TILES], I32, 206.5)
        spare = at("spare", [P, SLOT_TILES], F, 207)
        hot_f = [at(f"hot_f{k}", [P, NT, SLOT_TILES], HALF, kb) for k, kb in enumerate((100.5, 96))]
        wu4 = at("wu4", [P, 4, C * EI], F, 120)
        wd4 = at("wd4", [P, 4, EI // P * H], F, 136)
        xg = [at(f"xg{n}", [P, H], F, kb) for n, kb in enumerate((96, 98, 18, 20))]
        xT4 = at("xT4", [P, 2, C * P], F, 0)
        a4 = at("a4", [P, 2, EI], F, 8)
        aT4 = at("aT4", [P, 2, 2, EI], R, 10)
        yo = at("yo", [P, 2, H], F, 14)
        wds = at("wds", [P, 2, 2, EI // P * H], R, 34)
        idc = at("idc", [P, 4], I32, 100.0)
        idy = at("idy", [P, 2], I32, 100.125)
        yg = at("yg", [P, 4, TOPK * H], F, 104)
        acc = at("acc", [P, NT, H], F, 64)

        bank = [ctx.enter_context(nc.psum_tensor(f"bank{i}", [P, 512], F)) for i in range(8)]
        block = ctx.enter_context(nc.Block())

        RSQRT_STEPS = 3 + 9

        def rsqrt(dve, st, v, y):
            half, t = nsci[:, 0], nsc[:, 15]
            st.do(nc.vector.tensor_scalar(half, v.bitcast(I32), 1, None, ALU.logical_shift_right))
            st.sync()
            st.do(nc.vector.tensor_scalar(nsci[:, 1], half, -1.0, float(0x5F3759DF), ALU.mult, ALU.add))
            st.sync()
            st.do(nc.vector.tensor_copy(y, nsci[:, 1].bitcast(F)))
            for _ in range(3):
                st.sync()
                st.do(nc.vector.scalar_tensor_tensor(out=t, in0=y, scalar=-0.5, in1=y, op0=ALU.mult, op1=ALU.mult))
                st.sync()
                st.do(nc.vector.tensor_tensor(t, t, v, ALU.mult))
                st.sync()
                st.do(nc.vector.scalar_tensor_tensor(out=y, in0=t, scalar=1.5, in1=y, op0=ALU.add, op1=ALU.mult))
            st.sync()

        STATS_STEPS = 2 * BT + 1
        NORM_A = STATS_STEPS + 2 * RSQRT_STEPS + 6
        NORM_B = STATS_STEPS + RSQRT_STEPS + 3 * BT - 1
        S1 = NORM_A + NORM_B

        def stats(dve, st, src, eps):
            for j in range(BT):
                st.do(nc.vector.bn_stats(bns[:, j], src[:, j]))
            st.sync(apart=True)
            for j in range(BT):
                st.do(nc.vector.bn_aggr(bna[:, j], bns[:, j]))
            st.sync()
            st.do(nc.vector.tensor_scalar(nsc[:, 1], bna[:, :, 1], eps, None, ALU.add))
            st.sync()

        def dve_norms_a(dve, b):
            st = Steps(dve, sem("s1_dve"), b * S1)
            dve.wait_ge(sem("x_in"), 16 * b + 16)
            stats(dve, st, xb, EPS_OUT)
            rsqrt(dve, st, nsc[:, 1], nsc[:, 2])
            mean_b, rstd_b = mean0[:, bass.ds(b * BT, BT)], rstd0[:, bass.ds(b * BT, BT)]
            st.do(nc.vector.tensor_scalar(mean_b, bna[:, :, 0], 1.0, None, ALU.mult))
            st.do(nc.vector.tensor_scalar(rstd_b, nsc[:, 2], 1.0, None, ALU.mult))
            st.do(nc.vector.tensor_tensor(nsc[:, 3], nsc[:, 2], nsc[:, 2], ALU.mult))
            st.sync()
            st.do(nc.vector.tensor_tensor(nsc[:, 3], nsc[:, 3], bna[:, :, 1], ALU.mult))
            st.sync()
            st.do(nc.vector.tensor_scalar(nsc[:, 3], nsc[:, 3], EPS_IN, None, ALU.add))
            st.sync()
            rsqrt(dve, st, nsc[:, 3], nsc[:, 4])
            st.do(nc.vector.tensor_tensor(nsc[:, 4], nsc[:, 4], nsc[:, 2], ALU.mult))
            st.sync()
            assert st.k == NORM_A, (st.k, NORM_A)

        def dve_norms_b(dve, b):
            st = Steps(dve, sem("s1_dve"), b * S1 + NORM_A)
            for j in range(BT):
                i = nc.vector.scalar_tensor_tensor(out=x1[:, j], in0=xb[:, j], scalar=bna[:, j, 0:1],
                                                   in1=g1b[:, 0], op0=ALU.subtract, op1=ALU.mult)
                i.then_inc(sem("x_free"), 1) if j == BT - 1 else st.do(i)
            dve.wait_ge(sem("x_free"), b + 2)
            for j in range(BT):
                st.do(nc.vector.scalar_tensor_tensor(out=x1[:, j], in0=x1[:, j], scalar=nsc[:, 4, j:j + 1],
                                                     in1=g1b[:, 1], op0=ALU.mult, op1=ALU.add))
            st.sync()
            stats(dve, st, x1, EPS_IN)
            rsqrt(dve, st, nsc[:, 1], nsc[:, 2])
            for j in range(BT):
                st.do(nc.vector.scalar_tensor_tensor(out=x1[:, j], in0=x1[:, j], scalar=bna[:, j, 0:1],
                                                     in1=g1b[:, 2], op0=ALU.subtract, op1=ALU.mult))
            st.sync()
            dve.wait_ge(sem("m_done"), b + 1)
            for j in range(BT):
                nc.vector.scalar_tensor_tensor(out=xln[:, j], in0=x1[:, j], scalar=nsc[:, 2, j:j + 1],
                                               in1=g1b[:, 3], op0=ALU.mult, op1=ALU.add).then_inc(sem("xln_in"), 1)
            dve.wait_ge(sem("xln_in"), b * BT + BT)
            assert st.k == NORM_B, (st.k, NORM_B)

        def dve_mix(dve, b):
            for c in range(C):
                dve.wait_ge(sem("xt_in"), b * C + c + 3)
                nc.vector.scalar_tensor_tensor(out=mx[:, c], in0=xlnT[:, c, 0:BLK], scalar=omtf[:, c:c + 1],
                                               in1=mx[:, c], op0=ALU.mult, op1=ALU.add).then_inc(sem("mix_in"), 1)
            dve.wait_ge(sem("mix_in"), b * C + C)
            nc.vector.tensor_scalar(xlnT[:, :, 0:1], xlnT[:, :, BLK:BLK + 1], 1.0, None,
                                    ALU.mult).then_inc(sem("xt_free"), 1)

        def stage1_vector(dve):
            nc.vector.memset(xlnT[:, :, 0:1], 0.0).then_inc(sem("carry0"), 1)
            dve_norms_a(dve, 0)
            dve.wait_ge(sem("par_in"), 16 * 7)
            dve.wait_ge(sem("cst"), 5)
            nc.vector.tensor_scalar(omtf[:], tf[:], -1.0, 1.0, ALU.mult, ALU.add).then_inc(sem("omtf"), 1)
            dve.wait_ge(sem("omtf"), 1)
            dve.wait_ge(sem("carry0"), 1)
            dve_norms_b(dve, 0)
            with dve.Fori(1, NB) as b:
                dve_norms_a(dve, b)
                dve_mix(dve, b - 1)
                dve_norms_b(dve, b)
            dve_mix(dve, NB - 1)
            dve.wait_ge(sem("m_fin"), 1)
            dve.wait_ge(sem("wv_in"), 16)
            dve.wait_ge(sem("xt_free"), NB + 1)
            dve.wait_ge(sem("mixlo_in"), 4 + NB * C)
            for c in range(C):
                nc.vector.tensor_tensor(pv[:, c], wv[:, c], bank[c][:], ALU.mult).then_inc(sem("pv_in"), 1)
            dve.wait_ge(sem("vm_in"), 1)
            nc.vector.tensor_copy(vm[:], bank[4][:, 0:C]).then_inc(sem("vmc"), 1)
            dve.wait_ge(sem("vmc"), 1)
            for c in range(C):
                nc.vector.tensor_scalar(vmb[:, c], onesq[:], vm[:, c:c + 1], None, ALU.mult).then_inc(sem("vmb_in"), 1)
            dve.wait_ge(sem("wst"), 16 * NB + 16)
            front = dve_front_x(dve, 0)
            dve.wait_ge(sem("srow_in"), 1)
            nc.vector.tensor_tensor(sbc[:], bank[5][:], bob[:], ALU.add).then_inc(sem("sbc_in"), 1)
            dve.wait_ge(sem("sbc_in"), 1)
            return front

        def stage1_scalar(act):
            act.wait_ge(sem("par_in"), 16 * 7)
            act.wait_ge(sem("ages_in"), 1)
            act.wait_ge(sem("raw_in"), 16)
            nc.scalar.activation(wr[0][:].rearrange("p c n -> p (c n)"), raw[:], ACT.Copy).then_inc(sem("whi"), 1)
            act.wait_ge(sem("carry0"), 1)
            act_decay(act, 0)
            act_wck(act, 0)
            with act.Fori(0, NB - 1) as b:
                act_block1(act, b)
            act_block1(act, NB - 1, last=True)

        def act_decay(act, b):
            wait_apart(act, sem("m_done"), b + 1)
            for j in range(BT):
                nc.scalar.activation(dec[:, j], tdb[:], ACT.Exp,
                                     scale=ages[:, bass.ds(b * BT + j, 1)]).then_inc(sem("dec_in"), 1)

        def act_wck(act, b):
            wait_apart(act, sem("raw_in"), 32 * b + 32)
            nc.scalar.activation(wck[0][:, bass.ds(b, 1)].rearrange("p a n -> p (a n)"), raw[:],
                                 ACT.Copy).then_inc(sem("whi"), 1)

        def act_block1(act, b, last=False):
            act.wait_ge(sem("xt_free"), b + 1)
            act.wait_ge(sem("mixlo_in"), b * C + 4)
            for c in range(C):
                act.wait_ge(sem("tr_in"), b * C + c + 1)
                nc.scalar.activation(xlnT[:, c, 1:BLK + 1], bank[4 + c % 2][:], ACT.Copy)
                nc.scalar.activation(mx[:, c], bank[4 + c % 2][:], ACT.Copy,
                                     scale=tf[:, c:c + 1]).then_inc(sem("xt_in"), 1)
            for c in range(C):
                act.wait_ge(sem("mix_in"), b * C + c + 1)
                nc.scalar.activation(mixT[0][:, c], mx[:, c], ACT.Copy).then_inc(sem("mixhi_in"), 1)
            act.wait_ge(sem("raw_in"), 32 * b + 48)
            act.wait_ge(sem("wst"), 16 * b + 16)
            nc.scalar.activation(stage[:, :, 0], raw[:].rearrange("p (c n) -> p c n", c=C),
                                 ACT.Copy).then_inc(sem("whi"), 1)
            if not last:
                act_decay(act, b + 1)
            for j in range(BT):
                if j == 3 and not last:
                    act_wck(act, b + 1)
                if j == 3 and last:
                    act.wait_ge(sem("raw_in"), 32 * NB + 32)
                    nc.scalar.activation(wcr[0][:].rearrange("p c n -> p (c n)"), raw[:], ACT.Copy).then_inc(sem("whi"), 1)
                if j == 2 and last:
                    act_receptance(act, 0)
                act.wait_ge(sem("z_in"), b * BT + j + 1)
                act.wait_ge(sem(f"zo_st{j % 2}"), 32 * b + 16 * (j // 2) + 16)
                nc.scalar.activation(zo[:, j % 2], bank[6 + j % 2][:], ACT.Copy).then_inc(sem("z_free"), 1)

        def stage1_gpsimd(pool):
            nc.gpsimd.memset(ident[:], 0.0).then_inc(sem("cst"), 1)
            nc.gpsimd.memset(onesq[:], 1.0).then_inc(sem("cst"), 1)
            nc.gpsimd.memset(zrow[:], 0.0).then_inc(sem("cst"), 1)
            pool.wait_ge(sem("cst"), 3)
            nc.gpsimd.affine_select(out=ident[:], in_=ident[:], compare_op=ALU.not_equal, fill=1.0, base=0,
                                    pattern=[[-1, P]], channel_multiplier=1).then_inc(sem("cst"), 1)
            nc.gpsimd.affine_select(out=tri[:], in_=onesq[:], compare_op=ALU.is_gt, fill=0.0, base=0,
                                    pattern=[[1, P]], channel_multiplier=-1).then_inc(sem("cst"), 1)
            nc.gpsimd.iota(ages[:], [[-P, NT]], base=T - 1, channel_multiplier=-1,
                           allow_small_or_imprecise_dtypes=True).then_inc(sem("ages_in"), 1)
            pool.sem_inc(sem("mixlo_in"), 4)
            pool.wait_ge(sem("whi"), 1)
            nc.gpsimd.tensor_tensor(wr[1][:].rearrange("p c n -> p (c n)"), raw[:],
                                    wr[0][:].rearrange("p c n -> p (c n)"), ALU.subtract).then_inc(sem("wlo"), 1)
            with pool.Fori(0, NB) as b:
                wait_apart(pool, sem("whi"), 2 * b + 2)
                nc.gpsimd.tensor_tensor(wck[1][:, bass.ds(b, 1)].rearrange("p a n -> p (a n)"), raw[:],
                                        wck[0][:, bass.ds(b, 1)].rearrange("p a n -> p (a n)"),
                                        ALU.subtract).then_inc(sem("wlo"), 1)
                for c in range(C):
                    pool.wait_ge(sem("mixhi_in"), b * C + c + 1)
                    nc.gpsimd.tensor_tensor(mixT[1][:, c], mx[:, c], mixT[0][:, c],
                                            ALU.subtract).then_inc(sem("mixlo_in"), 1)
                pool.wait_ge(sem("whi"), 2 * b + 3)
                nc.gpsimd.tensor_tensor(stage[:, :, 1], raw[:].rearrange("p (c n) -> p c n", c=C),
                                        stage[:, :, 0], ALU.subtract).then_inc(sem("wlo"), 1)
            pool.wait_ge(sem("whi"), 2 * NB + 2)
            nc.gpsimd.tensor_tensor(wcr[1][:].rearrange("p c n -> p (c n)"), raw[:],
                                    wcr[0][:].rearrange("p c n -> p (c n)"), ALU.subtract).then_inc(sem("wlo"), 1)

        def pe_block1(pe, b, last=False):
            for c in range(C):
                for j in range(BT):
                    if c == 0:
                        pe.wait_ge(sem("xln_in"), b * BT + j + 1)
                    if j == 0:
                        pe.wait_ge(sem("xt_in"), b * C + c + 1)
                    i = nc.tensor.transpose(bank[4 + c % 2][:, j * P:(j + 1) * P], xln[:, j, c * P:(c + 1) * P], ident[:])
                i.then_inc(sem("tr_in"), 1)
            for j in range(BT):
                pe.wait_ge(sem("dec_in"), b * BT + j + 1)
                for c in range(C):
                    i = nc.tensor.matmul(bank[c][:], xln[:, j, c * P:(c + 1) * P], dec[:, j], start=False,
                                         stop=last and j == BT - 1)
            i.then_inc(sem("m_fin" if last else "m_done"), 1)
            pe.wait_ge(sem("wlo"), 1)
            pe.wait_ge(sem("mixlo_in"), b * C + C + 4)
            for j in range(BT):
                pe.wait_ge(sem("z_free"), b * BT + j + 1)
                i = split_product(bank[6 + j % 2][:], lambda s, c: mixT[s][:, c, j * P:(j + 1) * P],
                                  lambda s, c: wr[s][:, c], C)
                i.then_inc(sem("z_in"), 1)
                if last and j == 0:
                    pe_vmix(pe)
                if last and j == 2:
                    pe_row(pe)

        def pe_vmix(pe):
            pe.wait_ge(sem("pv_in"), C)
            pe.wait_ge(sem("xt_in"), NB * C + 2)
            for h in range(C):
                for c in range(C):
                    i = nc.tensor.matmul(bank[4][:, h:h + 1], pv[:, c, h * P:(h + 1) * P], onesq[:, 0:1],
                                         start=c == 0, stop=c == C - 1)
            i.then_inc(sem("vm_in"), 1)

        def pe_row(pe):
            pe.wait_ge(sem("vmb_in"), C)
            pe.wait_ge(sem("wo_in"), 16)
            for h in range(C):
                i = nc.tensor.matmul(bank[5][:], vmb[:, h], wo[:, h], start=h == 0, stop=h == C - 1)
            i.then_inc(sem("srow_in"), 1)

        def stage1_tensor(pe):
            pe.sem_inc(sem("m_done"), 1)
            pe.wait_ge(sem("cst"), 5)
            for c in range(C):
                nc.tensor.matmul(bank[c][:], zrow[:, 0:P], zrow[:], start=True, stop=False)
            with pe.Fori(0, NB - 1) as b:
                pe_block1(pe, b)
            pe_block1(pe, NB - 1, last=True)

        def split_product(dst, lhs, rhs, n):
            parts = [(0, 0), (0, 1), (1, 0)]
            for c in range(n):
                for k, (l, r) in enumerate(parts):
                    i = nc.tensor.matmul(dst, lhs(l, c), rhs(r, c), start=c == 0 and k == 0,
                                         stop=c == n - 1 and k == 2)
            return i

        def vec(name):
            return a[name].partition_broadcast(P)

        x_rows = a["L0_attn_x"][0].rearrange("(b j p) d -> b p j d", j=BT, p=P)
        wck_rows = a["L0_attn_Wck"].rearrange("(c p) n -> c p n", p=P)
        wcv_rows = a["L0_attn_Wcv"].rearrange("(g c p) n -> g p c n", c=C, p=P)

        def square(name):
            return a[name].rearrange("(c p) n -> p c n", p=P)

        def stage1_sync(sp):
            sp.dma_start(xb[:], x_rows[0]).then_inc(sem("x_in"), 16)
            for n, v in enumerate(("ln1_g", "ln1_b", "tm_g", "tm_b")):
                sp.dma_start(g1b[:, n], vec(f"L0_attn_{v}")).then_inc(sem("par_in"), 16)
            sp.dma_start(tdb[:], vec("L0_attn_time_decay")).then_inc(sem("par_in"), 16)
            sp.dma_start(bob[:], vec("L0_attn_bo")).then_inc(sem("par_in"), 16)
            sp.dma_start(tf[:], a["L0_attn_time_first"].rearrange("(c p) -> p c", p=P),
                         allow_slow_non_contiguous=True).then_inc(sem("par_in"), 16)
            sp.dma_start(raw[:].rearrange("p (c n) -> p c n", c=C), square("L0_attn_Wr")).then_inc(sem("raw_in"), 16)
            for name, credit in (("x_free", 1), ("xt_free", 1), ("xt_in", 2), ("z_free", 2), ("zo_st0", 16),
                                 ("zo_st1", 16), ("wst", 16)):
                sp.sem_inc(sem(name), credit)
            sp.wait_ge(sem("wlo"), 1)
            sp.dma_start(raw[:], wck_rows[0]).then_inc(sem("raw_in"), 16)
            sync_tokens(sp, 1)
            with sp.Fori(0, NB - 2) as b:
                sync_block1(sp, b, tokens=True)
            sync_block1(sp, NB - 2)
            sync_block1(sp, NB - 1, last=True)

        def sync_tokens(sp, b):
            wait_apart(sp, sem("x_free"), b + 1)
            sp.dma_start(xb[:], x_rows[bass.ds(b, 1)].rearrange("a p j d -> p (a j) d")).then_inc(sem("x_in"), 16)

        def sync_block1(sp, b, tokens=False, last=False):
            wait_apart(sp, sem("wlo"), 2 * b + 2)
            sp.dma_start(raw[:].rearrange("p (c n) -> p c n", c=C),
                         wcv_rows[bass.ds(b, 1)].rearrange("a p c n -> p (a c) n")).then_inc(sem("raw_in"), 16)
            if tokens:
                sync_tokens(sp, b + 2)
            if last:
                sync_squares(sp)
            wait_apart(sp, sem("wlo"), 2 * b + 3)
            if not last:
                sp.dma_start(raw[:], wck_rows[bass.ds(b + 1, 1)].rearrange("a p n -> p (a n)")).then_inc(sem("raw_in"), 16)
            if last:
                store_wcv(sp, b)
                sync_ahead(sp)
            for j in range(BT):
                wait_apart(sp, sem("z_free"), b * BT + j + 3)
                sp.dma_start(z_d[bass.ds((b * BT + j) * P, P)], zo[:, j % 2]).then_inc(sem(f"zo_st{j % 2}"), 16)
                if j == 1 and not last:
                    store_wcv(sp, b)

        def store_wcv(sp, b):
            sp.dma_start(wcv_d[bass.ds(b * C, C)].rearrange("c p m -> p c m"),
                         stage[:].bitcast(F).rearrange("p c s n -> p c (s n)")).then_inc(sem("wst"), 16)

        def sync_squares(sp):
            sp.wait_ge(sem("xln_in"), NB * BT)
            sp.dma_start(wv[:], square("L0_attn_Wv")).then_inc(sem("wv_in"), 16)
            sp.wait_ge(sem("dec_in"), NB * BT)
            sp.dma_start(wo[:], square("L0_attn_Wo")).then_inc(sem("wo_in"), 16)

        def sync_ahead(sp):
            sp.wait_ge(sem("m_fin"), 1)
            sp.dma_start(f1[:, 0], x_rows[0]).then_inc(sem("x2_in"), 16)
            sp.wait_ge(sem("xt_free"), NB + 1)
            sp.wait_ge(sem("zo_st0"), 32 + 16)
            sp.wait_ge(sem("zo_st1"), 32 + 16)
            sp.dma_start(f2[:], z_rows[0]).then_inc(sem("zl_in"), 16)
            sp.dma_start(raw[:].rearrange("p (c n) -> p c n", c=C), square("L0_attn_Wcr")).then_inc(sem("raw_in"), 16)
            for n, v in enumerate(("ln2_g", "ln2_b", "cm_g", "cm_b")):
                sp.dma_start(g2b[:, n], vec(f"L0_attn_{v}")).then_inc(sem("par2_in"), 16)
            sp.wait_ge(sem("x2_in"), 16)
            sp.dma_start(f1[:, 1], x_rows[1]).then_inc(sem("x2_in"), 16)

        TH_AT = 3
        FRONT, TAIL = 4 * BT + 2 * (STATS_STEPS + RSQRT_STEPS) + 3 * BT, STATS_STEPS + RSQRT_STEPS

        def xx(b, j):
            return f1[:, bass.ds(b & 1, 1), j].rearrange("p a d -> p (a d)")

        def dve_front_x(dve, b):
            st = Steps(dve, sem("front_dve"), b * FRONT)
            wait_apart(dve, sem("x2_in"), 16 * b + 16)
            if not isinstance(b, int):
                wait_apart(dve, sem("ht_st"), 16 * C * (b - 1) + 16)
                wait_apart(dve, sem("lg_in"), b - 1)
            for j in range(BT):
                st.do(nc.vector.tensor_scalar(tmp[:, j], xx(b, j), mean0[:, bass.ds(b * BT + j, 1)],
                                              rstd0[:, bass.ds(b * BT + j, 1)], ALU.subtract, ALU.mult))
            return st

        def dve_front(dve, b, st=None):
            if st is None:
                st = dve_front_x(dve, b)
            for j in range(BT):
                dve.wait_ge(sem("zs_in"), b * BT + j + 1)
                st.do(nc.vector.tensor_tensor(f2[:, j], f2[:, j], sbc[:], ALU.mult))
            st.sync()
            for j in range(BT):
                st.do(nc.vector.tensor_tensor(f2[:, j], f2[:, j], tmp[:, j], ALU.add))
            st.sync()
            for j in range(BT):
                st.do(nc.vector.tensor_tensor(xx(b, j), xx(b, j), f2[:, j], ALU.add))
            for n in (0, 2):
                stats(dve, st, f2, EPS_IN)
                rsqrt(dve, st, nsc[:, 1], nsc[:, 2])
                for j in range(BT):
                    st.do(nc.vector.scalar_tensor_tensor(out=f2[:, j], in0=f2[:, j], scalar=bna[:, j, 0:1],
                                                         in1=g2b[:, n], op0=ALU.subtract, op1=ALU.mult))
                st.sync()
                for j in range(BT):
                    i = nc.vector.scalar_tensor_tensor(out=f2[:, j], in0=f2[:, j], scalar=nsc[:, 2, j:j + 1],
                                                       in1=g2b[:, n + 1], op0=ALU.mult, op1=ALU.add)
                    st.do(i) if n == 0 else i.then_inc(sem("xc_in"), 1)
                if n == 0:
                    st.sync()
            dve.wait_ge(sem("xc_in"), b * BT + BT)
            assert st.k == FRONT, (st.k, FRONT)

        def dve_lo_xc(dve, b):
            for c in range(C):
                dve.wait_ge(sem("hiT_in"), b * C + c + 1)
                nc.vector.tensor_tensor(xcT[1][:, c, 1:BLK + 1], bank[6 + c % 2][:], xcT[0][:, c, 1:BLK + 1],
                                        ALU.subtract).then_inc(sem("loT_in"), 1)

        def dve_tail_a(dve, b):
            dve.wait_ge(sem("vc_done"), 2 + NCI * (b + 1))
            dve.wait_ge(sem("h_st"), 16 * b + 16)
            for j in range(BT):
                nc.vector.tensor_tensor(hb[:, j], rc[:, j], bank[j][:], ALU.mult).then_inc(sem("u_in"), 1)

        def dve_tail_b(dve, b):
            st = Steps(dve, sem("tail_dve"), b * TAIL)
            dve.wait_ge(sem("u_in"), 4 + b * BT + BT)
            for j in range(BT):
                nc.vector.tensor_tensor(xx(b, j), xx(b, j), hb[:, j], ALU.add).then_inc(sem("xp_in"), 1)
            wait_apart(dve, sem("xp_in"), b * BT + BT)
            stats(dve, st, f1[:, bass.ds(b & 1, 1)].rearrange("p a j d -> p (a j) d"), EPS_OUT)
            rsqrt(dve, st, nsc[:, 1], nsc[:, 2])
            for j in range(BT):
                nc.vector.tensor_scalar(hb[:, j], xx(b, j), bna[:, j, 0:1], nsc[:, 2, j:j + 1],
                                        ALU.subtract, ALU.mult).then_inc(sem("h_in"), 1)
            dve.wait_ge(sem("h_in"), b * BT + BT)
            assert st.k == TAIL, (st.k, TAIL)

        def dve_lo_h(dve, b):
            for c in range(C):
                dve.wait_ge(sem("hiTH_in"), b * C + c + 1)
                nc.vector.tensor_tensor(hT[c][:, 1], bank[6 + c % 2][:], hT[c][:, 0],
                                        ALU.subtract).then_inc(sem("loTH_in"), 1)

        def stage2_vector(dve, front):
            dve.wait_ge(sem("par2_in"), 16 * 4)
            dve_front(dve, 0, front)
            dve.wait_ge(sem("z_in"), NB * BT)
            for s in range(2):
                nc.vector.memset(xcT[s][:, :, 0:1].bitcast(F), 0.0).then_inc(sem("carry2"), 1)
            dve_lo_xc(dve, 0)
            dve.wait_ge(sem("gwhi"), 1)
            nc.vector.tensor_tensor(gw[1][:], gwf[:], gw[0][:], ALU.subtract).then_inc(sem("gwlo"), 1)
            dve_front(dve, 1)
            with dve.Fori(1, NB - 1) as b:
                dve_lo_xc(dve, b)
                dve_tail_a(dve, b - 1)
                dve_tail_b(dve, b - 1)
                dve_lo_h(dve, b - 1)
                dve_front(dve, b + 1)
            dve_lo_xc(dve, NB - 1)
            dve_tail_a(dve, NB - 2)
            dve_tail_b(dve, NB - 2)
            dve_lo_h(dve, NB - 2)
            lo3(dve, nc.vector, *ORDER3[:3])
            dve_tail_a(dve, NB - 1)
            lo3(dve, nc.vector, ORDER3[3])
            dve_tail_b(dve, NB - 1)
            dve_lo_h(dve, NB - 1)

        def act_receptance(act, b):
            act.wait_ge(sem("zl_in"), 16 * b + 16)
            for j in range(BT):
                nc.scalar.activation(f2[:, j], f2[:, j], ACT.Sigmoid).then_inc(sem("zs_in"), 1)

        def act_hi_xc(act, b, first=False):
            act.wait_ge(sem("trT_in"), b * C + 1)
            if first:
                act.wait_ge(sem("carry2"), 2)
            else:
                for s in range(2):
                    nc.scalar.activation(xcT[s][:, :, 0:1], xcT[s][:, :, BLK:BLK + 1], ACT.Copy).then_inc(sem("carry2"), 1)
                act.wait_ge(sem("carry2"), 2 + 2 * b)
            for c in range(C):
                act.wait_ge(sem("trT_in"), b * C + c + 1)
                nc.scalar.activation(xcT[0][:, c, 1:BLK + 1], bank[6 + c % 2][:], ACT.Copy).then_inc(sem("hiT_in"), 1)

        def act_rc(act, b):
            act.wait_ge(sem("u_in"), b * BT + 4)
            for j in range(BT):
                act.wait_ge(sem("rcp_in"), b * BT + j + 1)
                nc.scalar.activation(rc[:, j], bank[6 + j % 2][:], ACT.Sigmoid).then_inc(sem("rc_in"), 1)

        def act_inner(act, n, i, router=None):
            act.wait_ge(sem("kc_in"), n + 1)
            act.wait_ge(sem("klo_in"), n + 1)
            nc.scalar.activation(ra[:, i % 2], bank[4 + i % 2][:], ACT.Relu).then_inc(sem("kc_free"), 1)
            act.wait_ge(sem("kc_free"), n + 3)
            nc.scalar.activation(ra[:, i % 2], ra[:, i % 2], ACT.Square).then_inc(sem("sq"), 1)
            if router is not None:
                act_router_before(act, router, i)
            act.wait_ge(sem("sq"), n + 1)
            act.wait_ge(sem("vc_done"), n + 1)
            nc.scalar.activation(ksp[0][:, i % 2], ra[:, i % 2], ACT.Copy).then_inc(sem("khi_in"), 1)

        def act_hi_h(act, b, c):
            act.wait_ge(sem("trH_in"), b * C + c + 1)
            act.wait_ge(sem("ht_st"), 16 * C * b + 16)
            nc.scalar.activation(hT[c][:, 0], bank[6 + c % 2][:], ACT.Copy).then_inc(sem("hiTH_in"), 1)

        def act_router_before(act, b, i):
            if i == TH_AT:
                act_hi_h(act, b, 0)
                act_hi_h(act, b, 1)
            if i == TH_AT + 1:
                act.wait_ge(sem("lg_in"), b + 1)
                nc.scalar.activation(sgT[:], bank[5][0:E], ACT.Sigmoid).then_inc(sem("sg_in"), 1)

        def act_router_behind(act, b, i):
            if i == TH_AT:
                act_hi_h(act, b, 2)
                act_hi_h(act, b, 3)
            if i == TH_AT + 2:
                wait_apart(act, sem("tsc_in"), b + 1)
                nc.scalar.activation(scores[:, bass.ds(b * BT, BT)].rearrange("p j e -> p (j e)"), bank[6][:, 0:BT * E],
                                     ACT.Copy).then_inc(sem("sc_in"), 1)

        def act_block2(act, b, first=False, last=False):
            act_hi_xc(act, b, first)
            act_rc(act, b)
            for i in range(NCI):
                act_inner(act, b * NCI + i, i, None if first else b - 1)
                if i == 1 and not last:
                    act_receptance(act, b + 1)
                if not first:
                    act_router_behind(act, b - 1, i)

        def stage2_scalar(act):
            act.wait_ge(sem("gwf_in"), 16)
            nc.scalar.activation(gw[0][:], gwf[:], ACT.Copy).then_inc(sem("gwhi"), 1)
            act_block2(act, 0, first=True)
            with act.Fori(1, NB - 1) as b:
                act_block2(act, b)
            act_block2(act, NB - 1, last=True)

        def pool_inner(pool, n, i):
            pool.wait_ge(sem("khi_in"), n + 1)
            nc.gpsimd.tensor_tensor(ksp[1][:, i % 2], ra[:, i % 2], ksp[0][:, i % 2],
                                    ALU.subtract).then_inc(sem("klo_in"), 1)

        def stage2_gpsimd(pool):
            with pool.Fori(0, NB) as b:
                for i in range(NCI):
                    pool_inner(pool, b * NCI + i, i)

        def pe_inner_up(pe, n, i, weights, rhs):
            pe.wait_ge(sem("kc_free"), n + 1)
            split_product(bank[4 + i % 2][:], lambda s, c: weights[s][:, c, i * P:(i + 1) * P],
                          rhs, C).then_inc(sem("kc_in"), 1)

        def pe_inner_down(pe, n, i, last, rhs):
            pe.wait_ge(sem("klo_in"), n + 3)
            for j in range(BT):
                for k, (l, r) in enumerate(((0, 0), (0, 1), (1, 0))):
                    m = nc.tensor.matmul(bank[j][:], ksp[l][:, i % 2, j * P:(j + 1) * P], rhs(r),
                                         start=i == 0 and k == 0, stop=i == last and k == 2)
            m.then_inc(sem("vc_done"), 1)

        def pe_logits(pe, b, c):
            pe.wait_ge(sem("loTH_in"), 8 + b * C + c + 1)
            for k, (l, r) in enumerate(((0, 0), (0, 1), (1, 0))):
                m = nc.tensor.matmul(bank[5][0:E], gw[l][:, c], hT[c][:, r], start=c == 0 and k == 0,
                                     stop=c == C - 1 and k == 2)
            if c == C - 1:
                m.then_inc(sem("lg_in"), 1)

        def pe_turn_norm(pe, b, c):
            if c >= 2:
                pe.wait_ge(sem("loTH_in"), 8 + b * C + c - 1)
            for j in range(BT):
                m = nc.tensor.transpose(bank[6 + c % 2][:, j * P:(j + 1) * P], hb[:, j, c * P:(c + 1) * P], ident[:])
            m.then_inc(sem("trH_in"), 1)

        def pe_inner(pe, b, i, n, up, down, router, rc_done=None):
            if router and i == TH_AT + 2:
                pe.wait_ge(sem("sg_in"), b + 1)
            up(i)
            if router and i == TH_AT:
                pe.wait_ge(sem("h_in"), b * BT + BT)
                pe.wait_ge(sem("rc_in"), rc_done)
                pe_turn_norm(pe, b, 0)
                pe_turn_norm(pe, b, 1)
            if router and i == TH_AT + 1:
                pe_logits(pe, b, 2)
                pe_logits(pe, b, 3)
            if i >= 2:
                down(i - 2)
            if router and i == TH_AT:
                pe.wait_ge(sem("kc_free"), n + 3)
                pe_logits(pe, b, 0)
                pe_turn_norm(pe, b, 2)
                pe_logits(pe, b, 1)
                pe_turn_norm(pe, b, 3)
            if router and i == TH_AT + 2:
                pe_scores(pe, b)

        def pe_scores(pe, b):
            wait_apart(pe, sem("sg_in"), b + 1)
            for j in range(BT):
                m = nc.tensor.transpose(bank[6][:, j * E:(j + 1) * E], sgT[:, j * P:(j + 1) * P], ident[0:E, 0:E])
            m.then_inc(sem("tsc_in"), 1)

        def pe_turn_xc(pe, b, c):
            if c == 0:
                pe.wait_ge(sem("xc_in"), b * BT + BT)
                pe.wait_ge(sem("loTH_in"), 4 + b * C)
            if c >= 2:
                pe.wait_ge(sem("loT_in"), b * C + c - 1)
            for j in range(BT):
                m = nc.tensor.transpose(bank[6 + c % 2][:, j * P:(j + 1) * P], f2[:, j, c * P:(c + 1) * P], ident[:])
            m.then_inc(sem("trT_in"), 1)

        def pe_block2(pe, b, first=False, last=False):
            pe.wait_ge(sem("loT_in"), b * C + C)
            for j in range(BT):
                if j >= 2:
                    pe.wait_ge(sem("rc_in"), b * BT + j - 1)
                split_product(bank[6 + j % 2][:], lambda s, c: xcT[s][:, c, 1 + j * P:1 + (j + 1) * P],
                              lambda s, c: wcr[s][:, c], C).then_inc(sem("rcp_in"), 1)

            def down(i):
                if i == 0:
                    pe.wait_ge(sem("u_in"), b * BT + 4)
                pe.wait_ge(sem(f"vr_in{i % 4}"), 64 * b + 16 * (i // 4) + 16)
                pe_inner_down(pe, b * NCI + i, i, NCI - 1, lambda s: vring[:, i % 4, s * H:(s + 1) * H])

            def up(i):
                pe_inner_up(pe, b * NCI + i, i, wck, lambda s, c: xcT[s][:, c, 0:BLK])

            for i in range(NCI):
                pe_inner(pe, b - 1, i, b * NCI + i, up, down, not first, b * BT + BT)
            for i in (NCI - 2, NCI - 1):
                if not last:
                    c = 2 * (i - NCI + 2)
                    pe_turn_xc(pe, b + 1, c)
                    pe_turn_xc(pe, b + 1, c + 1)
                down(i)

        def stage2_tensor(pe):
            pe.wait_ge(sem("wlo"), 2 * NB + 2)
            for c in range(C):
                pe_turn_xc(pe, 0, c)
            pe_block2(pe, 0, first=True)
            pe.wait_ge(sem("gwlo"), 1)
            with pe.Fori(1, NB - 1) as b:
                pe_block2(pe, b)
            pe_block2(pe, NB - 1, last=True)

        hT_rows = hT_d.rearrange("b p s c t -> b c p s t")

        def sp_tail2(sp, b):
            wait_apart(sp, sem("xp_in"), b * BT + BT)
            sp.dma_start(xp_rows[bass.ds(b, 1)].rearrange("a p j d -> p (a j) d"),
                         f1[:, bass.ds(b & 1, 1)].rearrange("p a j d -> p (a j) d")).then_inc(sem("xp_st"), 16)
            wait_apart(sp, sem("h_in"), b * BT + BT)
            sp.dma_start(h_rows[bass.ds(b, 1)].rearrange("a p j d -> p (a j) d"), hb[:]).then_inc(sem("h_st"), 16)

        def sp_hT(sp, b):
            for c in range(C):
                wait_apart(sp, sem("loTH_in"), 8 + b * C + c + 1)
                sp.dma_start(hT_rows[bass.ds(b, 1), c].rearrange("a p s t -> p (a s) t"),
                             hT[c][:].bitcast(F)).then_inc(sem("ht_st"), 16)

        def sp_block2(sp, b, first=False, last=False):
            def ring(i):
                n = b * NCI + i
                if not (first and i < 4):
                    wait_apart(sp, sem("vc_done"), n - 1)
                sp.dma_start(vring[:, i % 4].bitcast(F), wcv_d[i]).then_inc(sem(f"vr_in{i % 4}"), 16)
            if not last:
                wait_apart(sp, sem("trT_in"), b * C + C)
                sp.dma_start(f2[:], z_rows[bass.ds(b + 1, 1)].rearrange("a p j d -> p (a j) d")).then_inc(sem("zl_in"), 16)
            for i in range(4):
                ring(i)
            if not first:
                sp_tail2(sp, b - 1)
                if not last:
                    wait_apart(sp, sem("xp_st"), 16 * b)
                    sp.dma_start(f1[:, bass.ds((b + 1) & 1, 1)].rearrange("p a j d -> p (a j) d"),
                                 x_rows[bass.ds(b + 1, 1)].rearrange("a p j d -> p (a j) d")).then_inc(sem("x2_in"), 16)
            ring(4)
            if not first:
                sp_hT(sp, b - 1)
            for i in range(5, NCI):
                ring(i)

        def stage2_sync(sp):
            for name, credit in (("u_in", 4), ("h_st", 16), ("kc_free", 2), ("klo_in", 2), ("vc_done", 2),
                                 ("loTH_in", 8), ("ht_st", 16),
                                 ("bs_st", 16), ("xt4", 2), ("u4", 2), ("r4", 2), ("at4", 2), ("al4", 2),
                                 ("d4", 2), ("y4", 2)):
                sp.sem_inc(sem(name), credit)
            sp.wait_ge(sem("wlo"), 2 * NB + 2)
            sp.dma_start(gwf[:], square("L0_ffn_gate_w")).then_inc(sem("gwf_in"), 16)
            sp.wait_ge(sem("zo_st0"), 32 * NB + 16)
            sp.wait_ge(sem("zo_st1"), 32 * NB + 16)
            sp.wait_ge(sem("sbc_in"), 1)
            sp.wait_ge(sem("wst"), 16 * NB + 16)
            sp_block2(sp, 0, first=True)
            with sp.Fori(1, NB - 1) as b:
                sp_block2(sp, b)
            sp_block2(sp, NB - 1, last=True)

        N3 = NB * NCI

        BETWEEN_AT = 2

        def pe_block3(pe, b, router=False, between=None):
            pe.wait_ge(sem("hb_in"), 16 * b + 16)

            def down(i):
                if i == 0:
                    if b == 0:
                        pe.wait_ge(sem("u_in"), NB * BT + 4)
                    else:
                        pe.wait_ge(sem("sh_in"), b * BT)
                pe.wait_ge(sem(f"wsd_lo{i // 4}"), i % 4 // 2 + 1)
                pe_inner_down(pe, N3 + b * NSI + i, i, NSI - 1, lambda s: wsd[s][:, i])

            rhs = lambda s, c: hTb[:, bass.ds(b & 1, 1), s, c].rearrange("p a t -> p (a t)")

            def up(i):
                pe.wait_ge(sem(f"wsu_lo{i // 4}"), i % 4 // 2 + 1)
                pe_inner_up(pe, N3 + b * NSI + i, i, wsu, rhs)

            for i in range(NSI):
                pe_inner(pe, NB - 1, i, N3 + b * NSI + i, up, down, router, NB * BT)
                if i == BETWEEN_AT and between:
                    between(pe)
            down(NSI - 2)
            down(NSI - 1)

        def pe_counts(pe):
            pe.wait_ge(sem("sel_in"), 1)
            sel = big[3][:].rearrange("p n e -> p (n e)")
            nc.tensor.matmul(bank[6][:], tri[:], sel, start=True, stop=True)
            nc.tensor.matmul(bank[7][:], onesq[:], sel, start=True, stop=True).then_inc(sem("cnt_in"), 1)

        def pe_ids(pe, choices):
            for k in choices:
                pe.wait_ge(sem("hot_in"), k + 1)
                if k == 0:
                    nc.tensor.matmul(bank[7][:], zrow[:, 0:P], zrow[:], start=True, stop=False)
                for n in range(NT):
                    nc.tensor.matmul(bank[7][:, k * SLOT_TILES:(k + 1) * SLOT_TILES], hot_p[:, k % 2, n],
                                     hot_f[k % 2][:, n], start=False, stop=k == TOPK - 1 and n == NT - 1)
                    m = nc.tensor.matmul(bank[6][:, 0:SLOT_TILES], hot_p[:, k % 2, n], hot_q[:, k % 2, n],
                                         start=k == 0 and n == 0, stop=k == TOPK - 1 and n == NT - 1)
                m.then_inc(sem("ids_mm"), 1)

        def stage3_tensor(pe):
            pe_block3(pe, 0, router=True)
            pe_block3(pe, 1, between=pe_counts)
            pe_block3(pe, 2, between=lambda pe: pe_ids(pe, (0, 1)))
            pe_block3(pe, 3, between=lambda pe: pe_ids(pe, (2, 3)))

        ORDER3 = (("u", 0), ("u", 1), ("d", 0), ("d", 1), ("u", 2), ("d", 2), ("u", 3), ("d", 3))

        def part3(m, which, k):
            if which == "u":
                return wsu[m][:, :, 2 * k * P:2 * (k + 1) * P], raw3[k % 2][:, 0].rearrange("p (c n) -> p c n", c=C)
            return wsd[m][:, 2 * k:2 * k + 2], raw3[k % 2][:, 1].rearrange("p (c n) -> p c n", c=2)

        def act_hi3(act, *parts):
            for which, k in parts:
                act.wait_ge(sem(f"raw3_in{k % 2}"), 32 * (k // 2) + 32)
                act.wait_ge(sem("kc_in"), N3)
                dst, src = part3(0, which, k)
                nc.scalar.activation(dst, src, ACT.Copy).then_inc(sem("w3hi"), 1)

        def lo3(engine, ops, *parts):
            for which, k in parts:
                engine.wait_ge(sem("w3hi"), ORDER3.index((which, k)) + 1)
                hi, src = part3(0, which, k)
                ops.tensor_tensor(part3(1, which, k)[0], src, hi, ALU.subtract).then_inc(sem(f"ws{which}_lo{k // 2}"), 1)

        def act_block3(act, b, router=False):
            for i in range(NSI):
                act_inner(act, N3 + b * NSI + i, i, NB - 1 if router else None)
                if router and i < 3:
                    act_hi3(act, *((("u", 2),), (("d", 2), ("u", 3)), (("d", 3),))[i])
                if i == 3 and router:
                    act.wait_ge(sem("xp_st"), 16 * NB)
                if router:
                    act_router_behind(act, NB - 1, i)
            act.wait_ge(sem("vc_done"), 2 + N3 + (b + 1) * NSI)
            act.wait_ge(sem("bs_st"), 16 * b + 16)
            for j in range(BT):
                nc.scalar.activation(so[:, j], bank[j][:], ACT.Copy).then_inc(sem("sh_in"), 1)

        def stage3_scalar(act):
            act_hi3(act, *ORDER3[:4])
            act_block3(act, 0, router=True)
            with act.Fori(1, NB) as b:
                act_block3(act, b)

        def pool_numbers(pool):
            pool.wait_ge(sem("sc_in"), NB)
            nc.gpsimd.iota(iota_p[:], [[1, P]], base=0, channel_multiplier=0, allow_small_or_imprecise_dtypes=True)
            nc.gpsimd.iota(iota_q[:], [[1, SLOT_TILES]], base=0, channel_multiplier=0, allow_small_or_imprecise_dtypes=True)
            nc.gpsimd.iota(token[:], [[P, NT]], base=0, channel_multiplier=1, allow_small_or_imprecise_dtypes=True)
            nc.gpsimd.iota(four[:], [[TOPK, NT]], base=0, channel_multiplier=0, allow_small_or_imprecise_dtypes=True)
            nc.gpsimd.iota(spare[:], [[0, SLOT_TILES // 2], [P, 2]], base=T * TOPK + 1, channel_multiplier=1,
                           allow_small_or_imprecise_dtypes=True)
            nc.gpsimd.memset(before[:], 1.0).then_inc(sem("num_in"), 1)
            pool.wait_ge(sem("num_in"), 1)
            nc.gpsimd.affine_select(out=before[:], in_=before[:], compare_op=ALU.is_gt, fill=0.0, base=0,
                                    pattern=[[1, GROUPS], [-1, GROUPS]], channel_multiplier=0).then_inc(sem("num_in"), 1)

        def pool_block3(pool, b, first=False, last=False):
            for i in range(NSI):
                pool_inner(pool, N3 + b * NSI + i, i)
                if first and i < 4:
                    lo3(pool, nc.gpsimd, ORDER3[4 + i])
                if first and i == TH_AT + 2:
                    pool_numbers(pool)
            if last:
                first_gathers(pool)
            wait_apart(pool, sem("xps_in"), 16 * b + 16)
            for j in range(BT):
                pool.wait_ge(sem("sh_in"), b * BT + j + 1)
                nc.gpsimd.tensor_tensor(so[:, j], so[:, j], xps[:, j], ALU.add).then_inc(sem("bs_in"), 1)

        def stage3_gpsimd(pool):
            pool_block3(pool, 0, first=True)
            with pool.Fori(1, NB - 1) as b:
                pool_block3(pool, b)
            pool_block3(pool, NB - 1, last=True)

        def sp_raw3(sp, k):
            if k >= 2:
                sp.wait_ge(sem("wsu_lo0"), k - 1)
                sp.wait_ge(sem("wsd_lo0"), k - 1)
            sp.dma_start(raw3[k % 2][:, 0].rearrange("p (c n) -> p c n", c=C),
                         square("L0_ffn_Wsu")[:, :, 2 * k * P:2 * (k + 1) * P]).then_inc(sem(f"raw3_in{k % 2}"), 16)
            sp.dma_start(raw3[k % 2][:, 1].rearrange("p (c n) -> p c n", c=2),
                         square("L0_ffn_Wsd")[:, 2 * k:2 * k + 2]).then_inc(sem(f"raw3_in{k % 2}"), 16)

        def sp_hTb(sp, b):
            sp.dma_start(hTb[:, b % 2].bitcast(F), hT_d[b]).then_inc(sem("hb_in"), 16)

        wu_rows = a["L0_ffn_Wu"].rearrange("e (c p) i -> e p c i", p=P)
        wd_rows = a["L0_ffn_Wd"].rearrange("e (c p) i -> e p c i", p=P)

        def load(sp, e, s):
            sp.dma_start(wu4[:, s].rearrange("p (c n) -> p c n", c=C),
                         wu_rows[bass.ds(e, 1)].rearrange("a p c i -> p (a c) i")).then_inc(sem(f"w4_in{s}"), 16)
            sp.dma_start(wd4[:, s].rearrange("p (c n) -> p c n", n=H),
                         wd_rows[bass.ds(e, 1)].rearrange("a p c i -> p (a c) i")).then_inc(sem(f"w4_in{s}"), 16)

        def landed(sp, r, s):
            wait_apart(sp, sem(f"w4_in{s}"), 32 * r + 32)
            sp.sem_inc(sem("win"), 1)

        def first_experts(sp):
            sp.wait_ge(sem("wsu_lo1"), 2)
            sp.wait_ge(sem("wsd_lo1"), 2)
            sp.wait_ge(sem("lg_in"), NB)
            for s in range(4):
                load(sp, s, s)

        def stage3_sync(sp):
            sp.wait_ge(sem("trT_in"), NB * C)
            sp_raw3(sp, 0)
            sp_raw3(sp, 1)
            sp.wait_ge(sem("ht_st"), 16 * C + 16)
            sp.wait_ge(sem("rcp_in"), NB * BT)
            sp_hTb(sp, 0)
            sp.wait_ge(sem("xp_st"), 16 * (NB - 1))
            sp.dma_start(xps[:], xp_rows[0]).then_inc(sem("xps_in"), 16)
            sp_raw3(sp, 2)
            sp_raw3(sp, 3)
            sp.wait_ge(sem("hb_in"), 16)
            sp.wait_ge(sem("vc_done"), 2 + N3)
            sp_hTb(sp, 1)
            sp_tail2(sp, NB - 1)
            sp_hT(sp, NB - 1)
            sp.wait_ge(sem("sc_in"), NB)
            sp.dma_start(ebias[:], a["L0_ffn_e_bias"].partition_broadcast(P)).then_inc(sem("eb_in"), 16)
            for b in range(NB):
                if b + 2 < NB:
                    sp.wait_ge(sem("kc_in"), N3 + (b + 1) * NSI)
                    sp.wait_ge(sem("hb_in"), 16 * (b + 2))
                    if b + 2 == NB - 1:
                        sp.wait_ge(sem("ht_st"), 16 * C * NB + 16)
                    sp_hTb(sp, b + 2)
                if b == 1:
                    first_experts(sp)
                if b == 2:
                    for s in range(3):
                        landed(sp, 0, s)
                sp.wait_ge(sem("bs_in"), (b + 1) * BT)
                sp.dma_start(base_rows[b], so[:]).then_inc(sem("bs_st"), 16)
                if b + 1 < NB:
                    if b + 1 == NB - 1:
                        sp.wait_ge(sem("xp_st"), 16 * NB)
                    sp.dma_start(xps[:], xp_rows[b + 1]).then_inc(sem("xps_in"), 16)

        def routing_vector(dve):
            st = Steps(dve, sem("route"))
            v = nc.vector

            def run(instruction):
                st.do(instruction)
                st.sync()
            tt = lambda o, x, y, op: run(v.tensor_tensor(o, x, y, op))
            dve.wait_ge(sem("eb_in"), 16)
            dve.wait_ge(sem("num_in"), 2)
            sfc, wa, wb, sel, wc, wd = (m[:] for m in big)
            sc = scores[:]
            per_tile = lambda m: m.unsqueeze(2).to_broadcast([P, NT, E])
            tt(sfc, sc, ebias[:].unsqueeze(1).to_broadcast([P, NT, E]), ALU.add)
            g8 = sfc.rearrange("p n (g k) -> p (n g) k", k=8)
            hi, lo = (m.rearrange("p n e -> p (n e)")[:, 0:256].rearrange("p (g k) -> p g k", k=4) for m in (wa, wb))
            t, u = (m.rearrange("p n e -> p (n e)")[:, 256:384].rearrange("p (g k) -> p g k", k=2) for m in (wa, wb))
            tt(hi, g8[:, :, 0:4], g8[:, :, 4:8], ALU.max)
            tt(lo, g8[:, :, 0:4], g8[:, :, 4:8], ALU.min)
            for w in (2, 1):
                a0, a1, b0, b1 = hi[:, :, 0:w], hi[:, :, w:2 * w], lo[:, :, 0:w], lo[:, :, w:2 * w]
                tt(t[:, :, 0:w], a0, a1, ALU.min)
                tt(u[:, :, 0:w], b0, b1, ALU.max)
                tt(a0, a0, a1, ALU.max)
                tt(b0, t[:, :, 0:w], u[:, :, 0:w], ALU.max)
            gs = small[:, 0].rearrange("p (n g) -> p n g", g=GROUPS)
            tt(gs, hi[:, :, 0].rearrange("p (n g) -> p n g", g=GROUPS), lo[:, :, 0].rearrange("p (n g) -> p n g", g=GROUPS), ALU.add)
            shape4 = [P, NT, GROUPS, GROUPS]
            other, own = gs.unsqueeze(2).to_broadcast(shape4), gs.unsqueeze(3).to_broadcast(shape4)
            gt4, eq4 = (m.rearrange("p n e -> p (n e)")[:, 0:256].rearrange("p (n g j) -> p n g j", g=GROUPS, j=GROUPS)
                        for m in (wc, wd))
            tt(gt4, other, own, ALU.is_gt)
            tt(eq4, other, own, ALU.is_equal)
            tt(eq4, eq4, before[:].unsqueeze(1).to_broadcast(shape4), ALU.mult)
            tt(gt4, gt4, eq4, ALU.add)
            gm = small[:, 1].rearrange("p (n g) -> p n g", g=GROUPS)
            run(v.tensor_reduce(gm, gt4, AX, ALU.add))
            run(v.tensor_scalar(gm, gm, 1.5, None, ALU.is_lt))
            tt(g8, g8, small[:, 1].unsqueeze(2).to_broadcast([P, NT * GROUPS, 8]), ALU.mult)
            for n in range(NT):
                st.do(v.max(top8[:, n], sfc[:, n]))
            st.sync()
            fourth = per_tile(top8[:, :, TOPK - 1])
            tt(wa, sfc, fourth, ALU.is_gt)
            tt(wb, sfc, fourth, ALU.is_equal)
            flat = lambda m: m.rearrange("p n e -> p (n e)")
            ones_row = onesq[:, 0:1].to_broadcast([P, NT * E])
            run(v.tensor_tensor_scan(flat(wc), ones_row, flat(wb), 0.0, ALU.mult, ALU.add))
            room = small[:, 2, 0:NT]
            st.do(v.memset(small[:, 3, 0:1], 0.0))
            run(v.tensor_copy(small[:, 3, 1:NT], wc[:, 0:NT - 1, E - 1]))
            run(v.tensor_reduce(room, wa, AX, ALU.add))
            tt(room, small[:, 3, 0:NT], room, ALU.subtract)
            run(v.tensor_scalar(room, room, float(TOPK), None, ALU.add))
            tt(wc, wc, per_tile(room), ALU.is_le)
            tt(wb, wb, wc, ALU.mult)
            st.do(v.tensor_tensor(sel, wa, wb, ALU.add))
            st.sync()
            v.tensor_scalar(small[:, 4, 0:1], small[:, 3, 0:1], 1.0, None, ALU.mult).then_inc(sem("sel_in"), 1)
            tt(wa, sc, sel, ALU.mult)
            den = small[:, 5, 0:NT]
            run(v.tensor_reduce(den, wa, AX, ALU.add))
            run(v.tensor_scalar(den, den, 1e-20, None, ALU.add))
            run(v.reciprocal(den, den))
            tt(wa, wa, per_tile(den), ALU.mult)
            run(v.tensor_scalar(wa, wa, ROUTE_SCALE, None, ALU.mult))
            run(v.tensor_tensor_scan(flat(wb), ones_row, flat(sel), 0.0, ALU.mult, ALU.add))
            tt(wb, wb, per_tile(four[:]), ALU.subtract)
            tt(wb, wb, sel, ALU.mult)
            dve.wait_ge(sem("cnt_in"), 1)
            run(v.tensor_copy(flat(wd), bank[7][:]))
            st.do(v.memset(wc[:, 0], 0.0))
            st.sync()
            for n in range(1, NT):
                tt(wc[:, n], wc[:, n - 1], wd[:, n - 1], ALU.add)
            cnt = small[:, 6, 0:E]
            tiles_of = small[:, 6, E:2 * E]
            tt(cnt, wc[:, NT - 1], wd[:, NT - 1], ALU.add)
            run(v.tensor_scalar(cnt, cnt, float(P - 1), None, ALU.add))
            run(v.tensor_copy(smi[:, 0, 0:E], cnt))
            run(v.tensor_scalar(smi[:, 1, 0:E], smi[:, 0, 0:E], 7, None, ALU.arith_shift_right))
            run(v.tensor_copy(tiles_of, smi[:, 1, 0:E]))
            run(v.tensor_scalar(tiles_of, tiles_of, 1.0, None, ALU.max))
            ends, first = small[:, 7, 0:E], small[:, 7, E:2 * E]
            run(v.tensor_tensor_scan(ends, onesq[:, 0:E], tiles_of, 0.0, ALU.mult, ALU.add))
            tt(first, ends, tiles_of, ALU.subtract)
            run(v.tensor_scalar(first, first, float(P), None, ALU.mult))
            run(v.tensor_copy(ends_i[:], ends))
            tt(flat(wc), flat(wc), bank[6][:], ALU.add)
            tt(wc, wc, first.unsqueeze(1).to_broadcast([P, NT, E]), ALU.add)
            slot_f = small[:, 0]
            for k in range(TOPK):
                st.do(v.scalar_tensor_tensor(out=wd, in0=wb, scalar=float(k + 1), in1=wc, op0=ALU.is_equal, op1=ALU.mult))
                run(v.scalar_tensor_tensor(out=sfc, in0=wb, scalar=float(k + 1), in1=wa, op0=ALU.is_equal, op1=ALU.mult))
                st.do(v.tensor_reduce(slot_f[:, k * NT:(k + 1) * NT], wd, AX, ALU.add))
                run(v.tensor_reduce(share[:, k], sfc, AX, ALU.add))
            slot_flat = slot_i[:].rearrange("p k n -> p (k n)")
            run(v.tensor_copy(slot_flat, slot_f))
            st.do(v.tensor_scalar(smi[:, 0], slot_flat, 7, None, ALU.arith_shift_right))
            run(v.tensor_scalar(smi[:, 1], slot_flat, P - 1, None, ALU.bitwise_and))
            q, r = small[:, 1], small[:, 2]
            st.do(v.tensor_copy(q, smi[:, 0]))
            run(v.tensor_copy(r, smi[:, 1]))
            for k in range(TOPK):
                if k >= 2:
                    dve.wait_ge(sem("ids_mm"), k - 1)
                col = lambda m: m[:, k * NT:(k + 1) * NT]
                st.do(v.tensor_tensor(hot_p[:, k % 2], iota_p[:].unsqueeze(1).to_broadcast([P, NT, P]),
                                      col(r).unsqueeze(2).to_broadcast([P, NT, P]), ALU.is_equal))
                shape_q = [P, NT, SLOT_TILES]
                run(v.tensor_tensor(hot_f[k % 2][:], iota_q[:].unsqueeze(1).to_broadcast(shape_q),
                                    col(q).unsqueeze(2).to_broadcast(shape_q), ALU.is_equal))
                v.tensor_tensor(hot_q[:, k % 2], hot_f[k % 2][:], token[:].unsqueeze(2).to_broadcast(shape_q),
                                ALU.mult).then_inc(sem("hot_in"), 1)
            for m in range(SLOT_TILES // E):
                sh = [P, E, E]
                run(v.tensor_tensor(cmp4[:], ends.unsqueeze(1).to_broadcast(sh),
                                    iota_q[:, m * E:(m + 1) * E].unsqueeze(2).to_broadcast(sh), ALU.is_le))
                run(v.tensor_reduce(small[:, 3 + m // 2, (m % 2) * E:(m % 2) * E + E], cmp4[:], AX, ALU.add))
            owner = small[:, 3:5].rearrange("p a b -> p (a b)")[:, 0:SLOT_TILES]
            run(v.tensor_scalar(owner, owner, float(E - 1), None, ALU.min))
            single = small[:, 6:8].rearrange("p a b -> p (a b)")[:, 0:SLOT_TILES].bitcast(I32)
            shifted = smi[:].rearrange("p a b -> p (a b)")[:, 0:SLOT_TILES]
            run(v.tensor_copy(single, owner))
            run(v.tensor_copy(owner_i[:], owner))
            for k in range(1, PACK):
                n = SLOT_TILES - k
                run(v.tensor_scalar(shifted[:, 0:n], single[:, k:], OWNER_BITS * k, None, ALU.logical_shift_left))
                run(v.tensor_tensor(owner_i[:, 0:n], owner_i[:, 0:n], shifted[:, 0:n], ALU.bitwise_or))
            whole = small[:, 5, 0:1]
            run(v.tensor_copy(whole, ends_i[:, E - 1:E]))
            run(v.tensor_scalar(whole, whole, float(GROUP_MUL), float(-GROUP_MUL), ALU.mult, ALU.add))
            run(v.tensor_copy(passes_i[:, 1:2], whole))
            v.tensor_scalar(passes_i[:, 0:1], passes_i[:, 1:2], GROUP_SHIFT, None,
                            ALU.arith_shift_right).then_inc(sem("owner_in"), 1)
            dve.wait_ge(sem("ids_mm"), TOPK)
            v.tensor_copy(ids[:], bank[6][:, 0:SLOT_TILES]).then_inc(sem("ids_in"), 1)
            choice, other_row = (small[:, n:n + 2].rearrange("p a b -> p (a b)")[:, 0:SLOT_TILES] for n in (0, 2))
            run(v.tensor_copy(choice, bank[7][:, 0:SLOT_TILES]))
            for k in range(1, TOPK):
                run(v.scalar_tensor_tensor(out=choice, in0=bank[7][:, k * SLOT_TILES:(k + 1) * SLOT_TILES],
                                           scalar=float(k + 1), in1=choice, op0=ALU.mult, op1=ALU.add))
            run(v.scalar_tensor_tensor(out=other_row, in0=choice, scalar=0.0, in1=spare[:], op0=ALU.is_equal, op1=ALU.mult))
            run(v.scalar_tensor_tensor(out=choice, in0=bank[6][:, 0:SLOT_TILES], scalar=float(TOPK), in1=choice,
                                       op0=ALU.mult, op1=ALU.add))
            run(v.scalar_tensor_tensor(out=choice, in0=choice, scalar=-1.0, in1=other_row, op0=ALU.add, op1=ALU.add))
            v.tensor_copy(rows_i[:], choice).then_inc(sem("rows_in"), 1)

        N4 = N3 + NB * NSI

        def passes_of(engine):
            return engine.value_load(passes_i[0:1, 0:1], min_val=E // GROUP - 1, max_val=PASSES - 1)

        PASSES = SLOT_TILES // GROUP

        def owners(engine, g, n=GROUP):
            for k in range(n):
                if k % PACK == 0:
                    word = engine.value_load(owner_i[0:1, bass.ds(g + k, 1)], min_val=0,
                                             max_val=(1 << OWNER_BITS * PACK) - 1)
                yield k, (word >> OWNER_BITS * (k % PACK)) & E - 1

        def first_owners(engine, n):
            return [e for _, e in owners(engine, 0, n)]

        def slot_of(ring, e):
            return ring[:, bass.ds(e & 3, 1)].rearrange("p a n -> p (a n)")

        def stage4_tensor(pe):
            def tin(g, u, s):
                pe.wait_ge(sem(f"xg_in{s}"), (g - s) * 4 + 16)
                pe.wait_ge(sem("xt4"), g + 1)
                for c in range(C):
                    m = nc.tensor.transpose(bank[u][:, c * P:(c + 1) * P], xg[s][:, c * P:(c + 1) * P], ident[:])
                m.then_inc(sem("t4"), 1)

            def up(g, u, e):
                pe.wait_ge(sem("win"), e + 1)
                pe.wait_ge(sem("xt4"), g + 3)
                pe.wait_ge(sem("r4"), g + 1)
                for c in range(C):
                    m = nc.tensor.matmul(bank[2 + u][:, 0:EI], xT4[:, u, c * P:(c + 1) * P],
                                         slot_of(wu4[:, :, c * EI:(c + 1) * EI], e), start=c == 0, stop=c == C - 1)
                m.then_inc(sem("u4"), 1)

            def turn(g, u):
                pe.wait_ge(sem("s4"), g + 1)
                pe.wait_ge(sem("al4"), g + 1)
                for c in range(EI // P):
                    m = nc.tensor.transpose(bank[4 + u][:, c * P:(c + 1) * P], a4[:, u, c * P:(c + 1) * P], ident[:])
                m.then_inc(sem("at4"), 1)

            def down(g, u):
                pe.wait_ge(sem("al4"), g + 3)
                pe.wait_ge(sem("wl4"), g + 1)
                pe.wait_ge(sem("y4"), g + 1)
                split_product(bank[6 + u][:], lambda s, c: aT4[:, u, s, c * P:(c + 1) * P],
                              lambda s, c: wds[:, u, s, c * H:(c + 1) * H], EI // P).then_inc(sem("d4"), 1)

            def step(g, u, e, s):
                up(g, u, e)
                tin(g + 1, 1 - u, s)
                down(g - 1, 1 - u)
                turn(g, u)

            pe.wait_ge(sem("sh_in"), NB * BT)
            pe.wait_ge(sem("owner_in"), 1)
            passes = passes_of(pe)
            tin(0, 0, 0)
            up(0, 0, first_owners(pe, 1)[0])
            tin(1, 1, 1)
            turn(0, 0)
            with pe.Fori(0, PASSES - 1) as i, pe.If(i < passes):
                for k, e in owners(pe, GROUP * i + 1):
                    step(GROUP * i + 1 + k, (1 + k) % 2, e, (2 + k) % 4)
            rest = GROUP * passes
            last = rest + GROUP - 1
            for k, e in owners(pe, rest + 1, GROUP - 1):
                if k < GROUP - 2:
                    step(rest + 1 + k, (1 + k) % 2, e, (2 + k) % 4)
            up(last, 1, e)
            down(last - 1, 0)
            turn(last, 1)
            down(last, 1)

        def stage4_scalar(act):
            def x_in(g, u):
                act.wait_ge(sem("t4"), g + 1)
                act.wait_ge(sem("u4"), g + 1)
                nc.scalar.activation(xT4[:, u], bank[u][:], ACT.Copy).then_inc(sem("xt4"), 1)

            def relu(g, u):
                act.wait_ge(sem("u4"), g + 3)
                act.wait_ge(sem("at4"), g + 1)
                nc.scalar.activation(a4[:, u], bank[2 + u][:, 0:EI], ACT.Relu).then_inc(sem("r4"), 1)

            def a_hi(g, u):
                act.wait_ge(sem("at4"), g + 3)
                act.wait_ge(sem("d4"), g + 1)
                nc.scalar.activation(aT4[:, u, 0], bank[4 + u][:, 0:EI], ACT.Copy).then_inc(sem("ah4"), 1)

            def w_hi(g, u, e):
                act.wait_ge(sem("d4"), g + 1)
                wait_apart(act, sem("win"), e + 1)
                nc.scalar.activation(wds[:, u, 0], slot_of(wd4, e), ACT.Copy).then_inc(sem("wh4"), 1)

            def take_y(g, u, first=False):
                act.wait_ge(sem("d4"), g + 3)
                if not first:
                    act.wait_ge(sem(f"y_st{u}"), (g - u) * 8)
                nc.scalar.activation(yo[:, u], bank[6 + u][:], ACT.Copy).then_inc(sem("y4"), 1)

            def step(g, u, e, more=True, first=False):
                a_hi(g - 1, 1 - u)
                w_hi(g, u, e)
                relu(g, u)
                if more:
                    x_in(g + 1, 1 - u)
                take_y(g - 1, 1 - u, first)

            act.wait_ge(sem("vc_done"), 2 + N4)
            act.wait_ge(sem("owner_in"), 1)
            passes = passes_of(act)
            e0, e1, e2 = first_owners(act, 3)
            w_hi(0, 0, e0)
            x_in(0, 0)
            relu(0, 0)
            x_in(1, 1)
            step(1, 1, e1, first=True)
            step(2, 0, e2, first=True)
            with act.Fori(0, PASSES - 1) as i, act.If(i < passes):
                for k, e in owners(act, GROUP * i + 3):
                    step(GROUP * i + 3 + k, (1 + k) % 2, e)
            rest = GROUP * passes
            last = rest + GROUP - 1
            for k, e in owners(act, rest + 3, GROUP - 3):
                step(rest + 3 + k, (1 + k) % 2, e, more=k < GROUP - 4)
            a_hi(last, 1)
            take_y(last, 1)

        def stage4_vector(dve):
            def square4(g, u):
                dve.wait_ge(sem("r4"), g + 3)
                nc.vector.tensor_tensor(a4[:, u], a4[:, u], a4[:, u], ALU.mult).then_inc(sem("s4"), 1)

            def a_lo(g, u):
                dve.wait_ge(sem("ah4"), g + 1)
                nc.vector.tensor_tensor(aT4[:, u, 1], bank[4 + u][:, 0:EI], aT4[:, u, 0],
                                        ALU.subtract).then_inc(sem("al4"), 1)

            def w_lo(g, u, e):
                dve.wait_ge(sem("wh4"), g + 1)
                nc.vector.tensor_tensor(wds[:, u, 1], slot_of(wd4, e), wds[:, u, 0], ALU.subtract).then_inc(sem("wl4"), 1)

            def step(g, u, e):
                a_lo(g - 1, 1 - u)
                square4(g, u)
                w_lo(g, u, e)

            dve.wait_ge(sem("owner_in"), 1)
            passes = passes_of(dve)
            w_lo(0, 0, first_owners(dve, 1)[0])
            square4(0, 0)
            with dve.Fori(0, PASSES - 1) as i, dve.If(i < passes):
                for k, e in owners(dve, GROUP * i + 1):
                    step(GROUP * i + 1 + k, (1 + k) % 2, e)
            rest = GROUP * passes
            last = rest + GROUP - 1
            for k, e in owners(dve, rest + 1, GROUP - 1):
                step(rest + 1 + k, (1 + k) % 2, e)
            a_lo(last, 1)

        def gather(pool, g, s):
            nc.gpsimd.tensor_copy(idc[:, s:s + 1], ids[:, bass.ds(g, 1)]).then_inc(sem("idc_in"), 1)
            wait_apart(pool, sem("idc_in"), g + 1)
            pool.indirect_dma_start(out=xg[s][:], out_offset=None, in_=h_d,
                                    in_offset=bass.IndirectOffsetOnAxis(ap=idc[:, s:s + 1].bitcast(U32), axis=0)
                                    ).then_inc(sem(f"xg_in{s}"), 16)

        def first_gathers(pool):
            pool.wait_ge(sem("ids_in"), 1)
            pool.wait_ge(sem("h_st"), 16 * NB + 16)
            gather(pool, 0, 0)
            gather(pool, 1, 1)

        def stage4_gpsimd(pool):
            def scatter(g, u):
                wait_apart(pool, sem("y4"), g + 3)
                nc.gpsimd.tensor_copy(idy[:, u:u + 1], rows_i[:, bass.ds(g, 1)]).then_inc(sem("idy_in"), 1)
                wait_apart(pool, sem("idy_in"), g + 1)
                pool.indirect_dma_start(out=y_d, out_offset=bass.IndirectOffsetOnAxis(ap=idy[:, u:u + 1].bitcast(U32), axis=0),
                                        in_=yo[:, u], in_offset=None).then_inc(sem(f"y_st{u}"), 16)

            def fetch(g, s):
                wait_apart(pool, sem("t4"), g - 3)
                gather(pool, g, s)

            pool.wait_ge(sem("owner_in"), 1)
            pool.wait_ge(sem("rows_in"), 1)
            passes = passes_of(pool)
            pool.wait_ge(sem("vc_done"), 2 + N4)
            gather(pool, 2, 2)
            gather(pool, 3, 3)
            with pool.Fori(0, PASSES - 1) as i, pool.If(i < passes):
                for k in range(GROUP):
                    fetch(GROUP * i + k + 4, k % 4)
                    scatter(GROUP * i + k, k % 2)
            rest = GROUP * passes
            for k in range(GROUP):
                if k < GROUP - 4:
                    fetch(rest + k + 4, k % 4)
                scatter(rest + k, k % 2)

        def stage4_sync(sp):
            base_load(sp)
            sp.wait_ge(sem("owner_in"), 1)
            with sp.Fori(1, E // 4) as r:
                for s in range(4):
                    end = sp.value_load(ends_i[0:1, bass.ds(4 * r + s - 4, 1)], min_val=1, max_val=SLOT_TILES)
                    wait_apart(sp, sem("d4"), end + 2)
                    load(sp, 4 * r + s, s)
                    landed(sp, r if s else r - 1, (s - 1) % 4)
            landed(sp, E // 4 - 1, 3)

        YRING = 4

        def base_load(sp):
            sp.wait_ge(sem("bs_st"), 16 * NB + 16)
            sp.wait_ge(sem("kc_in"), N4)
            for b in range(NB):
                sp.dma_start(acc[:, b * BT:(b + 1) * BT], base_rows[b]).then_inc(sem("acc_in"), 16)

        def stage5_sync(sp):
            sp.wait_ge(sem("owner_in"), 1)
            passes = passes_of(sp)
            for u in range(2):
                wait_apart(sp, sem(f"y_st{u}"), 8 * GROUP * passes + 8 * GROUP)

            def fetch(n, u):
                sp.dma_start(yg[:, u], y_rows[bass.ds(n, 1)].rearrange("a p m -> (a p) m")).then_inc(sem(f"yg_in{u}"), 16)

            for u in range(YRING):
                fetch(u, u)
            with sp.Fori(1, NT // YRING) as i:
                for u in range(YRING):
                    wait_apart(sp, sem("o5"), TOPK * (YRING * i + u - u % 2 - YRING + 2))
                    fetch(YRING * i + u, u)

        def stage5_vector(dve):
            dve.wait_ge(sem("acc_in"), 16 * NB)
            with dve.Fori(0, NT // YRING) as i:
                for pair in range(0, YRING, 2):
                    first = TOPK * (YRING * i + pair)
                    for u in (pair, pair + 1):
                        wait_apart(dve, sem(f"yg_in{u}"), 16 * i + 16)
                    for k in range(TOPK):
                        for u in (pair, pair + 1):
                            if k:
                                wait_apart(dve, sem("o5"), first + 2 * k + u - pair - 1)
                            row = acc[:, bass.ds(YRING * i + u, 1)].rearrange("p a d -> p (a d)")
                            nc.vector.scalar_tensor_tensor(out=row, in0=yg[:, u, k * H:(k + 1) * H],
                                                           scalar=share[:, k, bass.ds(YRING * i + u, 1)], in1=row,
                                                           op0=ALU.mult, op1=ALU.add).then_inc(sem("o5"), 1)

        def stage5_scalar(act):
            pair_rows = out[0].rearrange("(n t p) d -> n p t d", t=2, p=P)
            with act.Fori(0, NT // 2) as n:
                wait_apart(act, sem("o5"), 2 * TOPK * n + 2 * TOPK)
                act.dma_start(pair_rows[bass.ds(n, 1)].rearrange("a p t d -> p (a t) d"),
                              acc[:, bass.ds(2 * n, 2)]).then_inc(sem("o_st"), 16)
            act.wait_ge(sem("o_st"), 16 * (NT // 2))

        @block.sync
        def _(sp):
            stage1_sync(sp)
            stage2_sync(sp)
            stage3_sync(sp)
            stage4_sync(sp)
            stage5_sync(sp)

        @block.gpsimd
        def _(pool):
            stage1_gpsimd(pool)
            stage2_gpsimd(pool)
            stage3_gpsimd(pool)
            stage4_gpsimd(pool)

        @block.scalar
        def _(act):
            stage1_scalar(act)
            stage2_scalar(act)
            stage3_scalar(act)
            stage4_scalar(act)
            stage5_scalar(act)

        @block.vector
        def _(dve):
            front = stage1_vector(dve)
            stage2_vector(dve, front)
            routing_vector(dve)
            stage4_vector(dve)
            stage5_vector(dve)

        @block.tensor
        def _(pe):
            stage1_tensor(pe)
            stage2_tensor(pe)
            stage3_tensor(pe)
            stage4_tensor(pe)


def kernel(**inputs):
    import numpy as _np
    import concourse.bacc as _bacc
    from concourse import mybir as _mybir
    from concourse.bass_utils import run_bass_kernel_spmd as _run

    nc = _bacc.Bacc("TRN2", target_bir_lowering=False, num_devices=1)
    arrays, args = {}, {}
    for name, value in inputs.items():
        v = _np.ascontiguousarray(value)
        arrays[f"in_{name}"] = v
        args[name] = nc.dram_tensor(f"in_{name}", v.shape, _mybir.dt.from_np(v.dtype), kind="ExternalInput").ap()
    out = nc.dram_tensor("out", (1, T, H), _mybir.dt.float32, kind="ExternalOutput").ap()
    program(nc, args, out, lambda name, shape: nc.dram_tensor(name, shape, F).ap())
    r = _run(nc, [arrays], core_ids=[0])
    return r.results[0]["out"]
```
